# Optimizing a Trainium2 kernel written in Bass

```python
import numpy as np
import jax
import jax.numpy as jnp

def _softmax(x, axis=-1):
    return jax.nn.softmax(x, axis=axis)

def _gelu(x):
    return jax.nn.gelu(x, approximate=True)

def _silu(x):
    return jax.nn.silu(x)

def _sigmoid(x):
    return jax.nn.sigmoid(x)

def _layernorm(x, axis=-1, eps=1e-05):
    m = jnp.mean(x, axis=axis, keepdims=True)
    v = jnp.var(x, axis=axis, keepdims=True)
    return (x - m) / jnp.sqrt(v + eps)

def _scatter_add(tgt, idx, src, axis=0):
    return tgt.at[idx].add(src)

def _segment_sum(src, seg, n):
    return jax.ops.segment_sum(src, seg, n)
kernel_name = 'mk_seq_postln_d2_jaxref_r8_2b206b'

def setup_inputs(seed: int=0):
    np.random.seed(seed)
    _w = jnp.asarray

    def _L0_attn_setup():
        import jax, jax.numpy as jnp
        import numpy as np
        from math import sqrt
        DIM, RANK, NHEADS = (128, 64, 16)
        B, T = (2, 256)
        key = jax.random.key(seed)
        kx, kq, kk, kv = jax.random.split(key, 4)
        QK_a = sqrt(6.0 / (RANK + DIM))
        VO_a = sqrt(6.0 / (NHEADS * DIM + DIM))
        x = jax.random.normal(kx, (B, T, DIM), dtype=jnp.float32)
        Q = jax.random.uniform(kq, (NHEADS, RANK, DIM), jnp.float32, -QK_a, QK_a)
        K = jax.random.uniform(kk, (NHEADS, RANK, DIM), jnp.float32, -QK_a, QK_a)
        VO = jax.random.uniform(kv, (NHEADS, DIM, DIM), jnp.float32, -VO_a, VO_a)
        return {'x': x, 'Q': Q, 'K': K, 'VO': VO}
    _L0_attn_in = _L0_attn_setup()

    def _L0_ffn_setup():
        import jax, jax.numpy as jnp
        import numpy as np
        B, S, D = (1, 256, 128)
        E, K, F = (64, 8, 96)
        SF = 96
        C = 64
        ROUTED_SCALE = 1.0

        def _moe_forward(x, router_w, w_gate, w_up, w_down, ws_gate_up, ws_down):
            T = x.shape[0]
            logits = x.astype(jnp.float32) @ router_w.T
            probs = jax.nn.softmax(logits, axis=-1)
            topk_w, topk_ids = jax.lax.top_k(probs, K)
            topk_w = topk_w / jnp.sum(topk_w, axis=-1, keepdims=True)
            topk_w = topk_w.astype(x.dtype)
            N = T * K
            flat_e = topk_ids.reshape(-1)
            flat_w = topk_w.reshape(-1)
            tok = jnp.arange(N) // K
            onehot = flat_e[:, None] == jnp.arange(E)[None, :]
            pos = jnp.cumsum(onehot, axis=0)[jnp.arange(N), flat_e] - 1
            valid = pos < C
            idx = jnp.where(valid, flat_e * C + pos, E * C)
            x_buf = jnp.zeros((E * C + 1, x.shape[1]), x.dtype).at[idx].set(x[tok])
            xb = x_buf[:E * C].reshape(E, C, -1)
            g = jnp.einsum('ecd,edf->ecf', xb, w_gate)
            u = jnp.einsum('ecd,edf->ecf', xb, w_up)
            h = jax.nn.silu(g) * u
            y = jnp.einsum('ecf,efd->ecd', h, w_down).reshape(E * C, -1)
            safe = jnp.where(valid, idx, 0)
            contrib = y[safe] * (flat_w * valid.astype(flat_w.dtype))[:, None]
            routed = jax.ops.segment_sum(contrib, tok, num_segments=T)
            routed = routed * ROUTED_SCALE
            gu = x @ ws_gate_up
            sg, su = (gu[:, :SF], gu[:, SF:])
            shared = jax.nn.silu(sg) * su @ ws_down
            return routed + shared
        key = jax.random.key(seed)
        ks = jax.random.split(key, 7)
        w = 0.02
        return {'hidden_states': jax.random.normal(ks[0], (B, S, D), jnp.float32), 'router_w': jax.random.normal(ks[1], (E, D), jnp.float32) * w, 'w_gate': jax.random.normal(ks[2], (E, D, F), jnp.float32) * w, 'w_up': jax.random.normal(ks[3], (E, D, F), jnp.float32) * w, 'w_down': jax.random.normal(ks[4], (E, F, D), jnp.float32) * w, 'ws_gate_up': jax.random.normal(ks[5], (D, 2 * SF), jnp.float32) * w, 'ws_down': jax.random.normal(ks[6], (SF, D), jnp.float32) * w}
    _L0_ffn_in = _L0_ffn_setup()

    def _L1_attn_setup():
        import jax, jax.numpy as jnp
        import numpy as np
        D_MODEL = 128
        NUM_HEADS = 16
        HEAD_DIM = D_MODEL // NUM_HEADS
        EPS = 1e-06
        key = jax.random.key(seed)
        k1, k2, k3, k4 = jax.random.split(key, 4)
        scale = 1.0 / np.sqrt(D_MODEL)
        return {'x': jax.random.normal(k1, (4, 512, D_MODEL), dtype=jnp.float32), 'Wqkv': jax.random.normal(k2, (3 * D_MODEL, D_MODEL), dtype=jnp.float32) * scale, 'Wout': jax.random.normal(k3, (D_MODEL, D_MODEL), dtype=jnp.float32) * scale, 'bout': jax.random.normal(k4, (D_MODEL,), dtype=jnp.float32) * scale}
    _L1_attn_in = _L1_attn_setup()

    def _L1_ffn_setup():
        import jax, jax.numpy as jnp
        import numpy as np
        D_IN, D_HID = (128, 512)

        def _ternary(key, shape):
            return jax.random.randint(key, shape, -1, 2).astype(jnp.float32)

        def _tlin(x, w, s):
            return jnp.einsum('bsi,oi->bso', x, w) * s
        key = jax.random.key(seed)
        ks = jax.random.split(key, 12)
        inv = lambda fan: 1.0 / np.sqrt(fan).astype(np.float32)
        return {'x': jax.random.normal(ks[0], (4, 256, D_IN), dtype=jnp.float32), 'w1_w': _ternary(ks[1], (D_HID, D_IN)), 'w1_s': jax.random.uniform(ks[2], (D_HID,), dtype=jnp.float32) * inv(D_IN), 'w2_w': _ternary(ks[3], (D_HID, D_IN)), 'w2_s': jax.random.uniform(ks[4], (D_HID,), dtype=jnp.float32) * inv(D_IN), 'h1_w': _ternary(ks[5], (D_HID, D_HID)), 'h1_s': jax.random.uniform(ks[6], (D_HID,), dtype=jnp.float32) * inv(D_HID), 'h2_w': _ternary(ks[7], (D_HID, D_HID)), 'h2_s': jax.random.uniform(ks[8], (D_HID,), dtype=jnp.float32) * inv(D_HID), 'w3_w': _ternary(ks[9], (D_IN, D_HID)), 'w3_s': jax.random.uniform(ks[10], (D_IN,), dtype=jnp.float32) * inv(D_HID)}
    _L1_ffn_in = _L1_ffn_setup()
    _d = {'L0_attn_x': _L0_attn_in['x'], 'L0_attn_Q': _L0_attn_in['Q'], 'L0_attn_K': _L0_attn_in['K'], 'L0_attn_VO': _L0_attn_in['VO'], 'L0_ffn_router_w': _L0_ffn_in['router_w'], 'L0_ffn_w_gate': _L0_ffn_in['w_gate'], 'L0_ffn_w_up': _L0_ffn_in['w_up'], 'L0_ffn_w_down': _L0_ffn_in['w_down'], 'L0_ffn_ws_gate_up': _L0_ffn_in['ws_gate_up'], 'L0_ffn_ws_down': _L0_ffn_in['ws_down'], 'L1_attn_Wqkv': _L1_attn_in['Wqkv'], 'L1_attn_Wout': _L1_attn_in['Wout'], 'L1_attn_bout': _L1_attn_in['bout'], 'L1_ffn_w1_w': _L1_ffn_in['w1_w'], 'L1_ffn_w1_s': _L1_ffn_in['w1_s'], 'L1_ffn_w2_w': _L1_ffn_in['w2_w'], 'L1_ffn_w2_s': _L1_ffn_in['w2_s'], 'L1_ffn_h1_w': _L1_ffn_in['h1_w'], 'L1_ffn_h1_s': _L1_ffn_in['h1_s'], 'L1_ffn_h2_w': _L1_ffn_in['h2_w'], 'L1_ffn_h2_s': _L1_ffn_in['h2_s'], 'L1_ffn_w3_w': _L1_ffn_in['w3_w'], 'L1_ffn_w3_s': _L1_ffn_in['w3_s']}
    _x0 = _d['L0_attn_x']
    _d['L0_attn_x'] = jax.random.normal(jax.random.fold_in(jax.random.key(seed), 1), (32, 256, 128), dtype=_x0.dtype)
    del _x0
    return _d

def reference(L0_attn_x, L0_attn_Q, L0_attn_K, L0_attn_VO, L0_ffn_router_w, L0_ffn_w_gate, L0_ffn_w_up, L0_ffn_w_down, L0_ffn_ws_gate_up, L0_ffn_ws_down, L1_attn_Wqkv, L1_attn_Wout, L1_attn_bout, L1_ffn_w1_w, L1_ffn_w1_s, L1_ffn_w2_w, L1_ffn_w2_s, L1_ffn_h1_w, L1_ffn_h1_s, L1_ffn_h2_w, L1_ffn_h2_s, L1_ffn_w3_w, L1_ffn_w3_s):

    def _L0_attn_ref(x, Q, K, VO):
        import jax, jax.numpy as jnp
        import numpy as np
        from math import sqrt
        DIM, RANK, NHEADS = (128, 64, 16)
        B, T = (2, 256)
        dim = x.shape[-1]
        xq = jnp.einsum('btd,hrd->bthr', x, Q)
        xk = jnp.einsum('bud,hrd->buhr', x, K)
        scores = jnp.einsum('bthr,buhr->bthu', xq, xk) / sqrt(dim)
        attn = jax.nn.softmax(scores, axis=3)
        return jnp.einsum('bthu,bud,hde->bte', attn, x, VO)

    def _L0_ffn_ref(hidden_states, router_w, w_gate, w_up, w_down, ws_gate_up, ws_down):
        import jax, jax.numpy as jnp
        import numpy as np
        B, S, D = (1, 256, 128)
        E, K, F = (64, 8, 96)
        SF = 96
        C = 64
        ROUTED_SCALE = 1.0

        def _moe_forward(x, router_w, w_gate, w_up, w_down, ws_gate_up, ws_down):
            T = x.shape[0]
            logits = x.astype(jnp.float32) @ router_w.T
            probs = jax.nn.softmax(logits, axis=-1)
            topk_w, topk_ids = jax.lax.top_k(probs, K)
            topk_w = topk_w / jnp.sum(topk_w, axis=-1, keepdims=True)
            topk_w = topk_w.astype(x.dtype)
            N = T * K
            flat_e = topk_ids.reshape(-1)
            flat_w = topk_w.reshape(-1)
            tok = jnp.arange(N) // K
            onehot = flat_e[:, None] == jnp.arange(E)[None, :]
            pos = jnp.cumsum(onehot, axis=0)[jnp.arange(N), flat_e] - 1
            valid = pos < C
            idx = jnp.where(valid, flat_e * C + pos, E * C)
            x_buf = jnp.zeros((E * C + 1, x.shape[1]), x.dtype).at[idx].set(x[tok])
            xb = x_buf[:E * C].reshape(E, C, -1)
            g = jnp.einsum('ecd,edf->ecf', xb, w_gate)
            u = jnp.einsum('ecd,edf->ecf', xb, w_up)
            h = jax.nn.silu(g) * u
            y = jnp.einsum('ecf,efd->ecd', h, w_down).reshape(E * C, -1)
            safe = jnp.where(valid, idx, 0)
            contrib = y[safe] * (flat_w * valid.astype(flat_w.dtype))[:, None]
            routed = jax.ops.segment_sum(contrib, tok, num_segments=T)
            routed = routed * ROUTED_SCALE
            gu = x @ ws_gate_up
            sg, su = (gu[:, :SF], gu[:, SF:])
            shared = jax.nn.silu(sg) * su @ ws_down
            return routed + shared
        b, s, d = hidden_states.shape
        x = hidden_states.reshape(-1, d)
        out = _moe_forward(x, router_w, w_gate, w_up, w_down, ws_gate_up, ws_down)
        return out.reshape(b, s, d)

    def _L1_attn_ref(x, Wqkv, Wout, bout):
        import jax, jax.numpy as jnp
        import numpy as np
        D_MODEL = 128
        NUM_HEADS = 16
        HEAD_DIM = D_MODEL // NUM_HEADS
        EPS = 1e-06
        b, t, _ = x.shape
        h, d = (NUM_HEADS, HEAD_DIM)
        qkv = (x @ Wqkv.T).reshape(b, t, 3, h, d).transpose(2, 0, 3, 1, 4)
        q, k, v = (qkv[0], qkv[1], qkv[2])
        q = jax.nn.elu(q) + 1.0
        k = jax.nn.elu(k) + 1.0
        kv = jnp.einsum('bhtd,bhte->bhde', k, v)
        k_sum = k.sum(axis=2)
        z = 1.0 / (jnp.einsum('bhtd,bhd->bht', q, k_sum) + EPS)
        out = jnp.einsum('bhtd,bhde->bhte', q, kv) * z[..., None]
        out = out.transpose(0, 2, 1, 3).reshape(b, t, h * d)
        return out @ Wout.T + bout

    def _L1_ffn_ref(x, w1_w, w1_s, w2_w, w2_s, h1_w, h1_s, h2_w, h2_s, w3_w, w3_s):
        import jax, jax.numpy as jnp
        import numpy as np
        D_IN, D_HID = (128, 512)

        def _ternary(key, shape):
            return jax.random.randint(key, shape, -1, 2).astype(jnp.float32)

        def _tlin(x, w, s):
            return jnp.einsum('bsi,oi->bso', x, w) * s
        h = jax.nn.silu(_tlin(x, w1_w, w1_s)) * _tlin(x, w2_w, w2_s)
        h = jax.nn.gelu(_tlin(h, h1_w, h1_s), approximate=False)
        h = jax.nn.gelu(_tlin(h, h2_w, h2_s), approximate=False)
        return _tlin(h, w3_w, w3_s)
    x = L0_attn_x
    x = _layernorm(x + _L0_attn_ref(x, L0_attn_Q, L0_attn_K, L0_attn_VO), axis=-1)
    x = _layernorm(x + _L0_ffn_ref(x, L0_ffn_router_w, L0_ffn_w_gate, L0_ffn_w_up, L0_ffn_w_down, L0_ffn_ws_gate_up, L0_ffn_ws_down), axis=-1)
    x = _layernorm(x + _L1_attn_ref(x, L1_attn_Wqkv, L1_attn_Wout, L1_attn_bout), axis=-1)
    x = _layernorm(x + _L1_ffn_ref(x, L1_ffn_w1_w, L1_ffn_w1_s, L1_ffn_w2_w, L1_ffn_w2_s, L1_ffn_h1_w, L1_ffn_h1_s, L1_ffn_h2_w, L1_ffn_h2_s, L1_ffn_w3_w, L1_ffn_w3_s), axis=-1)
    return x

_drawn_inputs = setup_inputs


def setup_inputs(seed=0):
    import zlib

    import numpy as np

    out = dict(_drawn_inputs(seed))
    spreads = {}
    factors = {'L0_ffn_router_w': 8.0,
     'L0_ffn_w_gate': 8.0,
     'L0_ffn_w_up': 8.0,
     'L0_ffn_w_down': 8.0,
     'L0_ffn_ws_gate_up': 8.0,
     'L0_ffn_ws_down': 8.0,
     'L1_ffn_w1_w': 8.0,
     'L1_ffn_w1_s': 8.0,
     'L1_ffn_w2_w': 8.0,
     'L1_ffn_w2_s': 8.0,
     'L1_ffn_h1_w': 8.0,
     'L1_ffn_h1_s': 8.0,
     'L1_ffn_h2_w': 8.0,
     'L1_ffn_h2_s': 8.0,
     'L1_ffn_w3_w': 8.0,
     'L1_ffn_w3_s': 8.0}
    for name, (base, spread) in spreads.items():
        noise = np.random.default_rng([zlib.crc32(name.encode()), seed]).standard_normal(out[name].shape)
        drawn = base * np.exp(spread * noise) if base else spread * noise
        out[name] = jnp.asarray(drawn.astype(out[name].dtype))
    for name, factor in factors.items():
        out[name] = (out[name] * factor).astype(out[name].dtype)
    return out
```

```python
from contextlib import ExitStack

import numpy as np

import concourse.bass as bass
from concourse import mybir

F32 = mybir.dt.float32
F32R = mybir.dt.float32r
BF16 = mybir.dt.bfloat16
I32 = mybir.dt.int32
ALU = mybir.AluOpType
ACT = mybir.ActivationFunctionType
AX = mybir.AxisListType

P = 128
SCALE = 1.0 / float(np.sqrt(128.0))
LN_EPS = 1e-5
Z_EPS = 1e-6
CAPACITY = 64.0
HEAD_DIM1 = 8
STAGES = 17
PIECE = 512


class Signal:

    def __init__(self, nc, ctx, name, per=1, credit=0):
        self.sem = ctx.enter_context(nc.semaphore(name))
        self.per = per
        self.credit = credit

    def value(self, b, k=1):
        return b * self.per + (k + self.credit)


def wait(engine, signal, b, k=1):
    v = signal.value(b, k)
    if isinstance(v, int) and v <= 0:
        return
    engine.wait_ge(signal.sem, v)


def wait_alone(engine, signal, b, k, constants):
    engine.wait_ge(constants.sem, 5)
    wait(engine, signal, b, k)


class Order:

    def __init__(self, nc, ctx, engine, name, per):
        self.done = Signal(nc, ctx, name, per)
        self.engine = engine
        self.n = 0

    def start(self, b):
        self.b, self.n = b, 0

    def link(self, instruction):
        self.n += 1
        instruction.then_inc(self.done.sem, 1)
        wait(self.engine, self.done, self.b, self.n)

    def end(self):
        assert self.n == self.done.per, (self.n, self.done.per)


def interleave(attention, stage, a, b, more):
    if a is not None:
        attention("start", a, 0, more)
    if b is not None:
        stage(b, 0)
    for p in range(8):
        if a is not None:
            attention("scores", a, p, more)
        if b is not None:
            stage(b, 2 * p + 1)
        if a is not None:
            attention("values", a, p, more)
        if b is not None:
            stage(b, 2 * p + 2)
    if a is not None:
        attention("end", a, 0, more)


def build(nc, A):
    NB, T, D = A["x"].shape
    H = A["vo"].shape[1] // D
    E = A["wgu"].shape[0] * 4
    FX = A["wd"].shape[1]
    R = A["q"].shape[0]
    DH = A["w1"].shape[1]
    KB = DH // P
    HP = H // 2
    TC = T // P
    assert (T, D, H, E, FX, TC, HP, KB) == (256, 128, 16, 64, 96, 2, 8, 4)
    GROUPS = E // 4
    PAIRS = E // 2

    with ExitStack() as ctx:
        def sb(name, shape, dt=F32):
            return ctx.enter_context(nc.sbuf_tensor(name, shape, dt))

        def bank(name):
            return ctx.enter_context(nc.psum_tensor(name, [P, 512], F32))

        def sig(name, per=1, credit=0):
            return Signal(nc, ctx, name, per, credit)

        xT_in = sb("xT_in", [P, T])
        x_res = sb("x_res", [P, TC, D])
        xh, xl = sb("xh", [P, T], F32R), sb("xl", [P, T], F32R)
        Ah, Al = sb("Ah", [P, H * D], F32R), sb("Al", [P, H * D], F32R)
        VOh, VOl = sb("VOh", [P, H * D], F32R), sb("VOl", [P, H * D], F32R)
        yh, yl = sb("yh", [P, 2, 512], F32R), sb("yl", [P, 2, 512], F32R)
        V = sb("V", [P, TC, H, D + 1])
        Ex = sb("Ex", [P, 2, TC, 512])
        negm = sb("negm", [P, 2, TC, 2], BF16)
        rden = sb("rden", [P, 2, TC])
        acc = sb("acc", [P, TC, D])
        stage_in = sb("stage_in", [P, 4, PIECE])
        w_split = {}
        for name, cols in (("w1", DH), ("w2", DH), ("h1", KB * DH), ("h2", KB * DH),
                           ("wsgu", 2 * FX), ("wq", D), ("wkv", 2 * D)):
            w_split[name] = (sb(name + "h", [P, cols], F32R), sb(name + "l", [P, cols], F32R))
        w3 = sb("w3", [P, KB, D])
        wsd = sb("wsd", [FX, D])
        wout = sb("wout", [P, D])
        rw = sb("rw", [P, E])
        s1 = sb("s1", [P, KB])
        s2 = sb("s2", [P, KB])
        sh1 = sb("sh1", [P, KB])
        sh2 = sb("sh2", [P, KB])
        s1half = sb("s1half", [P, KB])
        s12half = sb("s12half", [P, KB])
        s3 = sb("s3", [P, D])
        bout = sb("bout", [P, D])
        ident = sb("ident", [P, P])
        ident_bf = sb("ident_bf", [P, P], BF16)
        ones_bf = sb("ones_bf", [P, P], BF16)
        before = sb("before", [P, P], BF16)
        headmask = sb("headmask", [P, P])
        ones = sb("ones", [P, P])
        minus_half = sb("minus_half", [P, TC])
        ln_eps = sb("ln_eps", [P, TC])
        spacer = sb("spacer", [P, 1])
        FF = sb("FF", [P, 3, KB * T])
        a1, a2, a3 = FF[:, 0, :], FF[:, 1, :], FF[:, 2, :]
        a1h, a1l = sb("a1h", [P, KB * T], F32R)[:], sb("a1l", [P, KB * T], F32R)[:]
        a2h, a2l = sb("a2h", [P, KB * T], F32R)[:], sb("a2l", [P, KB * T], F32R)[:]
        fth = sb("fth", [P, 512])
        ft = sb("ft", [P, 512])
        stats = sb("stats", [P, TC, 6])
        mv = sb("mv", [P, 4, TC, 2])
        veps = sb("veps", [P, TC])
        rstd = sb("rstd", [P, 4, TC])
        x1, x2, x3 = sb("x1", [P, TC, D]), sb("x2", [P, TC, D]), sb("x3", [P, TC, D])
        x2b = sb("x2b", [P, TC, D])
        res = sb("res", [P, TC, D])
        yout = sb("yout", [P, TC, D])
        x1T = sb("x1T", [P, T])
        x1h, x1l = sb("x1h", [P, T], F32R), sb("x1l", [P, T], F32R)
        x2h, x2l = sb("x2h", [P, T], F32R), sb("x2l", [P, T], F32R)
        x3h, x3l = sb("x3h", [P, T], F32R), sb("x3l", [P, T], F32R)
        top8 = sb("top8", [P, TC, 8])
        rest = sb("rest", [P, TC, E])
        mask = sb("mask", [P, TC, E], BF16)
        negmax = sb("negmax", [P, TC])
        ew = sb("ew", [P, TC, E])
        wm = sb("wm", [P, TC, E])
        wsum = sb("wsum", [P, TC])
        wrec = sb("wrec", [P, TC])
        pos = sb("pos", [P, TC, E])
        coef = sb("coef", [P, TC, E])
        taken = sb("taken", [P, E])
        live = sb("live", [P, E])
        livemax = sb("livemax", [P, 1])
        flag = sb("flag", [P, 1], I32)
        sth = sb("sth", [FX, T])
        st = sb("st", [FX, T])
        hs = sb("hs", [FX, T])
        kmin, kmax, ke, kf = (sb(n, [P, TC, D]) for n in ("kmin", "kmax", "ke", "kf"))
        qmin, qmax, qe, qf = (sb(n, [P, T]) for n in ("qmin", "qmax", "qe", "qf"))
        vt = sb("vt", [P, TC, D + 1])
        kvz = sb("kvz", [P, 2 * D])
        den = sb("den", [P, TC, D])
        dinv = sb("dinv", [P, TC, D])
        o1 = sb("o1", [P, TC, D])
        oT = sb("oT", [P, T])
        wgu_in = sb("wgu_in", [P, 2, 4 * 2 * FX])
        wd_in = sb("wd_in", [FX, 2, 4 * D])
        PAIR = TC * 2 * FX
        rth = a1[:, 0:PAIR].rearrange("p (c e n) -> p c e n", c=TC, e=2)
        rt = a1[:, PAIR:2 * PAIR].rearrange("p (c e n) -> p c e n", c=TC, e=2)
        rh = a2[:, 0:2 * PAIR].rearrange("p (s c e n) -> p s c e n", s=2, c=TC, e=2)
        rhT = a3[0:FX, :].rearrange("p (s n) -> p s n", s=2)
        coef8 = sb("coef8", [P, TC, 8])

        Y, G = bank("Y"), bank("G")
        S = [bank("S0"), bank("S1")]
        O = [bank("O0"), bank("O1")]
        P0, P1 = bank("P0"), bank("P1")

        x_ld, xT_ld = sig("x_ld", 16), sig("xT_ld", 16)
        xh_sb, xl_sb = sig("xh_sb"), sig("xl_sb")
        y_ps, yh_sb, yl_sb = sig("y_ps", HP), sig("yh_sb", HP), sig("yl_sb", HP)
        g_ps, negm_sb = sig("g_ps", 2 * HP), sig("negm_sb", 2 * HP)
        s_ps, ex_sb = sig("s_ps", 2 * HP), sig("ex_sb", 2 * HP)
        v_ps, v_sb = sig("v_ps", 8), sig("v_sb", 8)
        av_ps, comb = sig("av_ps", H), sig("comb", H)
        var_sb, rstd_sb = sig("var_sb", 4), sig("rstd_sb", 4)
        x1_sb, x1T_ps, x1T_sb, x1h_sb, x1l_sb = (sig(n) for n in ("x1_sb", "x1T_ps", "x1T_sb", "x1h_sb", "x1l_sb"))
        logits_ps, mask_sb, ew_sb = sig("logits_ps"), sig("mask_sb"), sig("ew_sb")
        sgu_ps, sth_sb, hs_sb, sd_ps = sig("sgu_ps"), sig("sth_sb"), sig("hs_sb"), sig("sd_ps")
        cum_ps, coef_sb = sig("cum_ps"), sig("coef_sb")
        x2_sb, x2T_ps, x2h_sb, x2l_sb, x2b_sb = (sig(n) for n in ("x2_sb", "x2T_ps", "x2h_sb", "x2l_sb", "x2b_sb"))
        moe_read = sig("moe_read")
        kv_ps, q_ps, kvm_sb, qm_sb, kve_sb, qe_sb, kf_sb, qf_sb = (
            sig(n) for n in ("kv_ps", "q_ps", "kvm_sb", "qm_sb", "kve_sb", "qe_sb", "kf_sb", "qf_sb"))
        kvp_ps, kvz_sb, nd_ps, o1_sb, oT_ps, oT_sb, wo_ps = (
            sig(n) for n in ("kvp_ps", "kvz_sb", "nd_ps", "o1_sb", "oT_ps", "oT_sb", "wo_ps"))
        wo_read = sig("wo_read")
        x3_sb, x3T_ps, x3h_sb, x3l_sb = (sig(n) for n in ("x3_sb", "x3T_ps", "x3h_sb", "x3l_sb"))
        w12_ps, fth_sb, a1_sb, a1h_sb, a1l_sb = (sig(n, 2) for n in ("w12_ps", "fth_sb", "a1_sb", "a1h_sb", "a1l_sb"))
        h1_ps, a2_sb, a2h_sb, a2l_sb = (sig(n, 2) for n in ("h1_ps", "a2_sb", "a2h_sb", "a2l_sb"))
        h2_ps, a3_sb = sig("h2_ps", 2), sig("a3_sb", 2)
        w3_ps, w3_read, yout_sb, out_st = sig("w3_ps"), sig("w3_read"), sig("yout_sb"), sig("out_st", 16)
        rw_ld = [sig(f"rw_ld{i}", 16 * GROUPS) for i in range(2)]
        rgu_ps, rth_sb, rt_sb = sig("rgu_ps", E), sig("rth_sb", E), sig("rt_sb", E, 2)
        rh_sb = sig("rh_sb", E, 4)
        rT_ps, rhT_sb = sig("rT_ps", PAIRS, 2), sig("rhT_sb", PAIRS, 2)
        rd_ps = sig("rd_ps", PAIRS, 4)
        c8_sb = sig("c8_sb", 8)
        const_sb, half_sb, ones_sb = sig("const_sb"), sig("half_sb"), sig("ones_sb")
        small_ld, qk_ld = sig("small_ld"), sig("qk_ld")
        vo_ld = [sig(f"vo_ld{i}") for i in range(4)]
        split_ld = [sig(f"split_ld{i}") for i in range(4)]
        vo_split = sig("vo_split")
        a_ps, ah_sb, al_sb = sig("a_ps"), sig("ah_sb"), sig("al_sb")
        split_hi, split_lo = sig("split_hi"), sig("split_lo")

        q_in = Ex[0:R, :, :, :].rearrange("p a b c -> p (a b c)")
        k_in = FF[0:R, 0:2, :].rearrange("p a b -> p (a b)")
        SMALL = [("w3", w3[:]), ("wsd", wsd[:]), ("wout", wout[:]), ("rw", rw[:]), ("s1", s1[:]), ("s2", s2[:]),
                 ("sh1", sh1[:]), ("sh2", sh2[:])]
        ROWS = [("s3", s3), ("bout", bout)]
        PIECES = [(name, c, min(PIECE, w_split[name][0].shape[1] - c))
                  for name in ("wsgu", "wkv", "wq", "w1", "w2", "h1", "h2")
                  for c in range(0, w_split[name][0].shape[1], PIECE)]

        block = ctx.enter_context(nc.Block())

        @block.sync
        def _(sp):
            sp.dma_start(q_in, A["q"]).then_inc(qk_ld.sem, 16)
            sp.dma_start(k_in, A["k"]).then_inc(qk_ld.sem, 16)
            sp.dma_start(xT_in[:], A["xT"][0]).then_inc(xT_ld.sem, 16)
            sp.dma_start(x_res[:], A["x"][0].rearrange("(c p) d -> p c d", p=P)).then_inc(x_ld.sem, 16)
            for i in range(4):
                sp.dma_start(stage_in[:, i, :], A["vo"][:, i * PIECE:(i + 1) * PIECE]).then_inc(vo_ld[i].sem, 16)
            for name, tile in SMALL:
                sp.dma_start(tile, A[name]).then_inc(small_ld.sem, 16)
            for name, tile in ROWS:
                sp.dma_start(tile[:], A[name].partition_broadcast(P)).then_inc(small_ld.sem, 16)
            for n, (name, c, w) in enumerate(PIECES):
                if n < 4:
                    sp.wait_ge(vo_split.sem, n + 1)
                else:
                    sp.wait_ge(split_lo.sem, n - 3)
                sp.dma_start(stage_in[:, n % 4, 0:w], A[name][:, c:c + w]).then_inc(split_ld[n % 4].sem, 16)

            def experts_in(b):
                wait_alone(sp, coef_sb, b, 1, const_sb)
                on = sp.value_load(flag[0:1, 0:1], min_val=0, max_val=1)
                with sp.If(on > 0):
                    with sp.Fori(0, GROUPS // 2) as it:
                        for half in range(2):
                            wait(sp, rd_ps, b, it * 4 + 2 * half - 2)
                            g = it * 2 + half
                            sp.dma_start(wgu_in[:, half, :], A["wgu"][bass.ds(g, 1)].rearrange("a p n -> (a p) n"))\
                                .then_inc(rw_ld[half].sem, 16)
                            sp.dma_start(wd_in[:, half, :], A["wd"][bass.ds(g, 1)].rearrange("a p n -> (a p) n"))\
                                .then_inc(rw_ld[half].sem, 16)
                with sp.Else():
                    for slot in rw_ld:
                        sp.sem_inc(slot.sem, slot.per)

            def rows(ap, b):
                if isinstance(b, int):
                    return ap[b]
                return ap[bass.ds(b, 1)].rearrange("a p d -> (a p) d")

            def step(a, b, more):
                if a is not None and more:
                    wait(sp, xl_sb, a)
                    sp.dma_start(xT_in[:], rows(A["xT"], a + 1)).then_inc(xT_ld.sem, 16)
                if b is not None:
                    experts_in(b)
                if a is not None and more:
                    wait(sp, comb, a, 1)
                    sp.dma_start(x_res[:], rows(A["x"], a + 1).rearrange("(c p) d -> p c d", p=P)).then_inc(x_ld.sem, 16)
                if b is not None:
                    wait(sp, yout_sb, b)
                    sp.dma_start(rows(A["out"], b).rearrange("(c p) d -> p c d", p=P), yout[:]).then_inc(out_st.sem, 16)

            step(0, None, True)
            step(1, 0, True)
            with sp.Fori(2, NB - 1) as i:
                step(i, i - 1, True)
            step(NB - 1, NB - 2, False)
            step(None, NB - 1, False)
            wait(sp, out_st, NB - 1, 16)

        @block.gpsimd
        def _(pool):
            nc.gpsimd.memset(ones[:], 1.0).then_inc(ones_sb.sem, 1)
            nc.gpsimd.memset(ones_bf[:], 1.0).then_inc(ones_sb.sem, 1)
            nc.gpsimd.memset(minus_half[:], -0.5).then_inc(ones_sb.sem, 1)
            nc.gpsimd.memset(ln_eps[:], LN_EPS).then_inc(ones_sb.sem, 1)
            nc.gpsimd.memset(V[:, :, :, D:D + 1], 1.0).then_inc(ones_sb.sem, 1)
            nc.gpsimd.memset(vt[:, :, D:D + 1], 1.0).then_inc(ones_sb.sem, 1)
            pool.wait_ge(ones_sb.sem, 6)
            for tile, src in ((ident, ones), (ident_bf, ones_bf)):
                nc.gpsimd.affine_select(out=tile[:], in_=src[:], compare_op=ALU.is_equal, fill=0.0, base=0,
                                        pattern=[[-1, P]], channel_multiplier=1).then_inc(const_sb.sem, 1)
            nc.gpsimd.affine_select(out=before[:], in_=ones_bf[:], compare_op=ALU.is_gt, fill=0.0, base=0,
                                    pattern=[[1, P]], channel_multiplier=-1).then_inc(const_sb.sem, 1)
            grid = headmask[:].rearrange("p (g e) -> p g e", e=HEAD_DIM1)
            steps = [[-HEAD_DIM1, P // HEAD_DIM1], [0, HEAD_DIM1]]
            nc.gpsimd.affine_select(out=grid, in_=ones[:].rearrange("p (g e) -> p g e", e=HEAD_DIM1),
                                    compare_op=ALU.is_ge, fill=0.0, base=0, pattern=steps,
                                    channel_multiplier=1).then_inc(const_sb.sem, 1)
            pool.wait_ge(const_sb.sem, 4)
            nc.gpsimd.affine_select(out=grid, in_=grid, compare_op=ALU.is_ge, fill=0.0, base=HEAD_DIM1 - 1,
                                    pattern=[[HEAD_DIM1, P // HEAD_DIM1], [0, HEAD_DIM1]],
                                    channel_multiplier=-1).then_inc(const_sb.sem, 1)
            for n, (name, c, w) in enumerate(PIECES):
                hi, lo = w_split[name]
                pool.wait_ge(split_ld[n % 4].sem, 16 * (n // 4 + 1))
                nc.gpsimd.tensor_copy(hi[:, c:c + w], stage_in[:, n % 4, 0:w]).then_inc(split_hi.sem, 1)
                pool.wait_ge(split_hi.sem, n + 1)
                nc.gpsimd.tensor_tensor(lo[:, c:c + w], stage_in[:, n % 4, 0:w], hi[:, c:c + w].bitcast(F32),
                                        ALU.subtract).then_inc(split_lo.sem, 1)

            veps_sb = sig("veps_sb", 4)

            def inverse_std(b, n):
                wait(pool, var_sb, b, n + 1)
                nc.gpsimd.tensor_tensor(veps[:], mv[:, n, :, 1], ln_eps[:], ALU.add).then_inc(veps_sb.sem, 1)
                wait(pool, veps_sb, b, n + 1)
                nc.gpsimd.tensor_tensor(rstd[:, n, :], veps[:], minus_half[:], ALU.pow).then_inc(rstd_sb.sem, 1)

            def low(out, full, hi, done):
                nc.gpsimd.tensor_tensor(out, full, hi.bitcast(F32), ALU.subtract).then_inc(done.sem, 1)

            def stage(b, k):
                if k == 0:
                    inverse_std(b, 0)
                    wait(pool, x1h_sb, b)
                    low(x1l[:], x1T[:], x1h[:], x1l_sb)
                elif k == 2:
                    inverse_std(b, 1)
                    wait(pool, x2_sb, b)
                    wait(pool, wo_read, b, 0)
                    for c in range(TC):
                        ins = nc.gpsimd.tensor_tensor(x2b[:, c, :], x2[:, c, :], bout[:], ALU.add)
                    ins.then_inc(x2b_sb.sem, 1)
                elif k == 8:
                    inverse_std(b, 2)
                elif k in (10, 11):
                    n = k - 10
                    wait(pool, a1h_sb, b, n + 1)
                    low(a1l[:, 512 * n:512 * n + 512], a1[:, 512 * n:512 * n + 512],
                        a1h[:, 512 * n:512 * n + 512], a1l_sb)
                elif k in (12, 13):
                    n = k - 12
                    wait(pool, a2h_sb, b, n + 1)
                    low(a2l[:, 512 * n:512 * n + 512], a2[:, 512 * n:512 * n + 512],
                        a2h[:, 512 * n:512 * n + 512], a2l_sb)
                elif k == 16:
                    inverse_std(b, 3)

            pool.wait_ge(small_ld.sem, 16 * (len(SMALL) + len(ROWS)))
            for k in range(STAGES):
                stage(0, k)
            with pool.Fori(1, NB) as b:
                for k in range(STAGES):
                    stage(b, k)

        @block.tensor
        def _(pe):
            mm = nc.tensor.matmul

            def three(out, wh, wl, mh, ml):
                mm(out, wh, mh, start=True, stop=False)
                mm(out, wh, ml, start=False, stop=False)
                return mm(out, wl, mh, start=False, stop=True)

            pe.sem_inc(rT_ps.sem, rT_ps.credit)
            pe.sem_inc(rd_ps.sem, rd_ps.credit)
            pe.wait_ge(qk_ld.sem, 32)
            for n in range(4):
                if n >= 2:
                    pe.wait_ge(al_sb.sem, n - 1)
                for j in range(4):
                    h = 4 * n + j
                    ins = mm(S[n % 2][:, j * D:(j + 1) * D], q_in[:, h * D:(h + 1) * D], k_in[:, h * D:(h + 1) * D],
                             start=True, stop=True)
                ins.then_inc(a_ps.sem, 1)

            def y(a, p):
                wait(pe, yl_sb, a, p)
                for j in range(2):
                    w = slice((2 * p + j) * D, (2 * p + j + 1) * D)
                    ins = three(Y[:, j * T:(j + 1) * T], Ah[:, w], Al[:, w], xh[:], xl[:])
                ins.then_inc(y_ps.sem, 1)

            def guard(a, p, tc):
                wait(pe, yh_sb, a, p + 1)
                wait(pe, negm_sb, a, 2 * p + tc)
                for j in range(2):
                    c = j * T + tc * P
                    ins = mm(G[:, j * T:(j + 1) * T], yh[:, p % 2, c:c + P], xh[:], start=True, stop=True)
                ins.then_inc(g_ps.sem, 1)

            def scores(a, p, uc):
                wait(pe, yl_sb, a, p + 1)
                wait(pe, ex_sb, a, 2 * p + uc - 1)
                if p == 0 and uc == 0 and isinstance(a, int) and a == 0:
                    pe.wait_ge(al_sb.sem, 4)
                u = slice(uc * P, (uc + 1) * P)
                mm(S[uc][:], xh[:, u], yh[:, p % 2, :], start=True, stop=False)
                mm(S[uc][:], xh[:, u], yl[:, p % 2, :], start=False, stop=False)
                mm(S[uc][:], xl[:, u], yh[:, p % 2, :], start=False, stop=False)

            def minus_max(a, p, uc):
                if uc == 0:
                    wait(pe, negm_sb, a, 2 * p + 2)
                for j in range(2):
                    for tc in range(TC):
                        c = j * T + tc * P
                        ins = mm(S[uc][:, c:c + P], negm[:, p % 2, tc, j:j + 1].to_broadcast([P, P]), ident_bf[:],
                                 start=False, stop=(j == 1 and tc == TC - 1))
                ins.then_inc(s_ps.sem, 1)

            def v_piece(a, n):
                uc, nb = n // 4, n % 4
                if n < 2:
                    wait(pe, comb, a, 0)
                else:
                    wait(pe, v_sb, a, n - 1)
                u = slice(uc * P, (uc + 1) * P)
                w = slice(nb * 512, (nb + 1) * 512)
                three(O[n % 2][:], xh[:, u], xl[:, u], VOh[:, w], VOl[:, w]).then_inc(v_ps.sem, 1)

            def weigh(a, p):
                wait(pe, ex_sb, a, 2 * p + 2)
                if p == 0:
                    wait(pe, v_sb, a, 8)
                    wait(pe, moe_read, a - 1)
                for j in range(2):
                    h = 2 * p + j
                    if h >= 2:
                        wait(pe, comb, a, h - 1)
                    for tc in range(TC):
                        c = j * T + tc * P
                        for uc in range(TC):
                            ins = mm(O[j][:, tc * T:tc * T + D + 1], Ex[:, p % 2, uc, c:c + P], V[:, uc, h, :],
                                     start=(uc == 0), stop=(uc == TC - 1))
                    ins.then_inc(av_ps.sem, 1)

            def attention(part, a, p, more):
                if part == "start":
                    wait(pe, xl_sb, a)
                    y(a, 0)
                    for n in range(4):
                        v_piece(a, n)
                    guard(a, 0, 0)
                    y(a, 1)
                    for n in range(4, 8):
                        v_piece(a, n)
                    guard(a, 0, 1)
                elif part == "scores":
                    scores(a, p, 0)
                    if p + 1 < HP:
                        guard(a, p + 1, 0)
                    scores(a, p, 1)
                    minus_max(a, p, 0)
                    minus_max(a, p, 1)
                elif part == "values":
                    if p + 2 < HP:
                        y(a, p + 2)
                    if p + 1 < HP:
                        guard(a, p + 1, 1)
                    if p >= 1:
                        weigh(a, p - 1)
                else:
                    weigh(a, HP - 1)

            def turn(out, src):
                for c in range(TC):
                    ins = nc.tensor.transpose(out[:, c * P:(c + 1) * P], src[:, c, :], ident[:])
                return ins

            def experts(b, a):
                wait_alone(pe, coef_sb, b, 1, const_sb)
                on = pe.value_load(flag[0:1, 0:1], min_val=0, max_val=1)
                with pe.If(on > 0):
                    def gate_up(it, l):
                        q = it * 4 + l
                        grp = l // 2
                        wait(pe, rw_ld[grp], b, it * 32 + 32)
                        banks = (P0, P1) if l % 2 == 0 else S
                        for c in range(TC):
                            wait(pe, rh_sb, b, q * 2 + c - 3)
                            w = wgu_in[:, grp, (l % 2) * 4 * FX:(l % 2 + 1) * 4 * FX]
                            mm(banks[c][:, 0:4 * FX], x1T[:, c * P:(c + 1) * P], w, start=True, stop=True)\
                                .then_inc(rgu_ps.sem, 1)

                    def turn_down(it, l):
                        q = it * 4 + l
                        wait(pe, rh_sb, b, q * 2 + 2)
                        wait(pe, rhT_sb, b, q)
                        for c in range(TC):
                            for e in range(2):
                                n = c * 2 + e
                                ins = nc.tensor.transpose(O[0][0:FX, n * P:(n + 1) * P], rh[:, l % 2, c, e, :],
                                                          ident[:])
                        ins.then_inc(rT_ps.sem, 1)

                    def down(it, l):
                        q = it * 4 + l
                        wait(pe, rhT_sb, b, q + 1)
                        for c in range(TC):
                            for e in range(2):
                                n = c * 2 + e
                                k = (l % 2) * 2 + e
                                ins = mm(O[1][:, c * P:(c + 1) * P], rhT[:, l % 2, n * P:(n + 1) * P],
                                         wd_in[:, l // 2, k * D:(k + 1) * D], start=False, stop=False,
                                         skip_group_check=True)
                        ins.then_inc(rd_ps.sem, 1)

                    def pairs(it, last):
                        for l in range(4):
                            if l < 3:
                                gate_up(it, l + 1)
                            elif not last:
                                gate_up(it + 1, 0)
                            turn_down(it, l)
                            down(it, l)

                    gate_up(0, 0)
                    with pe.Fori(0, 7) as it:
                        pairs(it, False)
                    pairs(7, True)
                with pe.Else():
                    pe.sem_inc(rgu_ps.sem, E)
                    pe.sem_inc(rT_ps.sem, PAIRS)
                    pe.sem_inc(rd_ps.sem, PAIRS)

            def stage(b, k):
                if k == 0:
                    wait(pe, x1_sb, b)
                    wait(pe, a3_sb, b, 0)
                    turn(P1, x1).then_inc(x1T_ps.sem, 1)
                elif k == 1:
                    wait(pe, x1T_sb, b)
                    wait(pe, w3_read, b, 0)
                    for c in range(TC):
                        ins = mm(P0[:, c * E:(c + 1) * E], x1T[:, c * P:(c + 1) * P], rw[:], start=True, stop=True)
                    ins.then_inc(logits_ps.sem, 1)
                    wait(pe, x1l_sb, b)
                    wh, wl = w_split["wsgu"]
                    for n in range(2):
                        w = slice(n * FX, (n + 1) * FX)
                        ins = three(P1[0:FX, n * T:(n + 1) * T], wh[:, w], wl[:, w], x1h[:], x1l[:])
                    ins.then_inc(sgu_ps.sem, 1)
                elif k == 2:
                    wait(pe, mask_sb, b)
                    wait(pe, ew_sb, b)
                    m0, m1 = mask[:, 0, :], mask[:, 1, :]
                    mm(P0[:, 0:E], before[:], m0, start=True, stop=True)
                    mm(P0[:, E:2 * E], before[:], m1, start=True, stop=False)
                    mm(P0[:, E:2 * E], ones_bf[:], m0, start=False, stop=True)
                    mm(P0[:, 2 * E:3 * E], ones_bf[:], m0, start=True, stop=False)
                    mm(P0[:, 2 * E:3 * E], ones_bf[:], m1, start=False, stop=True).then_inc(cum_ps.sem, 1)
                    wait(pe, hs_sb, b)
                    if isinstance(b, int) and b == NB - 1:
                        wait(pe, comb, b, H)
                    else:
                        wait(pe, v_sb, b + 1, 8)
                        wait(pe, ex_sb, b + 1, 2)
                    for c in range(TC):
                        ins = mm(O[1][:, c * P:(c + 1) * P], hs[:, c * P:(c + 1) * P], wsd[:], start=(c == 0),
                                 stop=False, skip_group_check=True)
                    ins.then_inc(sd_ps.sem, 1)
                    experts(b, None)
                elif k == 3:
                    wait(pe, x2_sb, b)
                    turn(P1, x2).then_inc(x2T_ps.sem, 1)
                elif k == 4:
                    wait(pe, x2l_sb, b)
                    wh, wl = w_split["wkv"]
                    for c in range(TC):
                        t = slice(c * P, (c + 1) * P)
                        ins = three(P0[:, c * 2 * D:(c + 1) * 2 * D], x2h[:, t], x2l[:, t], wh[:], wl[:])
                    ins.then_inc(kv_ps.sem, 1)
                    wh, wl = w_split["wq"]
                    three(P1[:, 0:T], wh[:], wl[:], x2h[:], x2l[:]).then_inc(q_ps.sem, 1)
                elif k == 5:
                    wait(pe, kf_sb, b)
                    for c in range(TC):
                        ins = mm(P0[:, 0:D + 1], kf[:, c, :], vt[:, c, :], start=(c == 0), stop=(c == TC - 1))
                    ins.then_inc(kvp_ps.sem, 1)
                elif k == 6:
                    wait(pe, kvz_sb, b)
                    wait(pe, qf_sb, b)
                    for c in range(TC):
                        ins = mm(P1[:, c * 2 * D:(c + 1) * 2 * D], qf[:, c * P:(c + 1) * P], kvz[:], start=True,
                                 stop=True)
                    ins.then_inc(nd_ps.sem, 1)
                elif k == 7:
                    wait(pe, o1_sb, b)
                    turn(P0, o1).then_inc(oT_ps.sem, 1)
                elif k == 8:
                    wait(pe, oT_sb, b)
                    for c in range(TC):
                        ins = mm(P1[:, c * D:(c + 1) * D], oT[:, c * P:(c + 1) * P], wout[:], start=True, stop=True)
                    ins.then_inc(wo_ps.sem, 1)
                elif k == 9:
                    wait(pe, x3_sb, b)
                    turn(P0, x3).then_inc(x3T_ps.sem, 1)
                elif k in (10, 11):
                    n = k - 10
                    wait(pe, x3l_sb, b)
                    if n:
                        wait(pe, a1_sb, b, 1)
                    for out, name in ((P0, "w1"), (P1, "w2")):
                        wh, wl = w_split[name]
                        for j in range(2):
                            w = slice((2 * n + j) * P, (2 * n + j + 1) * P)
                            ins = three(out[:, j * T:(j + 1) * T], wh[:, w], wl[:, w], x3h[:], x3l[:])
                    ins.then_inc(w12_ps.sem, 1)
                elif k in (12, 13, 14, 15):
                    n = k % 2
                    name, mh, ml, hi, lo, full, done = (
                        ("h1", a1h, a1l, a1h_sb, a1l_sb, a1_sb, h1_ps) if k < 14
                        else ("h2", a2h, a2l, a2h_sb, a2l_sb, a2_sb, h2_ps))
                    if k == 12:
                        wait(pe, a1_sb, b, 2)
                    if k >= 14:
                        wait(pe, a2_sb, b, n + 1)
                    out = P1 if n else P0
                    wh, wl = w_split[name]
                    wait(pe, lo, b, 2)
                    for j in range(2):
                        for kb in range(KB):
                            w = slice(kb * DH + (2 * n + j) * P, kb * DH + (2 * n + j + 1) * P)
                            t = slice(kb * T, (kb + 1) * T)
                            o = out[:, j * T:(j + 1) * T]
                            mm(o, wh[:, w], mh[:, t], start=(kb == 0), stop=False)
                            mm(o, wh[:, w], ml[:, t], start=False, stop=False)
                            ins = mm(o, wl[:, w], mh[:, t], start=False, stop=(kb == KB - 1))
                    ins.then_inc(done.sem, 1)
                elif k == 16:
                    wait(pe, a3_sb, b, 2)
                    for c in range(TC):
                        for kb in range(KB):
                            ins = mm(P0[:, c * D:(c + 1) * D], a3[:, kb * T + c * P:kb * T + (c + 1) * P], w3[:, kb, :],
                                     start=(kb == 0), stop=(kb == KB - 1))
                    ins.then_inc(w3_ps.sem, 1)

            pe.wait_ge(al_sb.sem, 4)
            pe.wait_ge(vo_split.sem, 4)
            pe.wait_ge(const_sb.sem, 5)
            pe.wait_ge(ones_sb.sem, 6)
            interleave(attention, stage, 0, None, True)
            pe.wait_ge(split_lo.sem, len(PIECES))
            pe.wait_ge(small_ld.sem, 16 * (len(SMALL) + len(ROWS)))
            interleave(attention, stage, 1, 0, True)
            with pe.Fori(2, NB - 1) as i:
                interleave(attention, stage, i, i - 1, True)
            interleave(attention, stage, NB - 1, NB - 2, False)
            interleave(attention, stage, None, NB - 1, False)

        @block.scalar
        def _(act):
            act_do = nc.scalar.activation
            act.sem_inc(rhT_sb.sem, rhT_sb.credit)
            for n in range(4):
                act.wait_ge(a_ps.sem, n + 1)
                act_do(Ah[:, n * 512:(n + 1) * 512], S[n % 2][:], ACT.Copy).then_inc(ah_sb.sem, 1)
            act.wait_ge(xT_ld.sem, 16)
            act_do(xh[:], xT_in[:], ACT.Copy).then_inc(xh_sb.sem, 1)

            def y_high(a, p):
                wait(act, y_ps, a, p + 1)
                wait(act, s_ps, a, 2 * p - 2)
                act_do(yh[:, p % 2, :], Y[:], ACT.Copy).then_inc(yh_sb.sem, 1)

            def v_copy(a, n):
                wait(act, v_ps, a, n + 1)
                if n == 0:
                    wait(act, av_ps, a, 0)
                uc, nb = n // 4, n % 4
                act_do(V[:, uc, 4 * nb:4 * nb + 4, 0:D], O[n % 2][:].rearrange("p (h d) -> p h d", d=D), ACT.Copy)\
                    .then_inc(v_sb.sem, 1)

            def attention(part, a, p, more):
                if part == "start":
                    y_high(a, 0)
                    for n in range(4):
                        v_copy(a, n)
                    y_high(a, 1)
                    for n in range(4, 8):
                        v_copy(a, n)
                elif part == "scores":
                    for uc in range(TC):
                        wait(act, s_ps, a, 2 * p + uc + 1)
                        wait(act, av_ps, a, 2 * p - 2)
                        act_do(Ex[:, p % 2, uc, :], S[uc][:], ACT.Exp, scale=SCALE).then_inc(ex_sb.sem, 1)
                elif part == "values":
                    if p + 2 < HP:
                        y_high(a, p + 2)
                    if p == HP - 1 and more:
                        wait(act, xT_ld, a + 1, 16)
                        wait(act, s_ps, a, 2 * HP)
                        act_do(xh[:], xT_in[:], ACT.Copy).then_inc(xh_sb.sem, 1)

            def experts(b):
                on = act.value_load(flag[0:1, 0:1], min_val=0, max_val=1)
                with act.If(on > 0):
                    def tanh(it, l):
                        q = it * 4 + l
                        banks = (P0, P1) if l % 2 == 0 else S
                        for c in range(TC):
                            wait(act, rgu_ps, b, q * 2 + c + 1)
                            wait(act, rt_sb, b, q * 2 + c - 1)
                            gate = banks[c][:, 0:4 * FX].rearrange("p (e n) -> p e n", e=2)[:, :, 0:FX]
                            act_do(rth[:, c, :, :], gate, ACT.Tanh, scale=0.5).then_inc(rth_sb.sem, 1)

                    def hidden(it, l):
                        q = it * 4 + l
                        wait(act, rT_ps, b, q + 1)
                        wait(act, rd_ps, b, q - 1)
                        act_do(rhT[:, l % 2, :], O[0][0:FX, :], ACT.Copy).then_inc(rhT_sb.sem, 1)

                    tanh(0, 0)
                    with act.Fori(0, 7) as it:
                        for l in range(4):
                            if l < 3:
                                tanh(it, l + 1)
                            else:
                                tanh(it + 1, 0)
                            hidden(it, l)
                    for l in range(4):
                        if l < 3:
                            tanh(7, l + 1)
                        hidden(7, l)
                with act.Else():
                    act.sem_inc(rth_sb.sem, E)
                    act.sem_inc(rhT_sb.sem, PAIRS)

            def stage(b, k):
                if k == 0:
                    wait(act, x1T_ps, b)
                    act_do(x1T[:], P1[:, 0:T], ACT.Copy).then_inc(x1T_sb.sem, 1)
                    act_do(x1h[:], P1[:, 0:T], ACT.Copy).then_inc(x1h_sb.sem, 1)
                elif k == 1:
                    wait(act, sgu_ps, b)
                    act_do(sth[:], P1[0:FX, 0:T], ACT.Tanh, scale=0.5).then_inc(sth_sb.sem, 1)
                    wait(act, mask_sb, b)
                    for c in range(TC):
                        ins = act_do(ew[:, c, :], P0[:, c * E:(c + 1) * E], ACT.Exp, bias=negmax[:, c:c + 1])
                    ins.then_inc(ew_sb.sem, 1)
                elif k == 2:
                    wait_alone(act, coef_sb, b, 1, const_sb)
                    experts(b)
                elif k == 3:
                    wait(act, x2T_ps, b)
                    act_do(x2h[:], P1[:, 0:T], ACT.Copy).then_inc(x2h_sb.sem, 1)
                elif k == 4:
                    wait(act, kvm_sb, b)
                    v = P0[:].rearrange("p (c n) -> p c n", c=TC)[:, :, D:2 * D]
                    act_do(vt[:, :, 0:D], v, ACT.Copy)
                    act_do(ke[:], kmin[:], ACT.Exp).then_inc(kve_sb.sem, 1)
                    wait(act, qm_sb, b)
                    act_do(qe[:], qmin[:], ACT.Exp).then_inc(qe_sb.sem, 1)
                elif k == 7:
                    wait(act, oT_ps, b)
                    act_do(oT[:], P0[:, 0:T], ACT.Copy).then_inc(oT_sb.sem, 1)
                elif k == 9:
                    wait(act, x3T_ps, b)
                    act_do(x3h[:], P0[:, 0:T], ACT.Copy).then_inc(x3h_sb.sem, 1)
                elif k in (10, 11):
                    n = k - 10
                    wait(act, w12_ps, b, n + 1)
                    wait(act, a1_sb, b, n)
                    for j in range(2):
                        f = 2 * n + j
                        ins = act_do(fth[:, j * T:(j + 1) * T], P0[:, j * T:(j + 1) * T], ACT.Tanh,
                                     scale=s1half[:, f:f + 1])
                    ins.then_inc(fth_sb.sem, 1)
                    wait(act, a1_sb, b, n + 1)
                    act_do(a1h[:, 512 * n:512 * n + 512], a1[:, 512 * n:512 * n + 512], ACT.Copy).then_inc(a1h_sb.sem, 1)
                elif k in (12, 13):
                    n = k - 12
                    wait(act, h1_ps, b, n + 1)
                    bank_ = P1 if n else P0
                    for j in range(2):
                        f = 2 * n + j
                        ins = act_do(a2[:, f * T:(f + 1) * T], bank_[:, j * T:(j + 1) * T], ACT.Gelu,
                                     scale=sh1[:, f:f + 1])
                    ins.then_inc(a2_sb.sem, 1)
                    wait(act, a2_sb, b, n + 1)
                    act_do(a2h[:, 512 * n:512 * n + 512], a2[:, 512 * n:512 * n + 512], ACT.Copy).then_inc(a2h_sb.sem, 1)
                elif k in (14, 15):
                    n = k - 14
                    wait(act, h2_ps, b, n + 1)
                    bank_ = P1 if n else P0
                    for j in range(2):
                        f = 2 * n + j
                        ins = act_do(a3[:, f * T:(f + 1) * T], bank_[:, j * T:(j + 1) * T], ACT.Gelu,
                                     scale=sh2[:, f:f + 1])
                    ins.then_inc(a3_sb.sem, 1)

            interleave(attention, stage, 0, None, True)
            act.wait_ge(half_sb.sem, 4)
            interleave(attention, stage, 1, 0, True)
            with act.Fori(2, NB - 1) as i:
                interleave(attention, stage, i, i - 1, True)
            interleave(attention, stage, NB - 1, NB - 2, False)
            interleave(attention, stage, None, NB - 1, False)

        @block.vector
        def _(dve):
            v = nc.vector
            links = Order(nc, ctx, dve, "stage_order", 17)
            den_order = sig("den_order", H)

            vo_hi = sig("vo_hi")
            for n in range(4):
                w = slice(n * PIECE, (n + 1) * PIECE)
                dve.wait_ge(vo_ld[n].sem, 16)
                v.tensor_copy(VOh[:, w], stage_in[:, n, :]).then_inc(vo_hi.sem, 1)
            for n in range(4):
                w = slice(n * PIECE, (n + 1) * PIECE)
                dve.wait_ge(vo_hi.sem, n + 1)
                v.tensor_tensor(VOl[:, w], stage_in[:, n, :], VOh[:, w].bitcast(F32), ALU.subtract)\
                    .then_inc(vo_split.sem, 1)
            for n in range(4):
                w = slice(n * 512, (n + 1) * 512)
                dve.wait_ge(ah_sb.sem, n + 1)
                v.tensor_tensor(Al[:, w], S[n % 2][:], Ah[:, w].bitcast(F32), ALU.subtract).then_inc(al_sb.sem, 1)
            dve.wait_ge(xh_sb.sem, 1)
            v.tensor_tensor(xl[:], xT_in[:], xh[:].bitcast(F32), ALU.subtract).then_inc(xl_sb.sem, 1)
            v.memset(taken[:], 0.0).then_inc(half_sb.sem, 1)
            dve.sem_inc(rt_sb.sem, rt_sb.credit)
            dve.sem_inc(rh_sb.sem, rh_sb.credit)

            def y_low(a, p):
                wait(dve, yh_sb, a, p + 1)
                v.tensor_tensor(yl[:, p % 2, :], Y[:], yh[:, p % 2, :].bitcast(F32), ALU.subtract)\
                    .then_inc(yl_sb.sem, 1)

            def row_max(a, p, tc):
                wait(dve, g_ps, a, 2 * p + tc + 1)
                wait(dve, s_ps, a, 2 * p - 2)
                v.tensor_reduce(negm[:, p % 2, tc, :], G[:].rearrange("p (j u) -> p j u", j=2), AX.X, ALU.max,
                                negate=True).then_inc(negm_sb.sem, 1)

            def combine(a, h):
                wait(dve, av_ps, a, h + 1)
                o = O[h % 2][:].rearrange("p (c n) -> p c n", c=TC)
                v.reciprocal(rden[:, h % 2, :], o[:, :, D]).then_inc(den_order.sem, 1)
                wait(dve, den_order, a, h + 1)
                if h == 0:
                    wait(dve, x_ld, a, 16)
                for tc in range(TC):
                    ins = v.scalar_tensor_tensor(out=acc[:, tc, :], in0=o[:, tc, 0:D], scalar=rden[:, h % 2, tc:tc + 1],
                                                 in1=(x_res if h == 0 else acc)[:, tc, :], op0=ALU.mult, op1=ALU.add)
                ins.then_inc(comb.sem, 1)

            def attention(part, a, p, more):
                if part == "start":
                    y_low(a, 0)
                    row_max(a, 0, 0)
                    y_low(a, 1)
                    row_max(a, 0, 1)
                elif part == "scores":
                    if p + 1 < HP:
                        row_max(a, p + 1, 0)
                elif part == "values":
                    if p + 2 < HP:
                        y_low(a, p + 2)
                    if p + 1 < HP:
                        row_max(a, p + 1, 1)
                    if p == HP - 1 and more:
                        wait(dve, xh_sb, a + 1)
                        v.tensor_tensor(xl[:], xT_in[:], xh[:].bitcast(F32), ALU.subtract).then_inc(xl_sb.sem, 1)
                    if p >= 1:
                        combine(a, 2 * p - 2)
                        combine(a, 2 * p - 1)
                else:
                    combine(a, H - 2)
                    combine(a, H - 1)

            def layernorm(b, n, src, dst, done):
                for c in range(TC):
                    ins = v.bn_stats(stats[:, c, :], src[:, c, :])
                links.link(ins)
                v.memset(spacer[:], 0.0)
                for c in range(TC):
                    ins = v.bn_aggr(mv[:, n, c, :], stats[:, c, :])
                ins.then_inc(var_sb.sem, 1)
                wait(dve, rstd_sb, b, n + 1)
                for c in range(TC):
                    ins = v.tensor_scalar(dst[:, c, :], src[:, c, :], mv[:, n, c, 0:1], rstd[:, n, c:c + 1],
                                          ALU.subtract, ALU.mult)
                ins.then_inc(done.sem, 1)

            def experts(b):
                on = dve.value_load(flag[0:1, 0:1], min_val=0, max_val=1)
                with dve.If(on > 0):
                    def hidden(it, l):
                        q = it * 4 + l
                        banks = (P0, P1) if l % 2 == 0 else S
                        halves = [banks[c][:, 0:4 * FX].rearrange("p (e n) -> p e n", e=2) for c in range(TC)]
                        for c in range(TC):
                            wait(dve, rth_sb, b, q * 2 + c + 1)
                            wait(dve, rh_sb, b, q * 2 + c - 1)
                            v.scalar_tensor_tensor(out=rt[:, c, :, :], in0=rth[:, c, :, :], scalar=1.0,
                                                   in1=halves[c][:, :, 0:FX], op0=ALU.add, op1=ALU.mult)\
                                .then_inc(rt_sb.sem, 1)
                        wait(dve, rT_ps, b, q - 1)
                        for c in range(TC):
                            wait(dve, rt_sb, b, q * 2 + c + 1)
                            for e in range(2):
                                ins = v.scalar_tensor_tensor(out=rh[:, l % 2, c, e, :], in0=rt[:, c, e, :],
                                                             scalar=coef8[:, c, 2 * l + e:2 * l + e + 1],
                                                             in1=halves[c][:, e, FX:2 * FX], op0=ALU.mult,
                                                             op1=ALU.mult)
                            ins.then_inc(rh_sb.sem, 1)

                    with dve.Fori(0, E // 8) as it:
                        wait(dve, rh_sb, b, it * 8)
                        v.tensor_copy(coef8[:], coef[:, :, bass.ds(it * 8, 8)]).then_inc(c8_sb.sem, 1)
                        wait(dve, c8_sb, b, it + 1)
                        for l in range(4):
                            hidden(it, l)
                with dve.Else():
                    dve.sem_inc(rt_sb.sem, E)
                    dve.sem_inc(rh_sb.sem, E)
                    dve.sem_inc(c8_sb.sem, E // 8)

            def stage(b, k):
                if k == 0:
                    links.start(b)
                    wait(dve, comb, b, H)
                    layernorm(b, 0, acc, x1, x1_sb)
                elif k == 1:
                    wait_alone(dve, logits_ps, b, 1, const_sb)
                    l3 = P0[:, 0:TC * E].rearrange("p (c e) -> p c e", c=TC)
                    for c in range(TC):
                        ins = v.max(top8[:, c, :], l3[:, c, :])
                    links.link(ins)
                    v.tensor_scalar(negmax[:], top8[:, :, 0], -1.0, None, ALU.mult)
                    for c in range(TC):
                        ins = v.match_replace(rest[:, c, :], top8[:, c, :], l3[:, c, :], -3.0e38)
                    links.link(ins)
                    v.tensor_tensor(mask[:], l3, rest[:], ALU.not_equal).then_inc(mask_sb.sem, 1)
                    wait(dve, sth_sb, b)
                    links.link(v.scalar_tensor_tensor(out=st[:], in0=sth[:], scalar=1.0, in1=P1[0:FX, 0:T],
                                                      op0=ALU.add, op1=ALU.mult))
                    v.scalar_tensor_tensor(out=hs[:], in0=st[:], scalar=0.5, in1=P1[0:FX, T:2 * T],
                                           op0=ALU.mult, op1=ALU.mult).then_inc(hs_sb.sem, 1)
                    wait(dve, ew_sb, b)
                    links.link(v.tensor_tensor(wm[:], ew[:], mask[:], ALU.mult))
                    links.link(v.tensor_reduce(wsum[:], wm[:], AX.X, ALU.add))
                    links.link(v.reciprocal(wrec[:], wsum[:]))
                elif k == 2:
                    wait(dve, cum_ps, b)
                    tot = P0[:, 2 * E:3 * E]
                    v.scalar_tensor_tensor(out=live[:], in0=taken[:], scalar=CAPACITY, in1=tot, op0=ALU.is_lt,
                                           op1=ALU.mult)
                    for c in range(TC):
                        ins = v.tensor_tensor(pos[:, c, :], P0[:, c * E:(c + 1) * E], taken[:], ALU.add)
                    links.link(ins)
                    v.tensor_tensor(taken[:], tot, taken[:], ALU.add)
                    v.tensor_reduce(livemax[:], live[:], AX.X, ALU.max)
                    links.link(v.scalar_tensor_tensor(out=pos[:], in0=pos[:], scalar=CAPACITY, in1=wm[:],
                                                      op0=ALU.is_lt, op1=ALU.mult))
                    wait(dve, rw_ld[1], b, 0)
                    v.tensor_scalar(flag[:], livemax[:], 1.0, None, ALU.min)
                    for c in range(TC):
                        ins = v.tensor_scalar(coef[:, c, :], pos[:, c, :], wrec[:, c:c + 1], 0.5, ALU.mult, ALU.mult)
                    ins.then_inc(coef_sb.sem, 1)
                    wait_alone(dve, coef_sb, b, 1, const_sb)
                    experts(b)
                    wait(dve, sd_ps, b)
                    wait(dve, rd_ps, b, PAIRS)
                    ins = v.tensor_tensor(res[:], O[1][:, 0:T].rearrange("p (c d) -> p c d", c=TC), x1[:], ALU.add)
                    ins.then_inc(moe_read.sem, 1)
                    wait(dve, moe_read, b)
                    layernorm(b, 1, res, x2, x2_sb)
                elif k == 3:
                    wait(dve, x2h_sb, b)
                    v.tensor_tensor(x2l[:], P1[:, 0:T], x2h[:].bitcast(F32), ALU.subtract).then_inc(x2l_sb.sem, 1)
                elif k == 4:
                    wait(dve, kv_ps, b)
                    kk = P0[:].rearrange("p (c n) -> p c n", c=TC)[:, :, 0:D]
                    v.tensor_scalar(kmax[:], kk, 0.0, None, ALU.max)
                    v.tensor_scalar(kmin[:], kk, 0.0, None, ALU.min).then_inc(kvm_sb.sem, 1)
                    wait(dve, q_ps, b)
                    v.tensor_scalar(qmax[:], P1[:, 0:T], 0.0, None, ALU.max)
                    v.tensor_scalar(qmin[:], P1[:, 0:T], 0.0, None, ALU.min).then_inc(qm_sb.sem, 1)
                    wait(dve, kve_sb, b)
                    wait(dve, qm_sb, b)
                    v.tensor_tensor(kf[:], kmax[:], ke[:], ALU.add).then_inc(kf_sb.sem, 1)
                    wait(dve, qe_sb, b)
                    v.tensor_tensor(qf[:], qmax[:], qe[:], ALU.add).then_inc(qf_sb.sem, 1)
                elif k == 5:
                    wait(dve, kvp_ps, b)
                    v.tensor_tensor(kvz[:, 0:D], P0[:, 0:D], headmask[:], ALU.mult)
                    v.tensor_scalar(kvz[:, D:2 * D], headmask[:], P0[:, D:D + 1], None, ALU.mult)\
                        .then_inc(kvz_sb.sem, 1)
                elif k == 6:
                    wait(dve, nd_ps, b)
                    nd = P1[:].rearrange("p (c n) -> p c n", c=TC)
                    links.link(v.tensor_scalar(den[:], nd[:, :, D:2 * D], Z_EPS, None, ALU.add))
                    links.link(v.reciprocal(dinv[:], den[:]))
                    v.tensor_tensor(o1[:], nd[:, :, 0:D], dinv[:], ALU.mult).then_inc(o1_sb.sem, 1)
                elif k == 8:
                    wait(dve, wo_ps, b)
                    wait(dve, x2b_sb, b)
                    ins = v.tensor_tensor(res[:], P1[:, 0:T].rearrange("p (c d) -> p c d", c=TC), x2b[:], ALU.add)
                    ins.then_inc(wo_read.sem, 1)
                    wait(dve, wo_read, b)
                    layernorm(b, 2, res, x3, x3_sb)
                elif k == 9:
                    wait(dve, x3h_sb, b)
                    v.tensor_tensor(x3l[:], P0[:, 0:T], x3h[:].bitcast(F32), ALU.subtract).then_inc(x3l_sb.sem, 1)
                elif k in (10, 11):
                    n = k - 10
                    wait(dve, fth_sb, b, n + 1)
                    links.link(v.scalar_tensor_tensor(out=ft[:], in0=fth[:], scalar=1.0, in1=P0[:], op0=ALU.add,
                                                      op1=ALU.mult))
                    for j in range(2):
                        f = 2 * n + j
                        ins = v.scalar_tensor_tensor(out=a1[:, f * T:(f + 1) * T], in0=P1[:, j * T:(j + 1) * T],
                                                     scalar=s12half[:, f:f + 1], in1=ft[:, j * T:(j + 1) * T],
                                                     op0=ALU.mult, op1=ALU.mult)
                    ins.then_inc(a1_sb.sem, 1)
                elif k == 16:
                    wait(dve, w3_ps, b)
                    for c in range(TC):
                        ins = v.tensor_tensor(res[:, c, :], P0[:, c * D:(c + 1) * D], s3[:], ALU.mult)
                    ins.then_inc(w3_read.sem, 1)
                    wait(dve, w3_read, b)
                    links.link(v.tensor_tensor(res[:], res[:], x3[:], ALU.add))
                    wait(dve, out_st, b, 0)
                    layernorm(b, 3, res, yout, yout_sb)
                    links.end()

            interleave(attention, stage, 0, None, True)
            dve.wait_ge(const_sb.sem, 5)
            dve.wait_ge(small_ld.sem, 16 * (len(SMALL) + len(ROWS)))
            v.tensor_scalar(s1half[:], s1[:], 0.5, None, ALU.mult).then_inc(half_sb.sem, 1)
            v.tensor_tensor(s12half[:], s1[:], s2[:], ALU.mult).then_inc(half_sb.sem, 1)
            dve.wait_ge(half_sb.sem, 3)
            v.tensor_scalar(s12half[:], s12half[:], 0.5, None, ALU.mult).then_inc(half_sb.sem, 1)
            dve.wait_ge(half_sb.sem, 4)
            interleave(attention, stage, 1, 0, True)
            with dve.Fori(2, NB - 1) as i:
                interleave(attention, stage, i, i - 1, True)
            interleave(attention, stage, NB - 1, NB - 2, False)
            interleave(attention, stage, None, NB - 1, False)


def kernel(**inputs):
    import concourse.bacc as bacc
    from concourse.bass_utils import run_bass_kernel_spmd

    g = {k: np.asarray(v) for k, v in inputs.items()}
    x = g["L0_attn_x"]
    nb, t, d = x.shape
    heads, rank, _ = g["L0_attn_Q"].shape
    experts, _, fx = g["L0_ffn_w_gate"].shape
    kb = g["L1_ffn_h1_w"].shape[0] // 128

    def blocks(w):
        wt = w.T
        return wt.reshape(-1, 128, wt.shape[1]).transpose(1, 0, 2)

    def by_feature(s):
        return s.reshape(-1, 128).T

    wqkv = g["L1_attn_Wqkv"]
    gate_up = np.concatenate([g["L0_ffn_w_gate"], g["L0_ffn_w_up"]], axis=2)
    arrays = {
        "x": x,
        "xT": x.transpose(0, 2, 1),
        "q": g["L0_attn_Q"].transpose(1, 0, 2).reshape(rank, heads * d),
        "k": g["L0_attn_K"].transpose(1, 0, 2).reshape(rank, heads * d),
        "vo": g["L0_attn_VO"].transpose(1, 0, 2).reshape(d, heads * d),
        "rw": g["L0_ffn_router_w"].T,
        "wgu": gate_up.reshape(experts // 4, 4, d, 2 * fx).transpose(0, 2, 1, 3).reshape(experts // 4, d, 8 * fx),
        "wd": g["L0_ffn_w_down"].reshape(experts // 4, 4, fx, d).transpose(0, 2, 1, 3)
        .reshape(experts // 4, fx, 4 * d),
        "wsgu": g["L0_ffn_ws_gate_up"],
        "wsd": g["L0_ffn_ws_down"],
        "wq": wqkv[0:d].T,
        "wkv": wqkv[d:3 * d].T,
        "wout": g["L1_attn_Wout"].T,
        "bout": g["L1_attn_bout"],
        "w1": g["L1_ffn_w1_w"].T,
        "w2": g["L1_ffn_w2_w"].T,
        "h1": blocks(g["L1_ffn_h1_w"]).reshape(128, -1),
        "h2": blocks(g["L1_ffn_h2_w"]).reshape(128, -1),
        "w3": blocks(g["L1_ffn_w3_w"]),
        "s1": by_feature(g["L1_ffn_w1_s"]),
        "s2": by_feature(g["L1_ffn_w2_s"]),
        "sh1": by_feature(g["L1_ffn_h1_s"]),
        "sh2": by_feature(g["L1_ffn_h2_s"]),
        "s3": g["L1_ffn_w3_s"],
    }
    nc = bacc.Bacc("TRN2", target_bir_lowering=False, num_devices=1)
    arrays = {k: np.ascontiguousarray(v) for k, v in arrays.items()}
    aps = {k: nc.dram_tensor("in_" + k, a.shape, mybir.dt.from_np(a.dtype), kind="ExternalInput").ap()
           for k, a in arrays.items()}
    aps["out"] = nc.dram_tensor("out", x.shape, F32, kind="ExternalOutput").ap()
    build(nc, aps)
    r = run_bass_kernel_spmd(nc, [{"in_" + k: a for k, a in arrays.items()}], core_ids=[0])
    return r.results[0]["out"]
```

```python
from contextlib import ExitStack

import numpy as np

import concourse.bass as bass
from concourse import mybir

F32 = mybir.dt.float32
F32R = mybir.dt.float32r
BF16 = mybir.dt.bfloat16
I32 = mybir.dt.int32
ALU = mybir.AluOpType
ACT = mybir.ActivationFunctionType
AX = mybir.AxisListType

P = 128
SCALE = 1.0 / float(np.sqrt(128.0))
LN_EPS = 1e-5
Z_EPS = 1e-6
CAPACITY = 64.0
HEAD_DIM1 = 8
POSITIONS = 18
PIECE = 512


class Signal:

    def __init__(self, nc, ctx, name, per=1, credit=0):
        self.sem = ctx.enter_context(nc.semaphore(name))
        self.per = per
        self.credit = credit

    def value(self, b, k=1):
        return b * self.per + (k + self.credit)


def wait(engine, signal, b, k=1):
    v = signal.value(b, k)
    if isinstance(v, int) and v <= 0:
        return
    engine.wait_ge(signal.sem, v)


def wait_alone(engine, signal, b, k, constants):
    engine.wait_ge(constants.sem, 5)
    wait(engine, signal, b, k)


class Order:

    def __init__(self, nc, ctx, engine, name, per):
        self.done = Signal(nc, ctx, name, per)
        self.engine = engine
        self.n = 0

    def start(self, b):
        self.b, self.n = b, 0

    def link(self, instruction):
        self.n += 1
        instruction.then_inc(self.done.sem, 1)
        wait(self.engine, self.done, self.b, self.n)

    def end(self):
        assert self.n == self.done.per, (self.n, self.done.per)


def interleave(attention, mid, ffn, a, b, c, more):
    for pos in range(POSITIONS):
        part = "start" if pos == 0 else "end" if pos == 17 else ("values", "scores")[pos % 2]

        def between():
            if b is not None:
                mid(b, pos)
            if c is not None:
                ffn(c, pos)

        if a is None:
            between()
        else:
            attention(part, a, (pos - 1) // 2, more, between)


def fill(attention, set_up=None):
    interleave(attention, set_up, None, 0, None if set_up is None else 0, None, True)


def pipeline(engine, attention, mid, ffn, n):
    interleave(attention, mid, ffn, 1, 0, None, True)
    interleave(attention, mid, ffn, 2, 1, 0, True)
    with engine.Fori(3, n - 1) as i:
        interleave(attention, mid, ffn, i, i - 1, i - 2, True)
    interleave(attention, mid, ffn, n - 1, n - 2, n - 3, False)
    interleave(attention, mid, ffn, None, n - 1, n - 2, False)
    interleave(attention, mid, ffn, None, None, n - 1, False)


def build(nc, A):
    NB, T, D = A["x"].shape
    H = A["vo"].shape[1] // D
    E = A["wgu"].shape[0] * 4
    FX = A["wd"].shape[1]
    R = A["q"].shape[0]
    DH = A["w1"].shape[1]
    KB = DH // P
    HP = H // 2
    TC = T // P
    assert (T, D, H, E, FX, TC, HP, KB) == (256, 128, 16, 64, 96, 2, 8, 4)
    GROUPS = E // 4
    PAIRS = E // 2

    with ExitStack() as ctx:
        def sb(name, shape, dt=F32):
            return ctx.enter_context(nc.sbuf_tensor(name, shape, dt))

        def bank(name):
            return ctx.enter_context(nc.psum_tensor(name, [P, 512], F32))

        def sig(name, per=1, credit=0):
            return Signal(nc, ctx, name, per, credit)

        xT_in = sb("xT_in", [P, T])
        x_res = sb("x_res", [P, TC, D])
        xh, xl = sb("xh", [P, T], F32R), sb("xl", [P, T], F32R)
        Ah, Al = sb("Ah", [P, H * D], F32R), sb("Al", [P, H * D], F32R)
        VOh, VOl = sb("VOh", [P, H * D], F32R), sb("VOl", [P, H * D], F32R)
        yh, yl = sb("yh", [P, 2, 512], F32R), sb("yl", [P, 2, 512], F32R)
        V = sb("V", [P, TC, H, D + 1])
        Ex = sb("Ex", [P, 2, TC, 512])
        negm = sb("negm", [P, 2, TC, 2], BF16)
        rden = sb("rden", [P, 2, TC])
        acc = sb("acc", [P, TC, D])
        stage_in = sb("stage_in", [P, 4, PIECE])
        w_split = {}
        for name, cols in (("w1", DH), ("w2", DH), ("h1", KB * DH), ("h2", KB * DH),
                           ("wsgu", 2 * FX), ("wq", D), ("wkv", 2 * D)):
            w_split[name] = (sb(name + "h", [P, cols], F32R), sb(name + "l", [P, cols], F32R))
        w3 = sb("w3", [P, KB, D])
        wsd = sb("wsd", [FX, D])
        wout = sb("wout", [P, D])
        rw = sb("rw", [P, E])
        s1 = sb("s1", [P, KB])
        s2 = sb("s2", [P, KB])
        sh1 = sb("sh1", [P, KB])
        sh2 = sb("sh2", [P, KB])
        s1half = sb("s1half", [P, KB])
        s12half = sb("s12half", [P, KB])
        s3 = sb("s3", [P, D])
        bout = sb("bout", [P, D])
        ident = sb("ident", [P, P])
        ident_bf = sb("ident_bf", [P, P], BF16)
        ones_bf = sb("ones_bf", [P, P], BF16)
        before = sb("before", [P, P], BF16)
        headmask = sb("headmask", [P, P])
        ones = sb("ones", [P, P])
        minus_half = sb("minus_half", [P, TC])
        ln_eps = sb("ln_eps", [P, TC])
        spacer = sb("spacer", [P, 4])
        FF = sb("FF", [P, 3, KB * T])
        a1, a2, a3 = FF[:, 0, :], FF[:, 1, :], FF[:, 2, :]
        a1h, a1l = sb("a1h", [P, KB * T], F32R)[:], sb("a1l", [P, KB * T], F32R)[:]
        a2h, a2l = sb("a2h", [P, KB * T], F32R)[:], sb("a2l", [P, KB * T], F32R)[:]
        fth = sb("fth", [P, T])
        ft = sb("ft", [P, T])
        stats = sb("stats", [P, 4, TC, 6])
        mv = sb("mv", [P, 4, TC, 2])
        veps = sb("veps", [P, 4, TC])
        rstd = sb("rstd", [P, 4, TC])
        x1, x2, x3 = sb("x1", [P, TC, D]), sb("x2", [P, TC, D]), sb("x3", [P, TC, D])
        x2b = sb("x2b", [P, TC, D])
        res, res_ffn = sb("res", [P, TC, D]), sb("res_ffn", [P, TC, D])
        yout = sb("yout", [P, TC, D])
        x1T, x2T, x3T = sb("x1T", [P, T]), sb("x2T", [P, T]), sb("x3T", [P, T])
        x1h, x1l = sb("x1h", [P, T], F32R), sb("x1l", [P, T], F32R)
        x2h, x2l = sb("x2h", [P, T], F32R), sb("x2l", [P, T], F32R)
        x3h, x3l = sb("x3h", [P, T], F32R), sb("x3l", [P, T], F32R)
        top8 = sb("top8", [P, TC, 8])
        rest = sb("rest", [P, TC, E])
        mask = sb("mask", [P, TC, E], BF16)
        negmax = sb("negmax", [P, TC])
        ew = sb("ew", [P, TC, E])
        wm = sb("wm", [P, TC, E])
        wsum = sb("wsum", [P, TC])
        wrec = sb("wrec", [P, TC])
        place = sb("place", [P, TC, E])
        coef = sb("coef", [P, TC, E])
        taken = sb("taken", [P, E])
        live = sb("live", [P, E])
        livemax = sb("livemax", [P, 1])
        flag = sb("flag", [P, 1], I32)
        sth = sb("sth", [FX, T])
        st = sb("st", [FX, T])
        hs = sb("hs", [FX, T])
        kparts = sb("kparts", [P, 4, TC, D])
        kmin, kmax, ke, kf = (kparts[:, i, :, :] for i in range(4))
        qmin, qmax, qe, qf = (sb(n, [P, T]) for n in ("qmin", "qmax", "qe", "qf"))
        vt = sb("vt", [P, TC, D + 1])
        G1 = D // HEAD_DIM1
        kvz = sb("kvz", [P, D + G1])
        den = sb("den", [P, TC, G1])
        dinv = sb("dinv", [P, TC, G1])
        o1 = sb("o1", [P, TC, D])
        oT = sb("oT", [P, T])
        wgu_in = sb("wgu_in", [P, 2, 4 * 2 * FX])
        wd_in = sb("wd_in", [FX, 2, 4 * D])
        PAIR = TC * 2 * FX
        rth = a1[:, 0:PAIR].rearrange("p (c e n) -> p c e n", c=TC, e=2)
        rt = a1[:, PAIR:2 * PAIR].rearrange("p (c e n) -> p c e n", c=TC, e=2)
        rh = a3[:, 0:2 * PAIR].rearrange("p (s c e n) -> p s c e n", s=2, c=TC, e=2)
        rhT = kparts[0:FX, :, :, :].rearrange("p (s a) c d -> p s (a c d)", s=2)
        coef8 = sb("coef8", [P, TC, 8])

        Y, G = bank("Y"), bank("G")
        S = [bank("S0"), bank("S1")]
        O = [bank("O0"), bank("O1")]
        M = bank("M")
        F = bank("F")

        x_ld, xT_ld = sig("x_ld", 16), sig("xT_ld", 16)
        xh_sb, xl_sb = sig("xh_sb"), sig("xl_sb")
        y_ps, yh_sb, yl_sb = sig("y_ps", HP), sig("yh_sb", HP), sig("yl_sb", HP)
        g_ps, negm_sb = sig("g_ps", 2 * HP), sig("negm_sb", 2 * HP)
        s_ps, ex_sb = sig("s_ps", 2 * HP), sig("ex_sb", 2 * HP)
        v_ps, v_sb = sig("v_ps", 8), sig("v_sb", 8)
        av_ps, comb = sig("av_ps", H), sig("comb", H)
        stats_sb, var_sb, veps_sb, rstd_sb = (
            [sig(f"{name}{n}") for n in range(4)] for name in ("stats_sb", "var_sb", "veps_sb", "rstd_sb"))
        x1_sb, x1T_ps, x1T_sb, x1h_sb, x1l_sb = (sig(n) for n in ("x1_sb", "x1T_ps", "x1T_sb", "x1h_sb", "x1l_sb"))
        logits_ps, mask_sb, ew_sb = sig("logits_ps"), sig("mask_sb"), sig("ew_sb")
        sgu_ps, sth_sb, hs_sb, sd_ps = sig("sgu_ps"), sig("sth_sb"), sig("hs_sb"), sig("sd_ps")
        cum_ps, coef_sb = sig("cum_ps"), sig("coef_sb")
        x2_sb, x2T_ps, x2h_sb, x2l_sb, x2b_sb = (sig(n) for n in ("x2_sb", "x2T_ps", "x2h_sb", "x2l_sb", "x2b_sb"))
        moe_read = sig("moe_read")
        kv_ps, q_ps, kvm_sb, qm_sb, kve_sb, qe_sb, kf_sb, qf_sb = (
            sig(n) for n in ("kv_ps", "q_ps", "kvm_sb", "qm_sb", "kve_sb", "qe_sb", "kf_sb", "qf_sb"))
        kvp_ps, kvz_sb, nd_ps, o1_sb, oT_ps, oT_sb, wo_ps = (
            sig(n) for n in ("kvp_ps", "kvz_sb", "nd_ps", "o1_sb", "oT_ps", "oT_sb", "wo_ps"))
        wo_read = sig("wo_read")
        x3_sb, x3T_ps, x3h_sb, x3l_sb = (sig(n) for n in ("x3_sb", "x3T_ps", "x3h_sb", "x3l_sb"))
        w12_ps, fth_sb, a1_sb, a1h_sb, a1l_sb = (sig(n, KB) for n in ("w12_ps", "fth_sb", "a1_sb", "a1h_sb", "a1l_sb"))
        h1_ps, a2_sb, a2h_sb, a2l_sb = (sig(n, 2) for n in ("h1_ps", "a2_sb", "a2h_sb", "a2l_sb"))
        h2_ps, a3_sb = sig("h2_ps", 2), sig("a3_sb", 2)
        w3_ps, w3_read, yout_sb, out_st = sig("w3_ps"), sig("w3_read"), sig("yout_sb"), sig("out_st", 16)
        rw_ld = [sig(f"rw_ld{i}", 16 * GROUPS) for i in range(2)]
        rgu_ps, rth_sb, rt_sb = sig("rgu_ps", E), sig("rth_sb", E), sig("rt_sb", E, 2)
        rh_sb = sig("rh_sb", E, 4)
        rT_ps, rhT_sb = sig("rT_ps", PAIRS, 2), sig("rhT_sb", PAIRS, 2)
        rd_ps = sig("rd_ps", PAIRS, 4)
        c8_sb = sig("c8_sb", 8)
        wm_sb, res_ffn_sb = sig("wm_sb"), sig("res_ffn_sb")
        const_sb, half_sb, ones_sb = sig("const_sb"), sig("half_sb"), sig("ones_sb")
        small_ld, qk_ld = sig("small_ld"), sig("qk_ld")
        vo_ld = [sig(f"vo_ld{i}") for i in range(4)]
        split_ld = [sig(f"split_ld{i}") for i in range(4)]
        vo_split = sig("vo_split")
        a_ps, ah_sb, al_sb = sig("a_ps"), sig("ah_sb"), sig("al_sb")
        split_hi, split_lo = sig("split_hi"), sig("split_lo")

        q_in = Ex[0:R, :, :, :].rearrange("p a b c -> p (a b c)")
        k_in = FF[0:R, 0:2, :].rearrange("p a b -> p (a b)")
        SMALL = [("w3", w3[:]), ("wsd", wsd[:]), ("wout", wout[:]), ("rw", rw[:]), ("s1", s1[:]), ("s2", s2[:]),
                 ("sh1", sh1[:]), ("sh2", sh2[:])]
        ROWS = [("s3", s3), ("bout", bout)]
        PIECES = [(name, c, min(PIECE, w_split[name][0].shape[1] - c))
                  for name in ("wsgu", "wkv", "wq", "w1", "w2", "h1", "h2")
                  for c in range(0, w_split[name][0].shape[1], PIECE)]

        FFN_WEIGHTS = ("w1", "w2", "h1", "h2")
        FIRST_FFN = [name for name, _, _ in PIECES].index("w1")
        FFN_PIECES = len(PIECES) - FIRST_FFN
        inexact = FF[:].rearrange("p a b -> p (a b)")[:, 0:FFN_PIECES * PIECE // 2].bitcast(BF16)
        inexact_sum, low_flag = sb("inexact_sum", [P, 1]), sb("low_flag", [P, 1], I32)
        inexact_sb, low_ps, low_sb, inexact_sum_sb = (sig(n) for n in ("inexact_sb", "low_ps", "low_sb", "inexact_sum_sb"))

        block = ctx.enter_context(nc.Block())

        @block.sync
        def _(sp):
            sp.dma_start(q_in, A["q"]).then_inc(qk_ld.sem, 16)
            sp.dma_start(k_in, A["k"]).then_inc(qk_ld.sem, 16)
            sp.dma_start(xT_in[:], A["xT"][0]).then_inc(xT_ld.sem, 16)
            sp.dma_start(x_res[:], A["x"][0].rearrange("(c p) d -> p c d", p=P)).then_inc(x_ld.sem, 16)
            for i in range(4):
                sp.dma_start(stage_in[:, i, :], A["vo"][:, i * PIECE:(i + 1) * PIECE]).then_inc(vo_ld[i].sem, 16)
            for name, tile in SMALL:
                sp.dma_start(tile, A[name]).then_inc(small_ld.sem, 16)
            for name, tile in ROWS:
                sp.dma_start(tile[:], A[name].partition_broadcast(P)).then_inc(small_ld.sem, 16)
            for n, (name, c, w) in enumerate(PIECES):
                if n < 4:
                    sp.wait_ge(vo_split.sem, n + 1)
                else:
                    sp.wait_ge(split_lo.sem, n - 3)
                sp.dma_start(stage_in[:, n % 4, 0:w], A[name][:, c:c + w]).then_inc(split_ld[n % 4].sem, 16)

            def experts_in(b):
                wait_alone(sp, coef_sb, b, 1, const_sb)
                on = sp.value_load(flag[0:1, 0:1], min_val=0, max_val=1)
                with sp.If(on > 0):
                    with sp.Fori(0, GROUPS // 2) as it:
                        for half in range(2):
                            wait(sp, rd_ps, b, it * 4 + 2 * half - 2)
                            g = it * 2 + half
                            sp.dma_start(wgu_in[:, half, :], A["wgu"][bass.ds(g, 1)].rearrange("a p n -> (a p) n"))\
                                .then_inc(rw_ld[half].sem, 16)
                            sp.dma_start(wd_in[:, half, :], A["wd"][bass.ds(g, 1)].rearrange("a p n -> (a p) n"))\
                                .then_inc(rw_ld[half].sem, 16)
                with sp.Else():
                    for slot in rw_ld:
                        sp.sem_inc(slot.sem, slot.per)

            def rows(ap, b):
                if isinstance(b, int):
                    return ap[b]
                return ap[bass.ds(b, 1)].rearrange("a p d -> (a p) d")

            def step(a, b, c, more):
                if a is not None and more:
                    wait(sp, xl_sb, a)
                    sp.dma_start(xT_in[:], rows(A["xT"], a + 1)).then_inc(xT_ld.sem, 16)
                if b is not None:
                    experts_in(b)
                if a is not None and more:
                    wait(sp, comb, a, 1)
                    sp.dma_start(x_res[:], rows(A["x"], a + 1).rearrange("(c p) d -> p c d", p=P)).then_inc(x_ld.sem, 16)
                if c is not None:
                    wait(sp, yout_sb, c)
                    sp.dma_start(rows(A["out"], c).rearrange("(c p) d -> p c d", p=P), yout[:]).then_inc(out_st.sem, 16)

            step(0, None, None, True)
            step(1, 0, None, True)
            step(2, 1, 0, True)
            with sp.Fori(3, NB - 1) as i:
                step(i, i - 1, i - 2, True)
            step(NB - 1, NB - 2, NB - 3, False)
            step(None, NB - 1, NB - 2, False)
            step(None, None, NB - 1, False)
            wait(sp, out_st, NB - 1, 16)

        @block.gpsimd
        def _(pool):
            nc.gpsimd.memset(ones[:], 1.0).then_inc(ones_sb.sem, 1)
            nc.gpsimd.memset(ones_bf[:], 1.0).then_inc(ones_sb.sem, 1)
            nc.gpsimd.memset(minus_half[:], -0.5).then_inc(ones_sb.sem, 1)
            nc.gpsimd.memset(ln_eps[:], LN_EPS).then_inc(ones_sb.sem, 1)
            nc.gpsimd.memset(V[:, :, :, D:D + 1], 1.0).then_inc(ones_sb.sem, 1)
            nc.gpsimd.memset(vt[:, :, D:D + 1], 1.0).then_inc(ones_sb.sem, 1)
            pool.wait_ge(ones_sb.sem, 6)
            for tile, src in ((ident, ones), (ident_bf, ones_bf)):
                nc.gpsimd.affine_select(out=tile[:], in_=src[:], compare_op=ALU.is_equal, fill=0.0, base=0,
                                        pattern=[[-1, P]], channel_multiplier=1).then_inc(const_sb.sem, 1)
            nc.gpsimd.affine_select(out=before[:], in_=ones_bf[:], compare_op=ALU.is_gt, fill=0.0, base=0,
                                    pattern=[[1, P]], channel_multiplier=-1).then_inc(const_sb.sem, 1)
            grid = headmask[:].rearrange("p (g e) -> p g e", e=HEAD_DIM1)
            steps = [[-HEAD_DIM1, P // HEAD_DIM1], [0, HEAD_DIM1]]
            nc.gpsimd.affine_select(out=grid, in_=ones[:].rearrange("p (g e) -> p g e", e=HEAD_DIM1),
                                    compare_op=ALU.is_ge, fill=0.0, base=0, pattern=steps,
                                    channel_multiplier=1).then_inc(const_sb.sem, 1)
            pool.wait_ge(const_sb.sem, 4)
            nc.gpsimd.affine_select(out=grid, in_=grid, compare_op=ALU.is_ge, fill=0.0, base=HEAD_DIM1 - 1,
                                    pattern=[[HEAD_DIM1, P // HEAD_DIM1], [0, HEAD_DIM1]],
                                    channel_multiplier=-1).then_inc(const_sb.sem, 1)
            for n, (name, c, w) in enumerate(PIECES):
                hi, lo = w_split[name]
                pool.wait_ge(split_hi.sem, n + 1)
                nc.gpsimd.tensor_tensor(lo[:, c:c + w], stage_in[:, n % 4, 0:w], hi[:, c:c + w].bitcast(F32),
                                        ALU.subtract).then_inc(split_lo.sem, 1)

            def inverse_std(b, n):
                wait(pool, var_sb[n], b)
                nc.gpsimd.tensor_tensor(veps[:, n, :], mv[:, n, :, 1], ln_eps[:], ALU.add).then_inc(veps_sb[n].sem, 1)
                wait(pool, veps_sb[n], b)
                nc.gpsimd.tensor_tensor(rstd[:, n, :], veps[:, n, :], minus_half[:], ALU.pow)\
                    .then_inc(rstd_sb[n].sem, 1)

            def low(out, full, hi, done):
                nc.gpsimd.tensor_tensor(out, full, hi.bitcast(F32), ALU.subtract).then_inc(done.sem, 1)

            def mid(b, pos):
                if pos == 0:
                    inverse_std(b, 0)
                elif pos == 3:
                    wait(pool, ew_sb, b)
                    wait(pool, mask_sb, b)
                    nc.gpsimd.tensor_tensor(wm[:], ew[:], mask[:], ALU.mult).then_inc(wm_sb.sem, 1)
                elif pos == 2:
                    wait(pool, x1h_sb, b)
                    low(x1l[:], x1T[:], x1h[:], x1l_sb)
                elif pos == 8:
                    inverse_std(b, 1)
                elif pos == 10:
                    wait(pool, x2h_sb, b)
                    low(x2l[:], x2T[:], x2h[:], x2l_sb)
                    for c in range(TC):
                        ins = nc.gpsimd.tensor_tensor(x2b[:, c, :], x2[:, c, :], bout[:], ALU.add)
                    ins.then_inc(x2b_sb.sem, 1)
                elif pos == 11:
                    wait(pool, kve_sb, b)
                    nc.gpsimd.tensor_tensor(kf, kmax, ke, ALU.add).then_inc(kf_sb.sem, 1)
                elif pos == 12:
                    wait(pool, qe_sb, b)
                    nc.gpsimd.tensor_tensor(qf[:], qmax[:], qe[:], ALU.add).then_inc(qf_sb.sem, 1)
                elif pos == 17:
                    inverse_std(b, 2)

            def ffn(c, pos):
                if pos == 1:
                    wait(pool, x3h_sb, c)
                    low(x3l[:], x3T[:], x3h[:], x3l_sb)
                elif 2 <= pos < 2 + KB:
                    t = slice((pos - 2) * T, (pos - 1) * T)
                    wait(pool, a1h_sb, c, pos - 1)
                    low(a1l[:, t], a1[:, t], a1h[:, t], a1l_sb)
                elif pos in (6, 7):
                    t = slice((pos - 6) * 512, (pos - 5) * 512)
                    wait(pool, a2h_sb, c, pos - 5)
                    low(a2l[:, t], a2[:, t], a2h[:, t], a2l_sb)
                elif pos == 13:
                    wait(pool, w3_read, c)
                    nc.gpsimd.tensor_tensor(res_ffn[:], res_ffn[:], x3[:], ALU.add).then_inc(res_ffn_sb.sem, 1)
                elif pos == 14:
                    inverse_std(c, 3)

            def attention(part, a, p, more, between):
                between()

            pool.wait_ge(small_ld.sem, 16 * (len(SMALL) + len(ROWS)))
            fill(attention)
            pipeline(pool, attention, mid, ffn, NB)

        @block.tensor
        def _(pe):
            mm = nc.tensor.matmul

            def three(out, wh, wl, mh, ml):
                mm(out, wh, mh, start=True, stop=False)
                mm(out, wh, ml, start=False, stop=False)
                return mm(out, wl, mh, start=False, stop=True)

            pe.sem_inc(rT_ps.sem, rT_ps.credit)
            pe.sem_inc(rd_ps.sem, rd_ps.credit)
            pe.wait_ge(qk_ld.sem, 32)
            for n in range(4):
                if n >= 2:
                    pe.wait_ge(al_sb.sem, n - 1)
                for j in range(4):
                    h = 4 * n + j
                    ins = mm(S[n % 2][:, j * D:(j + 1) * D], q_in[:, h * D:(h + 1) * D], k_in[:, h * D:(h + 1) * D],
                             start=True, stop=True)
                ins.then_inc(a_ps.sem, 1)

            def y(a, p):
                wait(pe, yl_sb, a, p)
                for j in range(2):
                    w = slice((2 * p + j) * D, (2 * p + j + 1) * D)
                    ins = three(Y[:, j * T:(j + 1) * T], Ah[:, w], Al[:, w], xh[:], xl[:])
                ins.then_inc(y_ps.sem, 1)

            def guard(a, p, tc):
                wait(pe, yh_sb, a, p + 1)
                wait(pe, negm_sb, a, 2 * p + tc)
                for j in range(2):
                    c = j * T + tc * P
                    ins = mm(G[:, j * T:(j + 1) * T], yh[:, p % 2, c:c + P], xh[:], start=True, stop=True)
                ins.then_inc(g_ps.sem, 1)

            def scores(a, p, uc):
                wait(pe, yl_sb, a, p + 1)
                if p == 0:
                    wait(pe, v_sb, a, 5 + uc)
                else:
                    wait(pe, ex_sb, a, 2 * p + uc - 1)
                if p == 0 and uc == 0 and isinstance(a, int) and a == 0:
                    pe.wait_ge(al_sb.sem, 4)
                u = slice(uc * P, (uc + 1) * P)
                mm(S[uc][:], xh[:, u], yh[:, p % 2, :], start=True, stop=False)
                mm(S[uc][:], xh[:, u], yl[:, p % 2, :], start=False, stop=False)
                mm(S[uc][:], xl[:, u], yh[:, p % 2, :], start=False, stop=False)

            def minus_max(a, p, uc):
                if uc == 0:
                    wait(pe, negm_sb, a, 2 * p + 2)
                for j in range(2):
                    for tc in range(TC):
                        c = j * T + tc * P
                        ins = mm(S[uc][:, c:c + P], negm[:, p % 2, tc, j:j + 1].to_broadcast([P, P]), ident_bf[:],
                                 start=False, stop=(j == 1 and tc == TC - 1))
                ins.then_inc(s_ps.sem, 1)

            def v_piece(a, n):
                uc, nb = n // 4, n % 4
                if n < 2:
                    wait(pe, ex_sb, a, 0)
                elif n < 4:
                    wait(pe, comb, a, 0)
                else:
                    wait(pe, v_sb, a, n - 3)
                u = slice(uc * P, (uc + 1) * P)
                w = slice(nb * 512, (nb + 1) * 512)
                three((S + O)[n % 4][:], xh[:, u], xl[:, u], VOh[:, w], VOl[:, w]).then_inc(v_ps.sem, 1)

            def weigh(a, p):
                wait(pe, ex_sb, a, 2 * p + 2)
                if p == 0:
                    wait(pe, v_sb, a, 8)
                for j in range(2):
                    h = 2 * p + j
                    if h >= 2:
                        wait(pe, comb, a, h - 1)
                    for tc in range(TC):
                        c = j * T + tc * P
                        for uc in range(TC):
                            ins = mm(O[j][:, tc * T:tc * T + D + 1], Ex[:, p % 2, uc, c:c + P], V[:, uc, h, :],
                                     start=(uc == 0), stop=(uc == TC - 1))
                    ins.then_inc(av_ps.sem, 1)

            def attention(part, a, p, more, between):
                if part == "start":
                    wait(pe, xl_sb, a)
                    y(a, 0)
                    for n in range(4):
                        v_piece(a, n)
                    guard(a, 0, 0)
                    y(a, 1)
                    for n in range(4, 6):
                        v_piece(a, n)
                    guard(a, 0, 1)
                elif part == "scores":
                    scores(a, p, 0)
                    if p + 1 < HP:
                        guard(a, p + 1, 0)
                    scores(a, p, 1)
                    minus_max(a, p, 0)
                    minus_max(a, p, 1)
                elif part == "values":
                    if p + 2 < HP:
                        y(a, p + 2)
                    if p + 1 < HP:
                        guard(a, p + 1, 1)
                    if p == 0:
                        v_piece(a, 6)
                        v_piece(a, 7)
                    else:
                        weigh(a, p - 1)
                else:
                    weigh(a, HP - 1)
                between()

            def turn(out, src):
                for c in range(TC):
                    ins = nc.tensor.transpose(out[:, c * P:(c + 1) * P], src[:, c, :], ident[:])
                return ins

            def experts(b):
                on = pe.value_load(flag[0:1, 0:1], min_val=0, max_val=1)
                with pe.If(on > 0):
                    if isinstance(b, int) and b == NB - 1:
                        wait(pe, comb, b, H)
                    else:
                        wait(pe, yl_sb, b + 1, 5)
                        wait(pe, ex_sb, b + 1, 8)
                        wait(pe, comb, b + 1, 4)

                    def gate_up(it, l):
                        q = it * 4 + l
                        grp = l // 2
                        wait(pe, rw_ld[grp], b, it * 32 + 32)
                        banks = (Y, O[1]) if l % 2 == 0 else S
                        for c in range(TC):
                            wait(pe, rh_sb, b, q * 2 + c - 3)
                            w = wgu_in[:, grp, (l % 2) * 4 * FX:(l % 2 + 1) * 4 * FX]
                            mm(banks[c][:, 0:4 * FX], x1T[:, c * P:(c + 1) * P], w, start=True, stop=True)\
                                .then_inc(rgu_ps.sem, 1)

                    def turn_down(it, l):
                        q = it * 4 + l
                        wait(pe, rh_sb, b, q * 2 + 2)
                        wait(pe, rhT_sb, b, q)
                        for c in range(TC):
                            for e in range(2):
                                n = c * 2 + e
                                ins = nc.tensor.transpose(O[0][0:FX, n * P:(n + 1) * P], rh[:, l % 2, c, e, :],
                                                          ident[:])
                        ins.then_inc(rT_ps.sem, 1)

                    def down(it, l):
                        q = it * 4 + l
                        wait(pe, rhT_sb, b, q + 1)
                        for c in range(TC):
                            for e in range(2):
                                n = c * 2 + e
                                k = (l % 2) * 2 + e
                                ins = mm(M[:, c * P:(c + 1) * P], rhT[:, l % 2, n * P:(n + 1) * P],
                                         wd_in[:, l // 2, k * D:(k + 1) * D], start=False, stop=False,
                                         skip_group_check=True)
                        ins.then_inc(rd_ps.sem, 1)

                    def pairs(it, last):
                        for l in range(4):
                            if l < 3:
                                gate_up(it, l + 1)
                            elif not last:
                                gate_up(it + 1, 0)
                            turn_down(it, l)
                            down(it, l)

                    gate_up(0, 0)
                    with pe.Fori(0, 7) as it:
                        pairs(it, False)
                    pairs(7, True)
                with pe.Else():
                    pe.sem_inc(rgu_ps.sem, E)
                    pe.sem_inc(rT_ps.sem, PAIRS)
                    pe.sem_inc(rd_ps.sem, PAIRS)

            def mid(b, pos):
                if pos == 0:
                    wait(pe, x1_sb, b)
                    wait(pe, wo_read, b, 0)
                    turn(M, x1).then_inc(x1T_ps.sem, 1)
                elif pos == 1:
                    wait(pe, x1h_sb, b)
                    for c in range(TC):
                        ins = mm(M[:, c * E:(c + 1) * E], x1T[:, c * P:(c + 1) * P], rw[:], start=True, stop=True)
                    ins.then_inc(logits_ps.sem, 1)
                elif pos == 3:
                    wait(pe, x1l_sb, b)
                    wait(pe, ew_sb, b)
                    wh, wl = w_split["wsgu"]
                    for n in range(2):
                        w = slice(n * FX, (n + 1) * FX)
                        ins = three(M[0:FX, n * T:(n + 1) * T], wh[:, w], wl[:, w], x1h[:], x1l[:])
                    ins.then_inc(sgu_ps.sem, 1)
                elif pos == 5:
                    wait(pe, hs_sb, b)
                    m0, m1 = mask[:, 0, :], mask[:, 1, :]
                    mm(M[:, 0:E], before[:], m0, start=True, stop=True)
                    mm(M[:, E:2 * E], before[:], m1, start=True, stop=False)
                    mm(M[:, E:2 * E], ones_bf[:], m0, start=False, stop=True)
                    mm(M[:, 2 * E:3 * E], ones_bf[:], m0, start=True, stop=False)
                    mm(M[:, 2 * E:3 * E], ones_bf[:], m1, start=False, stop=True).then_inc(cum_ps.sem, 1)
                elif pos == 6:
                    wait(pe, coef_sb, b)
                    for c in range(TC):
                        ins = mm(M[:, c * P:(c + 1) * P], hs[:, c * P:(c + 1) * P], wsd[:], start=(c == 0),
                                 stop=False, skip_group_check=True)
                    ins.then_inc(sd_ps.sem, 1)
                elif pos == 7:
                    wait_alone(pe, coef_sb, b, 1, const_sb)
                    experts(b)
                elif pos == 9:
                    wait(pe, x2_sb, b)
                    turn(M, x2).then_inc(x2T_ps.sem, 1)
                elif pos == 10:
                    wait(pe, x2l_sb, b)
                    wh, wl = w_split["wkv"]
                    for c in range(TC):
                        t = slice(c * P, (c + 1) * P)
                        ins = three(M[:, c * 2 * D:(c + 1) * 2 * D], x2h[:, t], x2l[:, t], wh[:], wl[:])
                    ins.then_inc(kv_ps.sem, 1)
                elif pos == 11:
                    wait(pe, kvm_sb, b)
                    wh, wl = w_split["wq"]
                    three(M[:, 0:T], wh[:], wl[:], x2h[:], x2l[:]).then_inc(q_ps.sem, 1)
                elif pos == 12:
                    wait(pe, kf_sb, b)
                    wait(pe, qm_sb, b)
                    for c in range(TC):
                        ins = mm(M[:, 0:D + 1], kf[:, c, :], vt[:, c, :], start=(c == 0), stop=(c == TC - 1))
                    ins.then_inc(kvp_ps.sem, 1)
                elif pos == 13:
                    wait(pe, kvz_sb, b)
                    wait(pe, qf_sb, b)
                    for c in range(TC):
                        ins = mm(M[:, c * 2 * D:c * 2 * D + D + G1], qf[:, c * P:(c + 1) * P], kvz[:], start=True,
                                 stop=True)
                    ins.then_inc(nd_ps.sem, 1)
                elif pos == 14:
                    wait(pe, o1_sb, b)
                    turn(M, o1).then_inc(oT_ps.sem, 1)
                elif pos == 15:
                    wait(pe, oT_sb, b)
                    for c in range(TC):
                        ins = mm(M[:, c * D:(c + 1) * D], oT[:, c * P:(c + 1) * P], wout[:], start=True, stop=True)
                    ins.then_inc(wo_ps.sem, 1)

            def ffn_products(c, pos, low):
                if pos == 0:
                    wait(pe, x3_sb, c)
                    wait(pe, w3_read, c, 0)
                    turn(F, x3).then_inc(x3T_ps.sem, 1)
                elif 1 <= pos < 1 + KB:
                    j = pos - 1
                    if j == 0:
                        wait(pe, x3l_sb, c)
                    else:
                        wait(pe, a1_sb, c, j)
                    for out, name in ((F[:, 0:T], "w1"), (F[:, T:2 * T], "w2")):
                        wh, wl = w_split[name]
                        w = slice(j * P, (j + 1) * P)
                        if low:
                            ins = three(out, wh[:, w], wl[:, w], x3h[:], x3l[:])
                        else:
                            mm(out, wh[:, w], x3h[:], start=True, stop=False)
                            ins = mm(out, wh[:, w], x3l[:], start=False, stop=True)
                    ins.then_inc(w12_ps.sem, 1)
                elif pos in (5, 6, 8, 9):
                    n, name, mh, ml, lo, done = {
                        5: (0, "h1", a1h, a1l, a1l_sb, h1_ps), 6: (1, "h1", a1h, a1l, a1l_sb, h1_ps),
                        8: (0, "h2", a2h, a2l, a2l_sb, h2_ps), 9: (1, "h2", a2h, a2l, a2l_sb, h2_ps)}[pos]
                    if pos == 5:
                        wait(pe, a1_sb, c, KB)
                    elif pos == 6:
                        wait(pe, a2_sb, c, 1)
                    elif pos == 8:
                        wait(pe, a2_sb, c, 2)
                    elif pos == 9:
                        wait(pe, a3_sb, c, 1)
                    wh, wl = w_split[name]
                    for j in range(2):
                        for kb in range(KB):
                            w = slice(kb * DH + (2 * n + j) * P, kb * DH + (2 * n + j + 1) * P)
                            t = slice(kb * T, (kb + 1) * T)
                            o = F[:, j * T:(j + 1) * T]
                            if j == 0 and n == 0:
                                wait(pe, lo, c, kb + 1 if lo is a1l_sb else kb // 2 + 1)
                            mm(o, wh[:, w], mh[:, t], start=(kb == 0), stop=False)
                            if low:
                                mm(o, wl[:, w], mh[:, t], start=False, stop=False)
                            ins = mm(o, wh[:, w], ml[:, t], start=False, stop=(kb == KB - 1))
                    ins.then_inc(done.sem, 1)
                elif pos == 12:
                    wait(pe, a3_sb, c, 2)
                    for t in range(TC):
                        for kb in range(KB):
                            ins = mm(F[:, t * D:(t + 1) * D], a3[:, kb * T + t * P:kb * T + (t + 1) * P], w3[:, kb, :],
                                     start=(kb == 0), stop=(kb == KB - 1))
                    ins.then_inc(w3_ps.sem, 1)

            pe.wait_ge(al_sb.sem, 4)
            pe.wait_ge(vo_split.sem, 4)
            pe.wait_ge(const_sb.sem, 5)
            pe.wait_ge(ones_sb.sem, 6)

            fill(attention)
            pe.wait_ge(small_ld.sem, 16 * (len(SMALL) + len(ROWS)))
            pe.wait_ge(inexact_sb.sem, FFN_PIECES)
            for n in range(FFN_PIECES):
                ins = mm(M[:], ones_bf[:], inexact[:, n * PIECE:(n + 1) * PIECE], start=(n == 0),
                         stop=(n == FFN_PIECES - 1))
            ins.then_inc(low_ps.sem, 1)
            pe.wait_ge(low_sb.sem, 1)
            low_on = pe.value_load(low_flag[0:1, 0:1], min_val=0, max_val=1)
            with pe.If(low_on > 0):
                pipeline(pe, attention, mid, lambda c, pos: ffn_products(c, pos, True), NB)
            with pe.Else():
                pipeline(pe, attention, mid, lambda c, pos: ffn_products(c, pos, False), NB)

        @block.scalar
        def _(act):
            act_do = nc.scalar.activation
            act.sem_inc(rhT_sb.sem, rhT_sb.credit)
            for n in range(4):
                act.wait_ge(a_ps.sem, n + 1)
                act_do(Ah[:, n * 512:(n + 1) * 512], S[n % 2][:], ACT.Copy).then_inc(ah_sb.sem, 1)
            act.wait_ge(xT_ld.sem, 16)
            act_do(xh[:], xT_in[:], ACT.Copy).then_inc(xh_sb.sem, 1)

            def y_high(a, p):
                wait(act, y_ps, a, p + 1)
                wait(act, s_ps, a, 2 * p - 2)
                act_do(yh[:, p % 2, :], Y[:], ACT.Copy).then_inc(yh_sb.sem, 1)

            def v_copy(a, n):
                wait(act, v_ps, a, n + 1)
                if n == 0:
                    wait(act, av_ps, a, 0)
                uc, nb = n // 4, n % 4
                act_do(V[:, uc, 4 * nb:4 * nb + 4, 0:D], (S + O)[n % 4][:].rearrange("p (h d) -> p h d", d=D), ACT.Copy)\
                    .then_inc(v_sb.sem, 1)

            LATE = 4

            def exponentials(a, p):
                for uc in range(TC):
                    wait(act, s_ps, a, 2 * p + uc + 1)
                    wait(act, av_ps, a, 2 * p - 2)
                    act_do(Ex[:, p % 2, uc, :], S[uc][:], ACT.Exp, scale=SCALE).then_inc(ex_sb.sem, 1)

            def attention(part, a, p, more, between):
                if part == "start":
                    between()
                    y_high(a, 0)
                    for n in range(4):
                        v_copy(a, n)
                    y_high(a, 1)
                    for n in range(4, 6):
                        v_copy(a, n)
                elif part == "scores":
                    between()
                    if p != LATE:
                        exponentials(a, p)
                elif part == "values":
                    between()
                    if p + 2 < HP:
                        y_high(a, p + 2)
                    if p == 0:
                        v_copy(a, 6)
                        v_copy(a, 7)
                    if p == LATE:
                        exponentials(a, p)
                    if p == HP - 1 and more:
                        wait(act, xT_ld, a + 1, 16)
                        wait(act, s_ps, a, 2 * HP)
                        act_do(xh[:], xT_in[:], ACT.Copy).then_inc(xh_sb.sem, 1)
                else:
                    between()

            def experts(b):
                on = act.value_load(flag[0:1, 0:1], min_val=0, max_val=1)
                with act.If(on > 0):
                    def tanh(it, l):
                        q = it * 4 + l
                        banks = (Y, O[1]) if l % 2 == 0 else S
                        for c in range(TC):
                            wait(act, rgu_ps, b, q * 2 + c + 1)
                            wait(act, rt_sb, b, q * 2 + c - 1)
                            gate = banks[c][:, 0:4 * FX].rearrange("p (e n) -> p e n", e=2)[:, :, 0:FX]
                            act_do(rth[:, c, :, :], gate, ACT.Tanh, scale=0.5).then_inc(rth_sb.sem, 1)

                    def hidden(it, l):
                        q = it * 4 + l
                        wait(act, rT_ps, b, q + 1)
                        wait(act, rd_ps, b, q - 1)
                        act_do(rhT[:, l % 2, :], O[0][0:FX, :], ACT.Copy).then_inc(rhT_sb.sem, 1)

                    tanh(0, 0)
                    with act.Fori(0, 7) as it:
                        for l in range(4):
                            if l < 3:
                                tanh(it, l + 1)
                            else:
                                tanh(it + 1, 0)
                            hidden(it, l)
                    for l in range(4):
                        if l < 3:
                            tanh(7, l + 1)
                        hidden(7, l)
                with act.Else():
                    act.sem_inc(rth_sb.sem, E)
                    act.sem_inc(rhT_sb.sem, PAIRS)

            def halves(full, hi, done):
                act_do(full, M[:, 0:T], ACT.Copy)
                act_do(hi, M[:, 0:T], ACT.Copy).then_inc(done.sem, 1)

            def mid(b, pos):
                if pos == 1:
                    wait(act, x1T_ps, b)
                    halves(x1T[:], x1h[:], x1h_sb)
                elif pos == 3:
                    wait(act, mask_sb, b)
                    for c in range(TC):
                        ins = act_do(ew[:, c, :], M[:, c * E:(c + 1) * E], ACT.Exp, bias=negmax[:, c:c + 1])
                    ins.then_inc(ew_sb.sem, 1)
                elif pos == 4:
                    wait(act, sgu_ps, b)
                    act_do(sth[:], M[0:FX, 0:T], ACT.Tanh, scale=0.5).then_inc(sth_sb.sem, 1)
                elif pos == 8:
                    wait_alone(act, coef_sb, b, 1, const_sb)
                    experts(b)
                elif pos == 10:
                    wait(act, x2T_ps, b)
                    halves(x2T[:], x2h[:], x2h_sb)
                elif pos == 11:
                    wait(act, kv_ps, b)
                    kv = M[:].rearrange("p (c n) -> p c n", c=TC)
                    act_do(kmin, kv[:, :, 0:D], ACT.Relu, scale=-1.0)
                    act_do(kmax, kv[:, :, 0:D], ACT.Relu)
                    act_do(vt[:, :, 0:D], kv[:, :, D:2 * D], ACT.Copy).then_inc(kvm_sb.sem, 1)
                    wait(act, kvm_sb, b)
                    act_do(ke, kmin, ACT.Exp, scale=-1.0).then_inc(kve_sb.sem, 1)
                elif pos == 12:
                    wait(act, q_ps, b)
                    act_do(qmin[:], M[:, 0:T], ACT.Relu, scale=-1.0)
                    act_do(qmax[:], M[:, 0:T], ACT.Relu).then_inc(qm_sb.sem, 1)
                    wait(act, qm_sb, b)
                    act_do(qe[:], qmin[:], ACT.Exp, scale=-1.0).then_inc(qe_sb.sem, 1)
                elif pos == 15:
                    wait(act, oT_ps, b)
                    act_do(oT[:], M[:, 0:T], ACT.Copy).then_inc(oT_sb.sem, 1)

            def a1_high(c, j):
                t = slice(j * T, (j + 1) * T)
                wait(act, a1_sb, c, j + 1)
                act_do(a1h[:, t], a1[:, t], ACT.Copy).then_inc(a1h_sb.sem, 1)

            def gelu(ps, out, scales, n, done):
                for j in range(2):
                    f = 2 * n + j
                    ins = act_do(out[:, f * T:(f + 1) * T], F[:, j * T:(j + 1) * T], ACT.Gelu, scale=scales[:, f:f + 1])
                ins.then_inc(done.sem, 1)

            def ffn(c, pos):
                if pos == 1:
                    wait(act, x3T_ps, c)
                    act_do(x3T[:], F[:, 0:T], ACT.Copy)
                    act_do(x3h[:], F[:, 0:T], ACT.Copy).then_inc(x3h_sb.sem, 1)
                if 2 <= pos < 2 + KB:
                    j = pos - 2
                    wait(act, w12_ps, c, j + 1)
                    wait(act, a1_sb, c, j)
                    act_do(fth[:], F[:, 0:T], ACT.Tanh, scale=s1half[:, j:j + 1]).then_inc(fth_sb.sem, 1)
                if pos in (3, 4, 5):
                    a1_high(c, pos - 3)
                if pos == 5:
                    a1_high(c, 3)
                if pos in (6, 7):
                    n = pos - 6
                    wait(act, h1_ps, c, n + 1)
                    gelu(h1_ps, a2, sh1, n, a2_sb)
                    wait(act, a2_sb, c, n + 1)
                    act_do(a2h[:, 512 * n:512 * n + 512], a2[:, 512 * n:512 * n + 512], ACT.Copy).then_inc(a2h_sb.sem, 1)
                if pos in (9, 10):
                    n = pos - 9
                    wait(act, h2_ps, c, n + 1)
                    gelu(h2_ps, a3, sh2, n, a3_sb)

            def high_halves(_, pos):
                if 1 <= pos <= len(PIECES):
                    n = pos - 1
                    name, c, w = PIECES[n]
                    act.wait_ge(split_ld[n % 4].sem, 16 * (n // 4 + 1))
                    act_do(w_split[name][0][:, c:c + w], stage_in[:, n % 4, 0:w], ACT.Copy).then_inc(split_hi.sem, 1)

            fill(attention, high_halves)
            act.wait_ge(half_sb.sem, 4)
            pipeline(act, attention, mid, ffn, NB)

        @block.vector
        def _(dve):
            v = nc.vector
            links = Order(nc, ctx, dve, "mid_order", 9)
            ffn_links = Order(nc, ctx, dve, "ffn_order", KB)
            den_order = sig("den_order", H)

            vo_hi = sig("vo_hi")
            for n in range(4):
                w = slice(n * PIECE, (n + 1) * PIECE)
                dve.wait_ge(vo_ld[n].sem, 16)
                v.tensor_copy(VOh[:, w], stage_in[:, n, :]).then_inc(vo_hi.sem, 1)
            for n in range(4):
                w = slice(n * PIECE, (n + 1) * PIECE)
                dve.wait_ge(vo_hi.sem, n + 1)
                v.tensor_tensor(VOl[:, w], stage_in[:, n, :], VOh[:, w].bitcast(F32), ALU.subtract)\
                    .then_inc(vo_split.sem, 1)
            for n in range(4):
                w = slice(n * 512, (n + 1) * 512)
                dve.wait_ge(ah_sb.sem, n + 1)
                v.tensor_tensor(Al[:, w], S[n % 2][:], Ah[:, w].bitcast(F32), ALU.subtract).then_inc(al_sb.sem, 1)
            dve.wait_ge(xh_sb.sem, 1)
            v.tensor_tensor(xl[:], xT_in[:], xh[:].bitcast(F32), ALU.subtract).then_inc(xl_sb.sem, 1)
            v.memset(taken[:], 0.0).then_inc(half_sb.sem, 1)
            dve.sem_inc(rt_sb.sem, rt_sb.credit)
            dve.sem_inc(rh_sb.sem, rh_sb.credit)

            def y_low(a, p):
                wait(dve, yh_sb, a, p + 1)
                v.tensor_tensor(yl[:, p % 2, :], Y[:], yh[:, p % 2, :].bitcast(F32), ALU.subtract)\
                    .then_inc(yl_sb.sem, 1)

            def row_max(a, p, tc):
                wait(dve, g_ps, a, 2 * p + tc + 1)
                wait(dve, s_ps, a, 2 * p - 2)
                v.tensor_reduce(negm[:, p % 2, tc, :], G[:].rearrange("p (j u) -> p j u", j=2), AX.X, ALU.max,
                                negate=True).then_inc(negm_sb.sem, 1)

            def combine(a, h):
                wait(dve, av_ps, a, h + 1)
                o = O[h % 2][:].rearrange("p (c n) -> p c n", c=TC)
                v.reciprocal(rden[:, h % 2, :], o[:, :, D]).then_inc(den_order.sem, 1)
                wait(dve, den_order, a, h + 1)
                if h == 0:
                    wait(dve, x_ld, a, 16)
                for tc in range(TC):
                    ins = v.scalar_tensor_tensor(out=acc[:, tc, :], in0=o[:, tc, 0:D], scalar=rden[:, h % 2, tc:tc + 1],
                                                 in1=(x_res if h == 0 else acc)[:, tc, :], op0=ALU.mult, op1=ALU.add)
                ins.then_inc(comb.sem, 1)

            def spread(b, n, src):
                for c in range(TC):
                    ins = v.bn_stats(stats[:, n, c, :], src[:, c, :])
                ins.then_inc(stats_sb[n].sem, 1)
                wait(dve, stats_sb[n], b)
                v.memset(spacer[:, n:n + 1], 0.0)
                for c in range(TC):
                    ins = v.bn_aggr(mv[:, n, c, :], stats[:, n, c, :])
                ins.then_inc(var_sb[n].sem, 1)

            def normalize(b, n, src, dst, done):
                wait(dve, rstd_sb[n], b)
                for c in range(TC):
                    ins = v.tensor_scalar(dst[:, c, :], src[:, c, :], mv[:, n, c, 0:1], rstd[:, n, c:c + 1],
                                          ALU.subtract, ALU.mult)
                ins.then_inc(done.sem, 1)

            def attention(part, a, p, more, between):
                if part == "start":
                    y_low(a, 0)
                    between()
                    row_max(a, 0, 0)
                    y_low(a, 1)
                    row_max(a, 0, 1)
                elif part == "scores":
                    between()
                    if p + 1 < HP:
                        row_max(a, p + 1, 0)
                elif part == "values":
                    between()
                    if p + 2 < HP:
                        y_low(a, p + 2)
                    if p + 1 < HP:
                        row_max(a, p + 1, 1)
                    if p >= 1:
                        combine(a, 2 * p - 2)
                        combine(a, 2 * p - 1)
                    if p == HP - 1 and more:
                        wait(dve, xh_sb, a + 1)
                        v.tensor_tensor(xl[:], xT_in[:], xh[:].bitcast(F32), ALU.subtract).then_inc(xl_sb.sem, 1)
                else:
                    between()
                    combine(a, H - 2)
                    combine(a, H - 1)
                    wait(dve, comb, a, H)
                    spread(a, 0, acc)

            def experts(b):
                on = dve.value_load(flag[0:1, 0:1], min_val=0, max_val=1)
                with dve.If(on > 0):
                    def hidden(it, l):
                        q = it * 4 + l
                        banks = (Y, O[1]) if l % 2 == 0 else S
                        halves = [banks[c][:, 0:4 * FX].rearrange("p (e n) -> p e n", e=2) for c in range(TC)]
                        for c in range(TC):
                            wait(dve, rth_sb, b, q * 2 + c + 1)
                            wait(dve, rh_sb, b, q * 2 + c - 1)
                            v.scalar_tensor_tensor(out=rt[:, c, :, :], in0=rth[:, c, :, :], scalar=1.0,
                                                   in1=halves[c][:, :, 0:FX], op0=ALU.add, op1=ALU.mult)\
                                .then_inc(rt_sb.sem, 1)
                        wait(dve, rT_ps, b, q - 1)
                        for c in range(TC):
                            wait(dve, rt_sb, b, q * 2 + c + 1)
                            for e in range(2):
                                ins = v.scalar_tensor_tensor(out=rh[:, l % 2, c, e, :], in0=rt[:, c, e, :],
                                                             scalar=coef8[:, c, 2 * l + e:2 * l + e + 1],
                                                             in1=halves[c][:, e, FX:2 * FX], op0=ALU.mult,
                                                             op1=ALU.mult)
                            ins.then_inc(rh_sb.sem, 1)

                    with dve.Fori(0, E // 8) as it:
                        wait(dve, rh_sb, b, it * 8)
                        v.tensor_copy(coef8[:], coef[:, :, bass.ds(it * 8, 8)]).then_inc(c8_sb.sem, 1)
                        wait(dve, c8_sb, b, it + 1)
                        for l in range(4):
                            hidden(it, l)
                with dve.Else():
                    dve.sem_inc(rt_sb.sem, E)
                    dve.sem_inc(rh_sb.sem, E)
                    dve.sem_inc(c8_sb.sem, E // 8)

            def mid(b, pos):
                if pos == 0:
                    links.start(b)
                    normalize(b, 0, acc, x1, x1_sb)
                elif pos == 2:
                    wait_alone(dve, logits_ps, b, 1, const_sb)
                    l3 = M[:, 0:TC * E].rearrange("p (c e) -> p c e", c=TC)
                    for c in range(TC):
                        ins = v.max(top8[:, c, :], l3[:, c, :])
                    links.link(ins)
                    v.tensor_scalar(negmax[:], top8[:, :, 0], -1.0, None, ALU.mult)
                    for c in range(TC):
                        ins = v.match_replace(rest[:, c, :], top8[:, c, :], l3[:, c, :], -3.0e38)
                    links.link(ins)
                    v.tensor_tensor(mask[:], l3, rest[:], ALU.not_equal).then_inc(mask_sb.sem, 1)
                elif pos == 4:
                    wait(dve, wm_sb, b)
                    links.link(v.tensor_reduce(wsum[:], wm[:], AX.X, ALU.add))
                    links.link(v.reciprocal(wrec[:], wsum[:]))
                elif pos == 5:
                    wait(dve, sth_sb, b)
                    links.link(v.scalar_tensor_tensor(out=st[:], in0=sth[:], scalar=1.0, in1=M[0:FX, 0:T],
                                                      op0=ALU.add, op1=ALU.mult))
                    v.scalar_tensor_tensor(out=hs[:], in0=st[:], scalar=0.5, in1=M[0:FX, T:2 * T],
                                           op0=ALU.mult, op1=ALU.mult).then_inc(hs_sb.sem, 1)
                elif pos == 6:
                    wait(dve, cum_ps, b)
                    tot = M[:, 2 * E:3 * E]
                    v.scalar_tensor_tensor(out=live[:], in0=taken[:], scalar=CAPACITY, in1=tot, op0=ALU.is_lt,
                                           op1=ALU.mult)
                    for c in range(TC):
                        ins = v.tensor_tensor(place[:, c, :], M[:, c * E:(c + 1) * E], taken[:], ALU.add)
                    links.link(ins)
                    v.tensor_tensor(taken[:], tot, taken[:], ALU.add)
                    v.tensor_reduce(livemax[:], live[:], AX.X, ALU.max)
                    links.link(v.scalar_tensor_tensor(out=place[:], in0=place[:], scalar=CAPACITY, in1=wm[:],
                                                      op0=ALU.is_lt, op1=ALU.mult))
                    wait(dve, rw_ld[1], b, 0)
                    v.tensor_scalar(flag[:], livemax[:], 1.0, None, ALU.min)
                    for c in range(TC):
                        ins = v.tensor_scalar(coef[:, c, :], place[:, c, :], wrec[:, c:c + 1], 0.5, ALU.mult, ALU.mult)
                    ins.then_inc(coef_sb.sem, 1)
                elif pos == 7:
                    wait_alone(dve, coef_sb, b, 1, const_sb)
                    experts(b)
                elif pos == 8:
                    wait(dve, sd_ps, b)
                    wait(dve, rd_ps, b, PAIRS)
                    v.tensor_tensor(res[:], M[:, 0:T].rearrange("p (c d) -> p c d", c=TC), x1[:], ALU.add)\
                        .then_inc(moe_read.sem, 1)
                    wait(dve, moe_read, b)
                    spread(b, 1, res)
                elif pos == 9:
                    normalize(b, 1, res, x2, x2_sb)
                elif pos == 13:
                    wait(dve, kvp_ps, b)
                    v.tensor_tensor(kvz[:, 0:D], M[:, 0:D], headmask[:], ALU.mult)
                    one_each = headmask[:].rearrange("p (g e) -> p g e", e=HEAD_DIM1)[:, :, 0]
                    v.tensor_scalar(kvz[:, D:D + G1], one_each, M[:, D:D + 1], None, ALU.mult)\
                        .then_inc(kvz_sb.sem, 1)
                elif pos == 14:
                    wait(dve, nd_ps, b)
                    nd = M[:].rearrange("p (c n) -> p c n", c=TC)
                    links.link(v.tensor_scalar(den[:], nd[:, :, D:D + G1], Z_EPS, None, ALU.add))
                    links.link(v.reciprocal(dinv[:], den[:]))
                    for c in range(TC):
                        ins = v.tensor_tensor(o1[:, c, :].rearrange("p (g e) -> p g e", e=HEAD_DIM1),
                                              nd[:, c, 0:D].rearrange("p (g e) -> p g e", e=HEAD_DIM1),
                                              dinv[:, c, :].to_broadcast([P, G1, HEAD_DIM1]), ALU.mult)
                    ins.then_inc(o1_sb.sem, 1)
                elif pos == 16:
                    wait(dve, wo_ps, b)
                    wait(dve, x2b_sb, b)
                    v.tensor_tensor(res[:], M[:, 0:T].rearrange("p (c d) -> p c d", c=TC), x2b[:], ALU.add)\
                        .then_inc(wo_read.sem, 1)
                elif pos == 17:
                    wait(dve, wo_read, b)
                    spread(b, 2, res)
                    links.end()

            def ffn(c, pos):
                if pos == 0:
                    ffn_links.start(c)
                    wait(dve, res_ffn_sb, c, 0)
                    normalize(c, 2, res, x3, x3_sb)
                elif 2 <= pos < 2 + KB:
                    j = pos - 2
                    wait(dve, fth_sb, c, j + 1)
                    ffn_links.link(v.scalar_tensor_tensor(out=ft[:], in0=fth[:], scalar=1.0, in1=F[:, 0:T],
                                                          op0=ALU.add, op1=ALU.mult))
                    v.scalar_tensor_tensor(out=a1[:, j * T:(j + 1) * T], in0=F[:, T:2 * T],
                                           scalar=s12half[:, j:j + 1], in1=ft[:], op0=ALU.mult, op1=ALU.mult)\
                        .then_inc(a1_sb.sem, 1)
                elif pos == 13:
                    wait(dve, w3_ps, c)
                    for t in range(TC):
                        ins = v.tensor_tensor(res_ffn[:, t, :], F[:, t * D:(t + 1) * D], s3[:], ALU.mult)
                    ins.then_inc(w3_read.sem, 1)
                elif pos == 14:
                    wait(dve, res_ffn_sb, c)
                    spread(c, 3, res_ffn)
                elif pos == 15:
                    wait(dve, out_st, c, 0)
                    normalize(c, 3, res_ffn, yout, yout_sb)
                    ffn_links.end()

            def scales_ready():
                dve.wait_ge(const_sb.sem, 5)
                dve.wait_ge(small_ld.sem, 16 * (len(SMALL) + len(ROWS)))
                v.tensor_scalar(s1half[:], s1[:], 0.5, None, ALU.mult).then_inc(half_sb.sem, 1)
                v.tensor_tensor(s12half[:], s1[:], s2[:], ALU.mult).then_inc(half_sb.sem, 1)
                dve.wait_ge(half_sb.sem, 3)
                v.tensor_scalar(s12half[:], s12half[:], 0.5, None, ALU.mult).then_inc(half_sb.sem, 1)
                dve.wait_ge(half_sb.sem, 4)

            def inexact_weights(_, pos):
                n = pos - 3
                if FIRST_FFN <= n < len(PIECES):
                    name, c, w = PIECES[n]
                    m = (n - FIRST_FFN) * PIECE
                    dve.wait_ge(split_lo.sem, n + 1)
                    v.tensor_scalar(inexact[:, m:m + w], w_split[name][1][:, c:c + w].bitcast(F32), 0.0, None,
                                    ALU.not_equal).then_inc(inexact_sb.sem, 1)

            def low_halves():
                dve.wait_ge(low_ps.sem, 1)
                v.tensor_reduce(inexact_sum[:], M[:], AX.X, ALU.add).then_inc(inexact_sum_sb.sem, 1)
                dve.wait_ge(inexact_sum_sb.sem, 1)
                v.tensor_scalar(low_flag[:], inexact_sum[:], 1.0, None, ALU.min).then_inc(low_sb.sem, 1)

            fill(attention, inexact_weights)
            low_halves()
            scales_ready()
            pipeline(dve, attention, mid, ffn, NB)


def kernel(**inputs):
    import concourse.bacc as bacc
    from concourse.bass_utils import run_bass_kernel_spmd

    g = {k: np.asarray(v) for k, v in inputs.items()}
    x = g["L0_attn_x"]
    nb, t, d = x.shape
    heads, rank, _ = g["L0_attn_Q"].shape
    experts, _, fx = g["L0_ffn_w_gate"].shape
    kb = g["L1_ffn_h1_w"].shape[0] // 128

    def blocks(w):
        wt = w.T
        return wt.reshape(-1, 128, wt.shape[1]).transpose(1, 0, 2)

    def by_feature(s):
        return s.reshape(-1, 128).T

    wqkv = g["L1_attn_Wqkv"]
    gate_up = np.concatenate([g["L0_ffn_w_gate"], g["L0_ffn_w_up"]], axis=2)
    arrays = {
        "x": x,
        "xT": x.transpose(0, 2, 1),
        "q": g["L0_attn_Q"].transpose(1, 0, 2).reshape(rank, heads * d),
        "k": g["L0_attn_K"].transpose(1, 0, 2).reshape(rank, heads * d),
        "vo": g["L0_attn_VO"].transpose(1, 0, 2).reshape(d, heads * d),
        "rw": g["L0_ffn_router_w"].T,
        "wgu": gate_up.reshape(experts // 4, 4, d, 2 * fx).transpose(0, 2, 1, 3).reshape(experts // 4, d, 8 * fx),
        "wd": g["L0_ffn_w_down"].reshape(experts // 4, 4, fx, d).transpose(0, 2, 1, 3)
        .reshape(experts // 4, fx, 4 * d),
        "wsgu": g["L0_ffn_ws_gate_up"],
        "wsd": g["L0_ffn_ws_down"],
        "wq": wqkv[0:d].T,
        "wkv": wqkv[d:3 * d].T,
        "wout": g["L1_attn_Wout"].T,
        "bout": g["L1_attn_bout"],
        "w1": g["L1_ffn_w1_w"].T,
        "w2": g["L1_ffn_w2_w"].T,
        "h1": blocks(g["L1_ffn_h1_w"]).reshape(128, -1),
        "h2": blocks(g["L1_ffn_h2_w"]).reshape(128, -1),
        "w3": blocks(g["L1_ffn_w3_w"]),
        "s1": by_feature(g["L1_ffn_w1_s"]),
        "s2": by_feature(g["L1_ffn_w2_s"]),
        "sh1": by_feature(g["L1_ffn_h1_s"]),
        "sh2": by_feature(g["L1_ffn_h2_s"]),
        "s3": g["L1_ffn_w3_s"],
    }
    nc = bacc.Bacc("TRN2", target_bir_lowering=False, num_devices=1)
    arrays = {k: np.ascontiguousarray(v) for k, v in arrays.items()}
    aps = {k: nc.dram_tensor("in_" + k, a.shape, mybir.dt.from_np(a.dtype), kind="ExternalInput").ap()
           for k, a in arrays.items()}
    aps["out"] = nc.dram_tensor("out", x.shape, F32, kind="ExternalOutput").ap()
    build(nc, aps)
    r = run_bass_kernel_spmd(nc, [{"in_" + k: a for k, a in arrays.items()}], core_ids=[0])
    return r.results[0]["out"]
```

```python
from contextlib import ExitStack

import numpy as np

import concourse.bass as bass
from concourse import mybir

F32 = mybir.dt.float32
F32R = mybir.dt.float32r
BF16 = mybir.dt.bfloat16
I32 = mybir.dt.int32
ALU = mybir.AluOpType
ACT = mybir.ActivationFunctionType
AX = mybir.AxisListType

P = 128
SCALE = 1.0 / float(np.sqrt(128.0))
LN_EPS = 1e-5
Z_EPS = 1e-6
CAPACITY = 64.0
HEAD_DIM1 = 8
POSITIONS = 18
FFN_FIRST = (5, 13)
LATE = 4
PIECE = 512


class Signal:

    def __init__(self, nc, ctx, name, per=1, credit=0):
        self.sem = ctx.enter_context(nc.semaphore(name))
        self.per = per
        self.credit = credit

    def value(self, b, k=1):
        return b * self.per + (k + self.credit)


def wait(engine, signal, b, k=1):
    v = signal.value(b, k)
    if isinstance(v, int) and v <= 0:
        return
    engine.wait_ge(signal.sem, v)


def wait_alone(engine, signal, b, k, constants):
    engine.wait_ge(constants.sem, 5)
    wait(engine, signal, b, k)


class Order:

    def __init__(self, nc, ctx, engine, name, per):
        self.done = Signal(nc, ctx, name, per)
        self.engine = engine
        self.n = 0

    def start(self, b):
        self.b, self.n = b, 0

    def link(self, instruction):
        self.n += 1
        instruction.then_inc(self.done.sem, 1)
        wait(self.engine, self.done, self.b, self.n)

    def end(self):
        assert self.n == self.done.per, (self.n, self.done.per)


def interleave(attention, mid, ffn, a, b, c, more):
    for pos in range(POSITIONS):
        part = "start" if pos == 0 else "end" if pos == 17 else ("values", "scores")[pos % 2]

        def between():
            if c is not None and pos in FFN_FIRST:
                ffn(c, pos)
            if b is not None:
                mid(b, pos)
            if c is not None and pos not in FFN_FIRST:
                ffn(c, pos)

        if a is None:
            between()
        else:
            attention(part, a, (pos - 1) // 2, more, between)


def fill(attention, set_up=None):
    interleave(attention, set_up, None, 0, None if set_up is None else 0, None, True)


def pipeline(engine, attention, mid, ffn, n):
    interleave(attention, mid, ffn, 1, 0, None, True)
    interleave(attention, mid, ffn, 2, 1, 0, True)
    with engine.Fori(3, n - 1) as i:
        interleave(attention, mid, ffn, i, i - 1, i - 2, True)
    interleave(attention, mid, ffn, n - 1, n - 2, n - 3, False)
    interleave(attention, mid, ffn, None, n - 1, n - 2, False)
    interleave(attention, mid, ffn, None, None, n - 1, False)


def build(nc, A):
    NB, T, D = A["x"].shape
    H = A["vo"].shape[1] // D
    E = A["wgu"].shape[0] * 2
    KX = A["wd"].shape[2] // D
    FX = KX * P // 4
    R = A["q"].shape[0]
    DH = A["w1"].shape[1]
    KB = DH // P
    HP = H // 2
    TC = T // P
    assert (T, D, H, E, FX, TC, HP, KB) == (256, 128, 16, 64, 96, 2, 8, 4)
    GROUPS = E // 4
    PAIRS = E // 2

    with ExitStack() as ctx:
        def sb(name, shape, dt=F32):
            return ctx.enter_context(nc.sbuf_tensor(name, shape, dt))

        def bank(name):
            return ctx.enter_context(nc.psum_tensor(name, [P, 512], F32))

        def sig(name, per=1, credit=0):
            return Signal(nc, ctx, name, per, credit)

        xT_in = sb("xT_in", [P, T])
        x_res = sb("x_res", [P, TC, D])
        xh, xl = sb("xh", [P, T], F32R), sb("xl", [P, T], F32R)
        Ah, Al = sb("Ah", [P, H * D], F32R), sb("Al", [P, H * D], F32R)
        VOh, VOl = sb("VOh", [P, H * D], F32R), sb("VOl", [P, H * D], F32R)
        yh, yl = sb("yh", [P, 2, 512], F32R), sb("yl", [P, 2, 512], F32R)
        V = sb("V", [P, TC, H, D + 1])
        Ex = sb("Ex", [P, 2, TC, 512])
        negm = sb("negm", [P, 2, TC, 2], BF16)
        rden = sb("rden", [P, 2, TC])
        acc = sb("acc", [P, TC, D])
        stage_in = sb("stage_in", [P, 4, PIECE])
        w_split = {}
        for name, cols in (("w1", DH), ("w2", DH), ("h1", KB * DH), ("h2", KB * DH),
                           ("w3", KB * D), ("wsgu", 2 * FX), ("wq", D), ("wkv", 2 * D)):
            w_split[name] = (sb(name + "h", [P, cols], F32R), sb(name + "l", [P, cols], F32R))
        wsd = sb("wsd", [FX, D])
        wout = sb("wout", [P, D])
        rw = sb("rw", [P, E])
        s1 = sb("s1", [P, KB])
        s2 = sb("s2", [P, KB])
        sh1 = sb("sh1", [P, KB])
        sh2 = sb("sh2", [P, KB])
        s1half = sb("s1half", [P, KB])
        s12half = sb("s12half", [P, KB])
        s3 = sb("s3", [P, 1])
        bout = sb("bout", [P, D])
        ident = sb("ident", [P, P])
        ident_bf = sb("ident_bf", [P, P], BF16)
        ones_bf = sb("ones_bf", [P, P], BF16)
        before = sb("before", [P, P], BF16)
        headmask = sb("headmask", [P, P])
        ones = sb("ones", [P, P])
        minus_half = sb("minus_half", [P, TC])
        ln_eps = sb("ln_eps", [P, TC])
        spacer = sb("spacer", [P, 4])
        FF = sb("FF", [P, 3, KB * T])
        a1, a2, a3 = FF[:, 0, :], FF[:, 1, :], FF[:, 2, :]
        a1h, a1l = sb("a1h", [P, KB * T], F32R)[:], sb("a1l", [P, KB * T], F32R)[:]
        a2h, a2l = sb("a2h", [P, KB * T], F32R)[:], sb("a2l", [P, KB * T], F32R)[:]
        a3h, a3l = a2h, a2l
        fT = sb("fT", [P, T])
        fth = sb("fth", [P, 2, T])
        ft = sb("ft", [P, T])
        stats = sb("stats", [P, 4, TC, 6])
        mv = sb("mv", [P, 4, TC, 2])
        veps = sb("veps", [P, 4, TC])
        rstd = sb("rstd", [P, 4, TC])
        x1, x2, x3 = sb("x1", [P, TC, D]), sb("x2", [P, TC, D]), sb("x3", [P, TC, D])
        x2b = sb("x2b", [P, TC, D])
        res, res_ffn = sb("res", [P, TC, D]), sb("res_ffn", [P, TC, D])
        yout = sb("yout", [P, TC, D])
        x1T, x2T, x3T = sb("x1T", [P, T]), sb("x2T", [P, T]), sb("x3T", [P, T])
        x1h, x1l = sb("x1h", [P, T], F32R), sb("x1l", [P, T], F32R)
        x2h, x2l = sb("x2h", [P, T], F32R), sb("x2l", [P, T], F32R)
        x3h, x3l = sb("x3h", [P, T], F32R), sb("x3l", [P, T], F32R)
        top8 = sb("top8", [P, TC, 8])
        rest = sb("rest", [P, TC, E])
        mask = sb("mask", [P, TC, E], BF16)
        negmax = sb("negmax", [P, TC])
        ew = sb("ew", [P, TC, E])
        wm = sb("wm", [P, TC, E])
        wsum = sb("wsum", [P, TC])
        wrec = sb("wrec", [P, TC])
        place = sb("place", [P, TC, E])
        coef = sb("coef", [P, TC, E])
        taken = sb("taken", [P, E])
        live = sb("live", [P, E])
        livemax = sb("livemax", [P, 1])
        flag = sb("flag", [P, 1], I32)
        sth = sb("sth", [FX, T])
        st = sb("st", [FX, T])
        hs = sb("hs", [FX, T])
        kparts = sb("kparts", [P, 4, TC, D])
        kmin, kmax, ke, kf = (kparts[:, i, :, :] for i in range(4))
        qmin, qmax, qe, qf = (sb(n, [P, T]) for n in ("qmin", "qmax", "qe", "qf"))
        vt = sb("vt", [P, TC, D + 1])
        G1 = D // HEAD_DIM1
        kvz = sb("kvz", [P, D + G1])
        den = sb("den", [P, TC, G1])
        dinv = sb("dinv", [P, TC, G1])
        o1 = sb("o1", [P, TC, D])
        oT = sb("oT", [P, T])
        wgu_in = sb("wgu_in", [P, 4, 2 * 2 * FX])
        wd_in = sb("wd_in", [P, 2, KX * D])
        PAIR = TC * 2 * FX
        rth = a1[:, 0:PAIR].rearrange("p (c e n) -> p c e n", c=TC, e=2)
        rt = a1[:, PAIR:2 * PAIR].rearrange("p (c e n) -> p c e n", c=TC, e=2)
        rh = a3[:, 0:2 * PAIR].rearrange("p (c e n) -> p c e n", c=TC, e=4)
        rhT = kparts[:].rearrange("p a c d -> p (a c d)")
        wguh, wgul = (a[:, 0:2 * 4 * FX].rearrange("p (s n) -> p s n", s=2) for a in (a1h, a1l))
        coef8 = sb("coef8", [P, TC, 8])

        Y, G = bank("Y"), bank("G")
        S = [bank("S0"), bank("S1")]
        O = [bank("O0"), bank("O1")]
        M = bank("M")
        F = bank("F")

        def w12_bank(c, j):
            return S[0] if alone(c) and j % 2 else F

        def alone(c):
            return isinstance(c, int) and c >= NB - 2

        def hidden_bank(c, n):
            return S[1] if alone(c) and n else F

        def before_w12(c, j):
            return j - 1 if alone(c) else j

        x_ld, xT_ld = sig("x_ld", 16), sig("xT_ld", 16)
        xh_sb, xl_sb = sig("xh_sb"), sig("xl_sb")
        y_ps, yh_sb, yl_sb = sig("y_ps", HP), sig("yh_sb", HP), sig("yl_sb", HP)
        g_ps, negm_sb = sig("g_ps", 2 * HP), sig("negm_sb", 2 * HP)
        s_ps, ex_sb = sig("s_ps", 2 * HP), sig("ex_sb", 2 * HP)
        v_ps, v_sb = sig("v_ps", 8), sig("v_sb", 8)
        av_ps, comb = sig("av_ps", H), sig("comb", H)
        stats_sb, var_sb, veps_sb, rstd_sb = (
            [sig(f"{name}{n}") for n in range(4)] for name in ("stats_sb", "var_sb", "veps_sb", "rstd_sb"))
        x1_sb, x1T_ps, x1T_sb, x1h_sb, x1l_sb = (sig(n) for n in ("x1_sb", "x1T_ps", "x1T_sb", "x1h_sb", "x1l_sb"))
        logits_ps, mask_sb, ew_sb = sig("logits_ps"), sig("mask_sb"), sig("ew_sb")
        sgu_ps, sth_sb, hs_sb, sd_ps = sig("sgu_ps"), sig("sth_sb"), sig("hs_sb"), sig("sd_ps")
        cum_ps, coef_sb = sig("cum_ps"), sig("coef_sb")
        x2_sb, x2T_ps, x2h_sb, x2l_sb, x2b_sb = (sig(n) for n in ("x2_sb", "x2T_ps", "x2h_sb", "x2l_sb", "x2b_sb"))
        moe_read = sig("moe_read")
        kv_ps, q_ps, kvm_sb, qm_sb, kve_sb, qe_sb, kf_sb, qf_sb = (
            sig(n) for n in ("kv_ps", "q_ps", "kvm_sb", "qm_sb", "kve_sb", "qe_sb", "kf_sb", "qf_sb"))
        kvp_ps, kvz_sb, nd_ps, o1_sb, oT_ps, oT_sb, wo_ps = (
            sig(n) for n in ("kvp_ps", "kvz_sb", "nd_ps", "o1_sb", "oT_ps", "oT_sb", "wo_ps"))
        wo_read = sig("wo_read")
        x3_sb, x3T_ps, x3h_sb, x3l_sb = (sig(n) for n in ("x3_sb", "x3T_ps", "x3h_sb", "x3l_sb"))
        w12_ps, fth_sb, a1_sb, a1h_sb, a1l_sb = (sig(n, KB) for n in ("w12_ps", "fth_sb", "a1_sb", "a1h_sb", "a1l_sb"))
        h1_ps, a2_sb, a2h_sb, a2l_sb = (sig(n, 2) for n in ("h1_ps", "a2_sb", "a2h_sb", "a2l_sb"))
        h2_ps, a3_sb = sig("h2_ps", 2), sig("a3_sb", 2)
        a3h_sb, a3l_sb = sig("a3h_sb", 2), sig("a3l_sb", 2)
        fT_sb, f_ps = sig("fT_sb"), sig("f_ps")
        w3_ps, w3_read, yout_sb, out_st = sig("w3_ps"), sig("w3_read"), sig("yout_sb"), sig("out_st", 16)
        rw_ld = [sig(f"rw_ld{i}", 4 * PAIRS) for i in range(4)]
        rwd_ld = [sig(f"rwd_ld{i}", 8 * GROUPS) for i in range(2)]
        rgu_ps, rth_sb, rt_sb = sig("rgu_ps", E), sig("rth_sb", E), sig("rt_sb", E, 2)
        rh_sb = sig("rh_sb", E, 4)
        rT_ps, rhT_sb = sig("rT_ps", TC * GROUPS, 2), sig("rhT_sb", TC * GROUPS, 2)
        rd_ps = sig("rd_ps", GROUPS, 4)
        rhi_sb, rlo_sb = sig("rhi_sb", PAIRS), sig("rlo_sb", PAIRS, 4)
        c8_sb = sig("c8_sb", 8)
        wm_sb, centred_sb = sig("wm_sb"), sig("centred_sb")
        const_sb, half_sb, ones_sb = sig("const_sb"), sig("half_sb"), sig("ones_sb")
        small_ld, qk_ld = sig("small_ld"), sig("qk_ld")
        vo_ld = [sig(f"vo_ld{i}") for i in range(4)]
        split_ld = [sig(f"split_ld{i}") for i in range(4)]
        vo_split = sig("vo_split")
        a_ps, ah_sb, al_sb = sig("a_ps"), sig("ah_sb"), sig("al_sb")
        split_hi, split_lo = sig("split_hi"), sig("split_lo")

        q_in = Ex[0:R, :, :, :].rearrange("p a b c -> p (a b c)")
        k_in = FF[0:R, 0:2, :].rearrange("p a b -> p (a b)")
        SMALL = [("s3", s3[:]), ("wsd", wsd[:]), ("wout", wout[:]), ("rw", rw[:]), ("s1", s1[:]), ("s2", s2[:]),
                 ("sh1", sh1[:]), ("sh2", sh2[:])]
        ROWS = [("bout", bout)]
        PIECES = [(name, c, min(PIECE, w_split[name][0].shape[1] - c))
                  for name in ("wsgu", "wkv", "wq", "w1", "w2", "h1", "h2", "w3")
                  for c in range(0, w_split[name][0].shape[1], PIECE)]

        FIRST_FFN = [name for name, _, _ in PIECES].index("w1")
        FFN_PIECES = len(PIECES) - FIRST_FFN
        inexact = FF[:].rearrange("p a b -> p (a b)")[:, 0:FFN_PIECES * PIECE // 2].bitcast(BF16)
        inexact_sum, low_flag = sb("inexact_sum", [P, 1]), sb("low_flag", [P, 1], I32)
        inexact_sb, low_ps, low_sb, inexact_sum_sb = (sig(n) for n in ("inexact_sb", "low_ps", "low_sb", "inexact_sum_sb"))

        block = ctx.enter_context(nc.Block())

        @block.sync
        def _(sp):
            sp.dma_start(q_in, A["q"]).then_inc(qk_ld.sem, 16)
            sp.dma_start(k_in, A["k"]).then_inc(qk_ld.sem, 16)
            sp.dma_start(xT_in[:], A["xT"][0]).then_inc(xT_ld.sem, 16)
            sp.dma_start(x_res[:], A["x"][0].rearrange("(c p) d -> p c d", p=P)).then_inc(x_ld.sem, 16)
            for i in range(4):
                sp.dma_start(stage_in[:, i, :], A["vo"][:, i * PIECE:(i + 1) * PIECE]).then_inc(vo_ld[i].sem, 16)
            for name, tile in SMALL:
                sp.dma_start(tile, A[name]).then_inc(small_ld.sem, 16)
            for name, tile in ROWS:
                sp.dma_start(tile[:], A[name].partition_broadcast(P)).then_inc(small_ld.sem, 16)
            for n, (name, c, w) in enumerate(PIECES):
                if n < 4:
                    sp.wait_ge(vo_split.sem, n + 1)
                else:
                    sp.wait_ge(split_lo.sem, n - 3)
                sp.dma_start(stage_in[:, n % 4, 0:w], A[name][:, c:c + w]).then_inc(split_ld[n % 4].sem, 16)

            def experts_in(b):
                wait_alone(sp, coef_sb, b, 1, const_sb)
                on = sp.value_load(flag[0:1, 0:1], min_val=0, max_val=1)
                with sp.If(on > 0):
                    with sp.Fori(0, GROUPS // 2) as it:
                        for l in range(4):
                            wait(sp, rlo_sb, b, it * 4 + l - 3)
                            sp.dma_start(wgu_in[:, l, :], A["wgu"][bass.ds(it * 4 + l, 1)].rearrange("a p n -> (a p) n"))\
                                .then_inc(rw_ld[l].sem, 16)
                with sp.Else():
                    for slot in rw_ld:
                        sp.sem_inc(slot.sem, slot.per)

            def rows(ap, b):
                if isinstance(b, int):
                    return ap[b]
                return ap[bass.ds(b, 1)].rearrange("a p d -> (a p) d")

            def step(a, b, c, more):
                if a is not None and more:
                    wait(sp, xl_sb, a)
                    sp.dma_start(xT_in[:], rows(A["xT"], a + 1)).then_inc(xT_ld.sem, 16)
                if b is not None:
                    experts_in(b)
                if a is not None and more:
                    wait(sp, comb, a, 1)
                    sp.dma_start(x_res[:], rows(A["x"], a + 1).rearrange("(c p) d -> p c d", p=P)).then_inc(x_ld.sem, 16)
                if c is not None:
                    wait(sp, yout_sb, c)
                    sp.dma_start(rows(A["out"], c).rearrange("(c p) d -> p c d", p=P), yout[:]).then_inc(out_st.sem, 16)

            step(0, None, None, True)
            step(1, 0, None, True)
            step(2, 1, 0, True)
            with sp.Fori(3, NB - 1) as i:
                step(i, i - 1, i - 2, True)
            step(NB - 1, NB - 2, NB - 3, False)
            step(None, NB - 1, NB - 2, False)
            step(None, None, NB - 1, False)
            wait(sp, out_st, NB - 1, 16)

        @block.gpsimd
        def _(pool):
            nc.gpsimd.memset(ones[:], 1.0).then_inc(ones_sb.sem, 1)
            nc.gpsimd.memset(ones_bf[:], 1.0).then_inc(ones_sb.sem, 1)
            nc.gpsimd.memset(minus_half[:], -0.5).then_inc(ones_sb.sem, 1)
            nc.gpsimd.memset(ln_eps[:], LN_EPS).then_inc(ones_sb.sem, 1)
            nc.gpsimd.memset(V[:, :, :, D:D + 1], 1.0).then_inc(ones_sb.sem, 1)
            nc.gpsimd.memset(vt[:, :, D:D + 1], 1.0).then_inc(ones_sb.sem, 1)
            pool.wait_ge(ones_sb.sem, 6)
            for tile, src in ((ident, ones), (ident_bf, ones_bf)):
                nc.gpsimd.affine_select(out=tile[:], in_=src[:], compare_op=ALU.is_equal, fill=0.0, base=0,
                                        pattern=[[-1, P]], channel_multiplier=1).then_inc(const_sb.sem, 1)
            nc.gpsimd.affine_select(out=before[:], in_=ones_bf[:], compare_op=ALU.is_gt, fill=0.0, base=0,
                                    pattern=[[1, P]], channel_multiplier=-1).then_inc(const_sb.sem, 1)
            grid = headmask[:].rearrange("p (g e) -> p g e", e=HEAD_DIM1)
            steps = [[-HEAD_DIM1, P // HEAD_DIM1], [0, HEAD_DIM1]]
            nc.gpsimd.affine_select(out=grid, in_=ones[:].rearrange("p (g e) -> p g e", e=HEAD_DIM1),
                                    compare_op=ALU.is_ge, fill=0.0, base=0, pattern=steps,
                                    channel_multiplier=1).then_inc(const_sb.sem, 1)
            pool.wait_ge(const_sb.sem, 4)
            nc.gpsimd.affine_select(out=grid, in_=grid, compare_op=ALU.is_ge, fill=0.0, base=HEAD_DIM1 - 1,
                                    pattern=[[HEAD_DIM1, P // HEAD_DIM1], [0, HEAD_DIM1]],
                                    channel_multiplier=-1).then_inc(const_sb.sem, 1)
            for n, (name, c, w) in enumerate(PIECES):
                hi, lo = w_split[name]
                pool.wait_ge(split_hi.sem, n + 1)
                nc.gpsimd.tensor_tensor(lo[:, c:c + w], stage_in[:, n % 4, 0:w], hi[:, c:c + w].bitcast(F32),
                                        ALU.subtract).then_inc(split_lo.sem, 1)

            def inverse_std(b, n):
                wait(pool, var_sb[n], b)
                nc.gpsimd.tensor_tensor(veps[:, n, :], mv[:, n, :, 1], ln_eps[:], ALU.add).then_inc(veps_sb[n].sem, 1)
                wait(pool, veps_sb[n], b)
                nc.gpsimd.tensor_tensor(rstd[:, n, :], veps[:, n, :], minus_half[:], ALU.pow)\
                    .then_inc(rstd_sb[n].sem, 1)

            def low(out, full, hi, done):
                nc.gpsimd.tensor_tensor(out, full, hi.bitcast(F32), ALU.subtract).then_inc(done.sem, 1)

            def experts(b):
                on = pool.value_load(flag[0:1, 0:1], min_val=0, max_val=1)
                with pool.If(on > 0):
                    with pool.Fori(0, E // 8) as it:
                        for l in range(4):
                            wait(pool, rhi_sb, b, it * 4 + l + 1)
                            low(wgul[:, l % 2, :], wgu_in[:, l, :], wguh[:, l % 2, :], rlo_sb)
                with pool.Else():
                    pool.sem_inc(rlo_sb.sem, PAIRS)

            def mid(b, pos):
                if pos == 0:
                    inverse_std(b, 0)
                elif pos == 3:
                    wait(pool, ew_sb, b)
                    wait(pool, mask_sb, b)
                    nc.gpsimd.tensor_tensor(wm[:], ew[:], mask[:], ALU.mult).then_inc(wm_sb.sem, 1)
                elif pos == 2:
                    wait(pool, x1h_sb, b)
                    low(x1l[:], x1T[:], x1h[:], x1l_sb)
                elif pos == 8:
                    wait_alone(pool, coef_sb, b, 1, const_sb)
                    experts(b)
                    inverse_std(b, 1)
                elif pos == 10:
                    wait(pool, x2h_sb, b)
                    low(x2l[:], x2T[:], x2h[:], x2l_sb)
                    for c in range(TC):
                        ins = nc.gpsimd.tensor_tensor(x2b[:, c, :], x2[:, c, :], bout[:], ALU.add)
                    ins.then_inc(x2b_sb.sem, 1)
                elif pos == 11:
                    wait(pool, kve_sb, b)
                    nc.gpsimd.tensor_tensor(kf, kmax, ke, ALU.add).then_inc(kf_sb.sem, 1)
                elif pos == 12:
                    wait(pool, qe_sb, b)
                    nc.gpsimd.tensor_tensor(qf[:], qmax[:], qe[:], ALU.add).then_inc(qf_sb.sem, 1)
                elif pos == 17:
                    inverse_std(b, 2)

            def ffn(c, pos):
                if pos == 1:
                    wait(pool, x3h_sb, c)
                    low(x3l[:], x3T[:], x3h[:], x3l_sb)
                elif 2 <= pos < 2 + KB:
                    t = slice((pos - 2) * T, (pos - 1) * T)
                    wait(pool, a1h_sb, c, pos - 1)
                    low(a1l[:, t], a1[:, t], a1h[:, t], a1l_sb)
                elif pos in (6, 7):
                    t = slice((pos - 6) * 512, (pos - 5) * 512)
                    wait(pool, a2h_sb, c, pos - 5)
                    low(a2l[:, t], a2[:, t], a2h[:, t], a2l_sb)
                elif pos == 12:
                    for n in range(2):
                        t = slice(n * 512, (n + 1) * 512)
                        wait(pool, a3h_sb, c, n + 1)
                        low(a3l[:, t], a3[:, t], a3h[:, t], a3l_sb)
                elif pos == 15:
                    inverse_std(c, 3)
                    wait(pool, out_st, c, 0)
                    nc.gpsimd.tensor_tensor(yout[:], res_ffn[:], mv[:, 3, :, 0:1].to_broadcast([P, TC, D]),
                                            ALU.subtract).then_inc(centred_sb.sem, 1)
                    wait(pool, centred_sb, c)
                    wait(pool, rstd_sb[3], c)
                    nc.gpsimd.tensor_tensor(yout[:], yout[:], rstd[:, 3, :].unsqueeze(2).to_broadcast([P, TC, D]),
                                            ALU.mult).then_inc(yout_sb.sem, 1)

            def attention(part, a, p, more, between):
                between()

            pool.sem_inc(rlo_sb.sem, rlo_sb.credit)
            pool.wait_ge(small_ld.sem, 16 * (len(SMALL) + len(ROWS)))
            fill(attention)
            pipeline(pool, attention, mid, ffn, NB)

        @block.tensor
        def _(pe):
            mm = nc.tensor.matmul

            def three(out, wh, wl, mh, ml):
                mm(out, wh, mh, start=True, stop=False)
                mm(out, wh, ml, start=False, stop=False)
                return mm(out, wl, mh, start=False, stop=True)

            pe.sem_inc(rT_ps.sem, rT_ps.credit)
            pe.sem_inc(rd_ps.sem, rd_ps.credit)
            pe.wait_ge(qk_ld.sem, 32)
            for n in range(4):
                for j in range(4):
                    h = 4 * n + j
                    ins = mm((M, F, O[0], O[1])[n][:, j * D:(j + 1) * D], q_in[:, h * D:(h + 1) * D], k_in[:, h * D:(h + 1) * D],
                             start=True, stop=True)
                ins.then_inc(a_ps.sem, 1)

            def y(a, p):
                wait(pe, yl_sb, a, p)
                if isinstance(a, int) and a == 0 and p % 2 == 0:
                    pe.wait_ge(al_sb.sem, p // 2 + 1)
                for j in range(2):
                    w = slice((2 * p + j) * D, (2 * p + j + 1) * D)
                    ins = three(Y[:, j * T:(j + 1) * T], Ah[:, w], Al[:, w], xh[:], xl[:])
                ins.then_inc(y_ps.sem, 1)

            def guard(a, p, tc):
                wait(pe, yh_sb, a, p + 1)
                wait(pe, negm_sb, a, 2 * p + tc)
                for j in range(2):
                    c = j * T + tc * P
                    ins = mm(G[:, j * T:(j + 1) * T], yh[:, p % 2, c:c + P], xh[:], start=True, stop=True)
                ins.then_inc(g_ps.sem, 1)

            def scores(a, p, uc):
                wait(pe, yl_sb, a, p + 1)
                if p == 0:
                    wait(pe, v_sb, a, 5 + uc)
                else:
                    wait(pe, ex_sb, a, 2 * p + uc - 1)
                u = slice(uc * P, (uc + 1) * P)
                mm(S[uc][:], xh[:, u], yh[:, p % 2, :], start=True, stop=False)
                mm(S[uc][:], xh[:, u], yl[:, p % 2, :], start=False, stop=False)
                mm(S[uc][:], xl[:, u], yh[:, p % 2, :], start=False, stop=False)

            def minus_max(a, p, uc):
                if uc == 0:
                    wait(pe, negm_sb, a, 2 * p + 2)
                for j in range(2):
                    for tc in range(TC):
                        c = j * T + tc * P
                        ins = mm(S[uc][:, c:c + P], negm[:, p % 2, tc, j:j + 1].to_broadcast([P, P]), ident_bf[:],
                                 start=False, stop=(j == 1 and tc == TC - 1))
                ins.then_inc(s_ps.sem, 1)

            def v_piece(a, n):
                uc, nb = n // 4, n % 4
                if n < 2:
                    wait(pe, ex_sb, a, 0)
                elif n < 4:
                    wait(pe, comb, a, 0)
                else:
                    wait(pe, v_sb, a, n - 3)
                if isinstance(a, int) and a == 0 and uc == 0:
                    pe.wait_ge(vo_split.sem, nb + 1)
                    if n >= 2:
                        pe.wait_ge(al_sb.sem, n + 1)
                u = slice(uc * P, (uc + 1) * P)
                w = slice(nb * 512, (nb + 1) * 512)
                three((S + O)[n % 4][:], xh[:, u], xl[:, u], VOh[:, w], VOl[:, w]).then_inc(v_ps.sem, 1)

            def weigh(a, p):
                wait(pe, ex_sb, a, 2 * p + 2)
                if p == 0:
                    wait(pe, v_sb, a, 8)
                for j in range(2):
                    h = 2 * p + j
                    if h >= 2:
                        wait(pe, comb, a, h - 1)
                    for tc in range(TC):
                        c = j * T + tc * P
                        for uc in range(TC):
                            ins = mm(O[j][:, tc * T:tc * T + D + 1], Ex[:, p % 2, uc, c:c + P], V[:, uc, h, :],
                                     start=(uc == 0), stop=(uc == TC - 1))
                    ins.then_inc(av_ps.sem, 1)

            def attention(part, a, p, more, between):
                if part == "start":
                    wait(pe, xl_sb, a)
                    y(a, 0)
                    for n in range(4):
                        v_piece(a, n)
                    guard(a, 0, 0)
                    y(a, 1)
                    for n in range(4, 6):
                        v_piece(a, n)
                    guard(a, 0, 1)
                elif part == "scores":
                    scores(a, p, 0)
                    if p + 1 < HP:
                        guard(a, p + 1, 0)
                    scores(a, p, 1)
                    minus_max(a, p, 0)
                    minus_max(a, p, 1)
                elif part == "values":
                    if p + 2 < HP:
                        y(a, p + 2)
                    if p + 1 < HP:
                        guard(a, p + 1, 1)
                    if p == 0:
                        v_piece(a, 6)
                        v_piece(a, 7)
                    else:
                        weigh(a, p - 1)
                else:
                    weigh(a, HP - 1)
                between()

            def turn(out, src):
                for c in range(TC):
                    ins = nc.tensor.transpose(out[:, c * P:(c + 1) * P], src[:, c, :], ident[:])
                return ins

            def experts(b):
                on = pe.value_load(flag[0:1, 0:1], min_val=0, max_val=1)
                with pe.If(on > 0):
                    if isinstance(b, int) and b == NB - 1:
                        wait(pe, comb, b, H)
                    else:
                        wait(pe, yl_sb, b + 1, 5)
                        wait(pe, negm_sb, b + 1, 9)
                        wait(pe, ex_sb, b + 1, 8)
                        wait(pe, comb, b + 1, 4)

                    def gate_up(it, l):
                        q = it * 4 + l
                        wait(pe, rlo_sb, b, q + 1)
                        banks = (Y, O[1]) if l % 2 == 0 else S
                        for c in range(TC):
                            wait(pe, rh_sb, b, q * 2 + c - 3)
                            t = slice(c * P, (c + 1) * P)
                            three(banks[c][:, 0:4 * FX], x1h[:, t], x1l[:, t], wguh[:, l % 2, :], wgul[:, l % 2, :])\
                                .then_inc(rgu_ps.sem, 1)

                    def turn_hidden(it, half):
                        g = it * 2 + half
                        for c in range(TC):
                            wait(pe, rh_sb, b, g * 4 + c + 3)
                            wait(pe, rhT_sb, b, g * 2 + c - 1)
                            for k in range(KX):
                                ins = nc.tensor.transpose((O[0], G)[c][:, k * P:(k + 1) * P],
                                                          rh[:, c, :, :].rearrange("p e n -> p (e n)")[:, k * P:(k + 1) * P],
                                                          ident[:])
                            ins.then_inc(rT_ps.sem, 1)

                    def down(it, half):
                        g = it * 2 + half
                        for c in range(TC):
                            wait(pe, rhT_sb, b, g * 2 + c + 1)
                            if c == 0:
                                wait(pe, rwd_ld[half], b, it * 16 + 16)
                            for k in range(KX):
                                ins = mm(M[:, c * P:(c + 1) * P], rhT[:, (c * KX + k) * P:(c * KX + k + 1) * P],
                                         wd_in[:, half, k * D:(k + 1) * D], start=False, stop=False,
                                         skip_group_check=True)
                        ins.then_inc(rd_ps.sem, 1)

                    def groups(it, first, last):
                        gate_up(it, 1)
                        if not first:
                            down(it - 1, 1)
                        gate_up(it, 2)
                        turn_hidden(it, 0)
                        gate_up(it, 3)
                        down(it, 0)
                        if not last:
                            gate_up(it + 1, 0)
                        turn_hidden(it, 1)

                    gate_up(0, 0)
                    groups(0, True, False)
                    with pe.Fori(1, 7) as it:
                        groups(it, False, False)
                    groups(7, False, True)
                    down(7, 1)
                with pe.Else():
                    pe.sem_inc(rgu_ps.sem, E)
                    pe.sem_inc(rT_ps.sem, rT_ps.per)
                    pe.sem_inc(rd_ps.sem, rd_ps.per)

            def mid(b, pos):
                if pos == 0:
                    wait(pe, x1_sb, b)
                    wait(pe, wo_read, b, 0)
                    turn(M, x1).then_inc(x1T_ps.sem, 1)
                elif pos == 1:
                    wait(pe, x1h_sb, b)
                    for c in range(TC):
                        ins = mm(M[:, c * E:(c + 1) * E], x1T[:, c * P:(c + 1) * P], rw[:], start=True, stop=True)
                    ins.then_inc(logits_ps.sem, 1)
                elif pos == 3:
                    wait(pe, x1l_sb, b)
                    wait(pe, ew_sb, b)
                    wh, wl = w_split["wsgu"]
                    for n in range(2):
                        w = slice(n * FX, (n + 1) * FX)
                        ins = three(M[0:FX, n * T:(n + 1) * T], wh[:, w], wl[:, w], x1h[:], x1l[:])
                    ins.then_inc(sgu_ps.sem, 1)
                elif pos == 5:
                    wait(pe, hs_sb, b)
                    m0, m1 = mask[:, 0, :], mask[:, 1, :]
                    mm(M[:, 0:E], before[:], m0, start=True, stop=True)
                    mm(M[:, E:2 * E], before[:], m1, start=True, stop=False)
                    mm(M[:, E:2 * E], ones_bf[:], m0, start=False, stop=True)
                    mm(M[:, 2 * E:3 * E], ones_bf[:], m0, start=True, stop=False)
                    mm(M[:, 2 * E:3 * E], ones_bf[:], m1, start=False, stop=True).then_inc(cum_ps.sem, 1)
                elif pos == 6:
                    wait(pe, coef_sb, b)
                    for c in range(TC):
                        ins = mm(M[:, c * P:(c + 1) * P], hs[:, c * P:(c + 1) * P], wsd[:], start=(c == 0),
                                 stop=False, skip_group_check=True)
                    ins.then_inc(sd_ps.sem, 1)
                elif pos == 7:
                    wait_alone(pe, coef_sb, b, 1, const_sb)
                    experts(b)
                elif pos == 9:
                    wait(pe, x2_sb, b)
                    turn(M, x2).then_inc(x2T_ps.sem, 1)
                elif pos == 10:
                    wait(pe, x2l_sb, b)
                    wh, wl = w_split["wkv"]
                    for c in range(TC):
                        t = slice(c * P, (c + 1) * P)
                        ins = three(M[:, c * 2 * D:(c + 1) * 2 * D], x2h[:, t], x2l[:, t], wh[:], wl[:])
                    ins.then_inc(kv_ps.sem, 1)
                elif pos == 11:
                    wait(pe, kvm_sb, b)
                    wh, wl = w_split["wq"]
                    three(M[:, 0:T], wh[:], wl[:], x2h[:], x2l[:]).then_inc(q_ps.sem, 1)
                elif pos == 12:
                    wait(pe, kf_sb, b)
                    wait(pe, qm_sb, b)
                    for c in range(TC):
                        ins = mm(M[:, 0:D + 1], kf[:, c, :], vt[:, c, :], start=(c == 0), stop=(c == TC - 1))
                    ins.then_inc(kvp_ps.sem, 1)
                elif pos == 13:
                    wait(pe, kvz_sb, b)
                    wait(pe, qf_sb, b)
                    for c in range(TC):
                        ins = mm(M[:, c * 2 * D:c * 2 * D + D + G1], qf[:, c * P:(c + 1) * P], kvz[:], start=True,
                                 stop=True)
                    ins.then_inc(nd_ps.sem, 1)
                elif pos == 14:
                    wait(pe, o1_sb, b)
                    turn(M, o1).then_inc(oT_ps.sem, 1)
                elif pos == 16:
                    wait(pe, oT_sb, b)
                    for c in range(TC):
                        ins = mm(M[:, c * D:(c + 1) * D], oT[:, c * P:(c + 1) * P], wout[:], start=True, stop=True)
                    ins.then_inc(wo_ps.sem, 1)

            def ffn_products(c, pos, low):
                if pos == 0:
                    wait(pe, x3_sb, c)
                    wait(pe, w3_read, c, 0)
                    turn(F, x3).then_inc(x3T_ps.sem, 1)
                elif 1 <= pos < 1 + KB:
                    j = pos - 1
                    if j == 0:
                        wait(pe, x3l_sb, c)
                    else:
                        wait(pe, a1_sb, c, before_w12(c, j))
                    B = w12_bank(c, j)
                    for out, name in ((B[:, 0:T], "w1"), (B[:, T:2 * T], "w2")):
                        wh, wl = w_split[name]
                        w = slice(j * P, (j + 1) * P)
                        if low:
                            ins = three(out, wh[:, w], wl[:, w], x3h[:], x3l[:])
                        else:
                            mm(out, wh[:, w], x3h[:], start=True, stop=False)
                            ins = mm(out, wh[:, w], x3l[:], start=False, stop=True)
                    ins.then_inc(w12_ps.sem, 1)
                elif pos in (5, 6, 8, 9):
                    n, name, mh, ml, lo, done = {
                        5: (0, "h1", a1h, a1l, a1l_sb, h1_ps), 6: (1, "h1", a1h, a1l, a1l_sb, h1_ps),
                        8: (0, "h2", a2h, a2l, a2l_sb, h2_ps), 9: (1, "h2", a2h, a2l, a2l_sb, h2_ps)}[pos]
                    if pos == 5:
                        wait(pe, a1_sb, c, KB)
                    elif pos == 6 and not alone(c):
                        wait(pe, a2_sb, c, 1)
                    elif pos == 8:
                        wait(pe, a2_sb, c, 2)
                    elif pos == 9 and not alone(c):
                        wait(pe, a3_sb, c, 1)
                    wh, wl = w_split[name]
                    for kb in range(KB):
                        if n == 0:
                            wait(pe, lo, c, kb + 1 if lo is a1l_sb else kb // 2 + 1)
                        for j in range(2):
                            w = slice(kb * DH + (2 * n + j) * P, kb * DH + (2 * n + j + 1) * P)
                            t = slice(kb * T, (kb + 1) * T)
                            o = hidden_bank(c, n)[:, j * T:(j + 1) * T]
                            first, last = kb == 0 and j == 0, kb == KB - 1 and j == 1
                            mm(o, wh[:, w], mh[:, t], start=first, stop=False, skip_group_check=True)
                            if low:
                                mm(o, wl[:, w], mh[:, t], start=False, stop=False, skip_group_check=True)
                            ins = mm(o, wh[:, w], ml[:, t], start=False, stop=last, skip_group_check=True)
                    ins.then_inc(done.sem, 1)
                elif pos == 13:
                    wait(pe, a3_sb, c, 2)
                    wh, wl = w_split["w3"]
                    for kb in range(KB):
                        w, t = slice(kb * D, (kb + 1) * D), slice(kb * T, (kb + 1) * T)
                        if kb % 2 == 0:
                            wait(pe, a3l_sb, c, kb // 2 + 1)
                        mm(F[:, 0:T], wh[:, w], a3h[:, t], start=(kb == 0), stop=False)
                        if low:
                            mm(F[:, 0:T], wl[:, w], a3h[:, t], start=False, stop=False)
                        ins = mm(F[:, 0:T], wh[:, w], a3l[:, t], start=False, stop=(kb == KB - 1))
                    ins.then_inc(w3_ps.sem, 1)
                elif pos == 14:
                    wait(pe, fT_sb, c)
                    for t in range(TC):
                        ins = nc.tensor.transpose(F[:, T + t * P:T + (t + 1) * P], fT[:, t * P:(t + 1) * P], ident[:])
                    ins.then_inc(f_ps.sem, 1)

            pe.wait_ge(const_sb.sem, 5)
            pe.wait_ge(ones_sb.sem, 6)

            fill(attention)
            pe.wait_ge(small_ld.sem, 16 * (len(SMALL) + len(ROWS)))
            pe.wait_ge(inexact_sb.sem, FFN_PIECES)
            for n in range(FFN_PIECES):
                ins = mm(M[:], ones_bf[:], inexact[:, n * PIECE:(n + 1) * PIECE], start=(n == 0),
                         stop=(n == FFN_PIECES - 1))
            ins.then_inc(low_ps.sem, 1)
            pe.wait_ge(low_sb.sem, 1)
            low_on = pe.value_load(low_flag[0:1, 0:1], min_val=0, max_val=1)
            with pe.If(low_on > 0):
                pipeline(pe, attention, mid, lambda c, pos: ffn_products(c, pos, True), NB)
            with pe.Else():
                pipeline(pe, attention, mid, lambda c, pos: ffn_products(c, pos, False), NB)

        @block.scalar
        def _(act):
            act_do = nc.scalar.activation
            act.sem_inc(rhT_sb.sem, rhT_sb.credit)
            for n in range(4):
                act.wait_ge(a_ps.sem, n + 1)
                act_do(Ah[:, n * 512:(n + 1) * 512], (M, F, O[0], O[1])[n][:], ACT.Copy).then_inc(ah_sb.sem, 1)
                if n == 0:
                    act.wait_ge(xT_ld.sem, 16)
                    act_do(xh[:], xT_in[:], ACT.Copy).then_inc(xh_sb.sem, 1)

            def y_high(a, p):
                wait(act, y_ps, a, p + 1)
                wait(act, s_ps, a, 2 * p - 2)
                act_do(yh[:, p % 2, :], Y[:], ACT.Copy).then_inc(yh_sb.sem, 1)

            def v_copy(a, n):
                wait(act, v_ps, a, n + 1)
                if n == 0:
                    wait(act, av_ps, a, 0)
                uc, nb = n // 4, n % 4
                act_do(V[:, uc, 4 * nb:4 * nb + 4, 0:D], (S + O)[n % 4][:].rearrange("p (h d) -> p h d", d=D), ACT.Copy)\
                    .then_inc(v_sb.sem, 1)

            def exponentials(a, p):
                for uc in range(TC):
                    wait(act, s_ps, a, 2 * p + uc + 1)
                    wait(act, av_ps, a, 2 * p - 2)
                    act_do(Ex[:, p % 2, uc, :], S[uc][:], ACT.Exp, scale=SCALE).then_inc(ex_sb.sem, 1)

            def attention(part, a, p, more, between):
                if part == "start":
                    between()
                    y_high(a, 0)
                    for n in range(4):
                        v_copy(a, n)
                    y_high(a, 1)
                    for n in range(4, 6):
                        v_copy(a, n)
                elif part == "scores":
                    between()
                    if p != LATE:
                        exponentials(a, p)
                elif part == "values":
                    between()
                    if p == LATE:
                        exponentials(a, p)
                    if p + 2 < HP:
                        y_high(a, p + 2)
                    if p == 0:
                        v_copy(a, 6)
                        v_copy(a, 7)
                    if p == HP - 1 and more:
                        wait(act, xT_ld, a + 1, 16)
                        wait(act, s_ps, a, 2 * HP)
                        act_do(xh[:], xT_in[:], ACT.Copy).then_inc(xh_sb.sem, 1)
                else:
                    between()

            def experts(b):
                on = act.value_load(flag[0:1, 0:1], min_val=0, max_val=1)
                with act.If(on > 0):
                    def high(it, l):
                        wait(act, rw_ld[l], b, it * 16 + 16)
                        act_do(wguh[:, l % 2, :], wgu_in[:, l, :], ACT.Copy).then_inc(rhi_sb.sem, 1)

                    def tanh(it, l):
                        q = it * 4 + l
                        banks = (Y, O[1]) if l % 2 == 0 else S
                        for c in range(TC):
                            wait(act, rgu_ps, b, q * 2 + c + 1)
                            wait(act, rt_sb, b, q * 2 + c - 1)
                            gate = banks[c][:, 0:4 * FX].rearrange("p (e n) -> p e n", e=2)[:, :, 0:FX]
                            act_do(rth[:, c, :, :], gate, ACT.Tanh, scale=0.5).then_inc(rth_sb.sem, 1)

                    def down_weights(it, half):
                        act.dma_start(wd_in[:, half, :], A["wd"][bass.ds(it * 2 + half, 1)]
                                      .rearrange("a p n -> (a p) n")).then_inc(rwd_ld[half].sem, 16)

                    def hidden(it, half, more=True):
                        g = it * 2 + half
                        wait(act, rd_ps, b, g)
                        if half == 0:
                            down_weights(it, 1)
                        elif more:
                            down_weights(it + 1, 0)
                        for c in range(TC):
                            wait(act, rT_ps, b, g * 2 + c + 1)
                            act_do(rhT[:, c * KX * P:(c + 1) * KX * P], (O[0], G)[c][:, 0:KX * P], ACT.Copy)\
                                .then_inc(rhT_sb.sem, 1)

                    def pairs(it, first, last):
                        for l in range(4):
                            tanh(it, l)
                            if l < 2:
                                high(it, l + 2)
                            elif not last:
                                high(it + 1, l - 2)
                            if l == 0 and not first:
                                hidden(it - 1, 1)
                            elif l == 2:
                                hidden(it, 0)

                    down_weights(0, 0)
                    high(0, 0)
                    high(0, 1)
                    pairs(0, True, False)
                    with act.Fori(1, 7) as it:
                        pairs(it, False, False)
                    pairs(7, False, True)
                    hidden(7, 1, False)
                with act.Else():
                    act.sem_inc(rth_sb.sem, E)
                    act.sem_inc(rhT_sb.sem, rhT_sb.per)
                    for slot in rwd_ld:
                        act.sem_inc(slot.sem, slot.per)
                    act.sem_inc(rhi_sb.sem, PAIRS)

            def halves(full, hi, done):
                act_do(full, M[:, 0:T], ACT.Copy)
                act_do(hi, M[:, 0:T], ACT.Copy).then_inc(done.sem, 1)

            def mid(b, pos):
                if pos == 1:
                    wait(act, x1T_ps, b)
                    halves(x1T[:], x1h[:], x1h_sb)
                elif pos == 3:
                    wait(act, mask_sb, b)
                    for c in range(TC):
                        ins = act_do(ew[:, c, :], M[:, c * E:(c + 1) * E], ACT.Exp, bias=negmax[:, c:c + 1])
                    ins.then_inc(ew_sb.sem, 1)
                elif pos == 4:
                    wait(act, sgu_ps, b)
                    act_do(sth[:], M[0:FX, 0:T], ACT.Tanh, scale=0.5).then_inc(sth_sb.sem, 1)
                elif pos == 8:
                    wait_alone(act, coef_sb, b, 1, const_sb)
                    experts(b)
                elif pos == 10:
                    wait(act, x2T_ps, b)
                    halves(x2T[:], x2h[:], x2h_sb)
                elif pos == 11:
                    wait(act, kv_ps, b)
                    kv = M[:].rearrange("p (c n) -> p c n", c=TC)
                    act_do(kmin, kv[:, :, 0:D], ACT.Relu, scale=-1.0)
                    act_do(kmax, kv[:, :, 0:D], ACT.Relu)
                    act_do(vt[:, :, 0:D], kv[:, :, D:2 * D], ACT.Copy).then_inc(kvm_sb.sem, 1)
                    wait(act, kvm_sb, b)
                    act_do(ke, kmin, ACT.Exp, scale=-1.0).then_inc(kve_sb.sem, 1)
                elif pos == 12:
                    wait(act, q_ps, b)
                    act_do(qmin[:], M[:, 0:T], ACT.Relu, scale=-1.0)
                    act_do(qmax[:], M[:, 0:T], ACT.Relu).then_inc(qm_sb.sem, 1)
                    wait(act, qm_sb, b)
                    act_do(qe[:], qmin[:], ACT.Exp, scale=-1.0).then_inc(qe_sb.sem, 1)
                elif pos == 15:
                    wait(act, oT_ps, b)
                    act_do(oT[:], M[:, 0:T], ACT.Copy).then_inc(oT_sb.sem, 1)

            def a1_high(c, j):
                t = slice(j * T, (j + 1) * T)
                wait(act, a1_sb, c, j + 1)
                act_do(a1h[:, t], a1[:, t], ACT.Copy).then_inc(a1h_sb.sem, 1)

            def gelu(B, out, scales, n, done):
                for j in range(2):
                    f = 2 * n + j
                    ins = act_do(out[:, f * T:(f + 1) * T], B[:, j * T:(j + 1) * T], ACT.Gelu, scale=scales[:, f:f + 1])
                ins.then_inc(done.sem, 1)

            def ffn(c, pos):
                if pos == 1:
                    wait(act, x3T_ps, c)
                    act_do(x3T[:], F[:, 0:T], ACT.Copy)
                    act_do(x3h[:], F[:, 0:T], ACT.Copy).then_inc(x3h_sb.sem, 1)
                if 2 <= pos < 2 + KB:
                    j = pos - 2
                    wait(act, w12_ps, c, j + 1)
                    wait(act, a1_sb, c, before_w12(c, j))
                    act_do(fth[:, j % 2, :], w12_bank(c, j)[:, 0:T], ACT.Tanh, scale=s1half[:, j:j + 1])\
                        .then_inc(fth_sb.sem, 1)
                if pos in (3, 4, 5):
                    a1_high(c, pos - 3)
                if pos == 5:
                    a1_high(c, 3)
                if pos in (6, 7):
                    n = pos - 6
                    wait(act, h1_ps, c, n + 1)
                    gelu(hidden_bank(c, n), a2, sh1, n, a2_sb)
                    wait(act, a2_sb, c, n + 1)
                    act_do(a2h[:, 512 * n:512 * n + 512], a2[:, 512 * n:512 * n + 512], ACT.Copy).then_inc(a2h_sb.sem, 1)
                if pos in (9, 10):
                    n = pos - 9
                    wait(act, h2_ps, c, n + 1)
                    gelu(hidden_bank(c, n), a3, sh2, n, a3_sb)
                if pos == 11:
                    for n in range(2):
                        wait(act, a3_sb, c, n + 1)
                        t = slice(512 * n, 512 * n + 512)
                        act_do(a3h[:, t], a3[:, t], ACT.Copy).then_inc(a3h_sb.sem, 1)
                if pos == 14:
                    wait(act, w3_ps, c)
                    act_do(fT[:], F[:, 0:T], ACT.Copy, scale=s3[:, 0:1]).then_inc(fT_sb.sem, 1)

            def high_halves(_, pos):
                if 1 <= pos <= len(PIECES):
                    n = pos - 1
                    name, c, w = PIECES[n]
                    act.wait_ge(split_ld[n % 4].sem, 16 * (n // 4 + 1))
                    act_do(w_split[name][0][:, c:c + w], stage_in[:, n % 4, 0:w], ACT.Copy).then_inc(split_hi.sem, 1)

            fill(attention, high_halves)
            act.wait_ge(half_sb.sem, 4)
            pipeline(act, attention, mid, ffn, NB)

        @block.vector
        def _(dve):
            v = nc.vector
            links = Order(nc, ctx, dve, "mid_order", 9)
            ffn_links = Order(nc, ctx, dve, "ffn_order", KB)
            den_order = sig("den_order", H)

            vo_hi = sig("vo_hi")
            for n in range(4):
                w = slice(n * PIECE, (n + 1) * PIECE)
                dve.wait_ge(ah_sb.sem, n + 1)
                v.tensor_tensor(Al[:, w], (M, F, O[0], O[1])[n][:], Ah[:, w].bitcast(F32), ALU.subtract)\
                    .then_inc(al_sb.sem, 1)
                if n == 0:
                    dve.wait_ge(xh_sb.sem, 1)
                    v.tensor_tensor(xl[:], xT_in[:], xh[:].bitcast(F32), ALU.subtract).then_inc(xl_sb.sem, 1)
                dve.wait_ge(vo_ld[n].sem, 16)
                v.tensor_copy(VOh[:, w], stage_in[:, n, :]).then_inc(vo_hi.sem, 1)
                dve.wait_ge(vo_hi.sem, n + 1)
                v.tensor_tensor(VOl[:, w], stage_in[:, n, :], VOh[:, w].bitcast(F32), ALU.subtract)\
                    .then_inc(vo_split.sem, 1)
            v.memset(taken[:], 0.0).then_inc(half_sb.sem, 1)
            dve.sem_inc(rt_sb.sem, rt_sb.credit)
            dve.sem_inc(rh_sb.sem, rh_sb.credit)

            def y_low(a, p):
                wait(dve, yh_sb, a, p + 1)
                v.tensor_tensor(yl[:, p % 2, :], Y[:], yh[:, p % 2, :].bitcast(F32), ALU.subtract)\
                    .then_inc(yl_sb.sem, 1)

            def row_max(a, p, tc):
                wait(dve, g_ps, a, 2 * p + tc + 1)
                wait(dve, s_ps, a, 2 * p - 2)
                v.tensor_reduce(negm[:, p % 2, tc, :], G[:].rearrange("p (j u) -> p j u", j=2), AX.X, ALU.max,
                                negate=True).then_inc(negm_sb.sem, 1)

            def combine(a, h):
                wait(dve, av_ps, a, h + 1)
                o = O[h % 2][:].rearrange("p (c n) -> p c n", c=TC)
                v.reciprocal(rden[:, h % 2, :], o[:, :, D]).then_inc(den_order.sem, 1)
                wait(dve, den_order, a, h + 1)
                if h == 0:
                    wait(dve, x_ld, a, 16)
                for tc in range(TC):
                    ins = v.scalar_tensor_tensor(out=acc[:, tc, :], in0=o[:, tc, 0:D], scalar=rden[:, h % 2, tc:tc + 1],
                                                 in1=(x_res if h == 0 else acc)[:, tc, :], op0=ALU.mult, op1=ALU.add)
                ins.then_inc(comb.sem, 1)

            def spread(b, n, src):
                for c in range(TC):
                    ins = v.bn_stats(stats[:, n, c, :], src[:, c, :])
                ins.then_inc(stats_sb[n].sem, 1)
                wait(dve, stats_sb[n], b)
                v.memset(spacer[:, n:n + 1], 0.0)
                for c in range(TC):
                    ins = v.bn_aggr(mv[:, n, c, :], stats[:, n, c, :])
                ins.then_inc(var_sb[n].sem, 1)

            def normalize(b, n, src, dst, done):
                wait(dve, rstd_sb[n], b)
                for c in range(TC):
                    ins = v.tensor_scalar(dst[:, c, :], src[:, c, :], mv[:, n, c, 0:1], rstd[:, n, c:c + 1],
                                          ALU.subtract, ALU.mult)
                ins.then_inc(done.sem, 1)

            def attention(part, a, p, more, between):
                if part == "start":
                    y_low(a, 0)
                    between()
                    row_max(a, 0, 0)
                    y_low(a, 1)
                    row_max(a, 0, 1)
                elif part == "scores":
                    between()
                    if p + 1 < HP:
                        row_max(a, p + 1, 0)
                    if p == 2:
                        combine(a, 1)
                elif part == "values":
                    between()
                    if p + 1 < HP:
                        row_max(a, p + 1, 1)
                    if p + 2 < HP and p != LATE:
                        y_low(a, p + 2)
                    if p >= 1:
                        combine(a, 2 * p - 2)
                        if p > 1:
                            combine(a, 2 * p - 1)
                    if p == LATE:
                        y_low(a, p + 2)
                    if p == HP - 1 and more:
                        wait(dve, xh_sb, a + 1)
                        v.tensor_tensor(xl[:], xT_in[:], xh[:].bitcast(F32), ALU.subtract).then_inc(xl_sb.sem, 1)
                else:
                    between()
                    combine(a, H - 2)
                    combine(a, H - 1)

            def experts(b):
                on = dve.value_load(flag[0:1, 0:1], min_val=0, max_val=1)
                with dve.If(on > 0):
                    def hidden(it, l):
                        q = it * 4 + l
                        banks = (Y, O[1]) if l % 2 == 0 else S
                        halves = [banks[c][:, 0:4 * FX].rearrange("p (e n) -> p e n", e=2) for c in range(TC)]
                        for c in range(TC):
                            wait(dve, rth_sb, b, q * 2 + c + 1)
                            wait(dve, rh_sb, b, q * 2 + c - 1)
                            v.scalar_tensor_tensor(out=rt[:, c, :, :], in0=rth[:, c, :, :], scalar=1.0,
                                                   in1=halves[c][:, :, 0:FX], op0=ALU.add, op1=ALU.mult)\
                                .then_inc(rt_sb.sem, 1)
                        if l % 2 == 0:
                            wait(dve, rT_ps, b, q)
                        for c in range(TC):
                            wait(dve, rt_sb, b, q * 2 + c + 1)
                            for e in range(2):
                                ins = v.scalar_tensor_tensor(out=rh[:, c, (l % 2) * 2 + e, :], in0=rt[:, c, e, :],
                                                             scalar=coef8[:, c, 2 * l + e:2 * l + e + 1],
                                                             in1=halves[c][:, e, FX:2 * FX], op0=ALU.mult,
                                                             op1=ALU.mult)
                            ins.then_inc(rh_sb.sem, 1)

                    with dve.Fori(0, E // 8) as it:
                        wait(dve, rh_sb, b, it * 8)
                        v.tensor_copy(coef8[:], coef[:, :, bass.ds(it * 8, 8)]).then_inc(c8_sb.sem, 1)
                        wait(dve, c8_sb, b, it + 1)
                        for l in range(4):
                            hidden(it, l)
                with dve.Else():
                    dve.sem_inc(rt_sb.sem, E)
                    dve.sem_inc(rh_sb.sem, E)
                    dve.sem_inc(c8_sb.sem, E // 8)

            def mid(b, pos):
                if pos == 0:
                    links.start(b)
                    wait(dve, comb, b, H)
                    spread(b, 0, acc)
                    if not (isinstance(b, int) and b == 0):
                        normalize(b - 1, 2, res, x3, x3_sb)
                    normalize(b, 0, acc, x1, x1_sb)
                elif pos == 2:
                    wait_alone(dve, logits_ps, b, 1, const_sb)
                    l3 = M[:, 0:TC * E].rearrange("p (c e) -> p c e", c=TC)
                    for c in range(TC):
                        ins = v.max(top8[:, c, :], l3[:, c, :])
                    links.link(ins)
                    v.tensor_scalar(negmax[:], top8[:, :, 0], -1.0, None, ALU.mult)
                    for c in range(TC):
                        ins = v.match_replace(rest[:, c, :], top8[:, c, :], l3[:, c, :], -3.0e38)
                    links.link(ins)
                    v.tensor_tensor(mask[:], l3, rest[:], ALU.not_equal).then_inc(mask_sb.sem, 1)
                elif pos == 5:
                    wait(dve, sth_sb, b)
                    links.link(v.scalar_tensor_tensor(out=st[:], in0=sth[:], scalar=1.0, in1=M[0:FX, 0:T],
                                                      op0=ALU.add, op1=ALU.mult))
                    v.scalar_tensor_tensor(out=hs[:], in0=st[:], scalar=0.5, in1=M[0:FX, T:2 * T],
                                           op0=ALU.mult, op1=ALU.mult).then_inc(hs_sb.sem, 1)
                    wait(dve, wm_sb, b)
                    links.link(v.tensor_reduce(wsum[:], wm[:], AX.X, ALU.add))
                    links.link(v.reciprocal(wrec[:], wsum[:]))
                elif pos == 6:
                    wait(dve, cum_ps, b)
                    tot = M[:, 2 * E:3 * E]
                    v.scalar_tensor_tensor(out=live[:], in0=taken[:], scalar=CAPACITY, in1=tot, op0=ALU.is_lt,
                                           op1=ALU.mult)
                    for c in range(TC):
                        ins = v.tensor_tensor(place[:, c, :], M[:, c * E:(c + 1) * E], taken[:], ALU.add)
                    links.link(ins)
                    v.tensor_tensor(taken[:], tot, taken[:], ALU.add)
                    v.tensor_reduce(livemax[:], live[:], AX.X, ALU.max)
                    links.link(v.scalar_tensor_tensor(out=place[:], in0=place[:], scalar=CAPACITY, in1=wm[:],
                                                      op0=ALU.is_lt, op1=ALU.mult))
                    wait(dve, rw_ld[3], b, 0)
                    v.tensor_scalar(flag[:], livemax[:], 1.0, None, ALU.min)
                    for c in range(TC):
                        ins = v.tensor_scalar(coef[:, c, :], place[:, c, :], wrec[:, c:c + 1], 0.5, ALU.mult, ALU.mult)
                    ins.then_inc(coef_sb.sem, 1)
                elif pos == 8:
                    wait_alone(dve, coef_sb, b, 1, const_sb)
                    experts(b)
                    wait(dve, sd_ps, b)
                    wait(dve, rd_ps, b, GROUPS)
                    v.tensor_tensor(res[:], M[:, 0:T].rearrange("p (c d) -> p c d", c=TC), x1[:], ALU.add)\
                        .then_inc(moe_read.sem, 1)
                    wait(dve, moe_read, b)
                    spread(b, 1, res)
                elif pos == 9:
                    normalize(b, 1, res, x2, x2_sb)
                elif pos == 13:
                    wait(dve, kvp_ps, b)
                    v.tensor_tensor(kvz[:, 0:D], M[:, 0:D], headmask[:], ALU.mult)
                    one_each = headmask[:].rearrange("p (g e) -> p g e", e=HEAD_DIM1)[:, :, 0]
                    v.tensor_scalar(kvz[:, D:D + G1], one_each, M[:, D:D + 1], None, ALU.mult)\
                        .then_inc(kvz_sb.sem, 1)
                elif pos == 14:
                    wait(dve, nd_ps, b)
                    nd = M[:].rearrange("p (c n) -> p c n", c=TC)
                    links.link(v.tensor_scalar(den[:], nd[:, :, D:D + G1], Z_EPS, None, ALU.add))
                    links.link(v.reciprocal(dinv[:], den[:]))
                    for c in range(TC):
                        ins = v.tensor_tensor(o1[:, c, :].rearrange("p (g e) -> p g e", e=HEAD_DIM1),
                                              nd[:, c, 0:D].rearrange("p (g e) -> p g e", e=HEAD_DIM1),
                                              dinv[:, c, :].to_broadcast([P, G1, HEAD_DIM1]), ALU.mult)
                    ins.then_inc(o1_sb.sem, 1)
                elif pos == 17:
                    wait(dve, wo_ps, b)
                    wait(dve, x2b_sb, b)
                    v.tensor_tensor(res[:], M[:, 0:T].rearrange("p (c d) -> p c d", c=TC), x2b[:], ALU.add)\
                        .then_inc(wo_read.sem, 1)
                    wait(dve, wo_read, b)
                    spread(b, 2, res)
                    links.end()

            def ffn(c, pos):
                if pos == 0:
                    ffn_links.start(c)
                    if isinstance(c, int) and c == NB - 1:
                        normalize(c, 2, res, x3, x3_sb)
                elif 2 <= pos < 2 + KB:
                    j = pos - 2
                    B = w12_bank(c, j)
                    wait(dve, fth_sb, c, j + 1)
                    wait(dve, a1_sb, c, j)
                    ffn_links.link(v.scalar_tensor_tensor(out=ft[:], in0=fth[:, j % 2, :], scalar=1.0, in1=B[:, 0:T],
                                                          op0=ALU.add, op1=ALU.mult))
                    v.scalar_tensor_tensor(out=a1[:, j * T:(j + 1) * T], in0=B[:, T:2 * T],
                                           scalar=s12half[:, j:j + 1], in1=ft[:], op0=ALU.mult, op1=ALU.mult)\
                        .then_inc(a1_sb.sem, 1)
                elif pos == 15:
                    wait(dve, f_ps, c)
                    v.tensor_tensor(res_ffn[:], F[:, T:2 * T].rearrange("p (c d) -> p c d", c=TC), x3[:], ALU.add)\
                        .then_inc(w3_read.sem, 1)
                    wait(dve, w3_read, c)
                    spread(c, 3, res_ffn)
                    ffn_links.end()

            def scales_ready():
                dve.wait_ge(const_sb.sem, 5)
                dve.wait_ge(small_ld.sem, 16 * (len(SMALL) + len(ROWS)))
                v.tensor_scalar(s1half[:], s1[:], 0.5, None, ALU.mult).then_inc(half_sb.sem, 1)
                v.tensor_tensor(s12half[:], s1[:], s2[:], ALU.mult).then_inc(half_sb.sem, 1)
                dve.wait_ge(half_sb.sem, 3)
                v.tensor_scalar(s12half[:], s12half[:], 0.5, None, ALU.mult).then_inc(half_sb.sem, 1)
                dve.wait_ge(half_sb.sem, 4)

            def inexact_weights(_, pos):
                n = pos - 3
                if FIRST_FFN <= n < len(PIECES):
                    name, c, w = PIECES[n]
                    m = (n - FIRST_FFN) * PIECE
                    dve.wait_ge(split_lo.sem, n + 1)
                    v.tensor_scalar(inexact[:, m:m + w], w_split[name][1][:, c:c + w].bitcast(F32), 0.0, None,
                                    ALU.not_equal).then_inc(inexact_sb.sem, 1)

            def low_halves():
                dve.wait_ge(low_ps.sem, 1)
                v.tensor_reduce(inexact_sum[:], M[:], AX.X, ALU.add).then_inc(inexact_sum_sb.sem, 1)
                dve.wait_ge(inexact_sum_sb.sem, 1)
                v.tensor_scalar(low_flag[:], inexact_sum[:], 1.0, None, ALU.min).then_inc(low_sb.sem, 1)

            fill(attention, inexact_weights)
            low_halves()
            scales_ready()
            pipeline(dve, attention, mid, ffn, NB)


def kernel(**inputs):
    import concourse.bacc as bacc
    from concourse.bass_utils import run_bass_kernel_spmd

    g = {k: np.asarray(v) for k, v in inputs.items()}
    x = g["L0_attn_x"]
    nb, t, d = x.shape
    heads, rank, _ = g["L0_attn_Q"].shape
    experts, _, fx = g["L0_ffn_w_gate"].shape
    kb = g["L1_ffn_h1_w"].shape[0] // 128

    def blocks(w):
        wt = w.T
        return wt.reshape(-1, 128, wt.shape[1]).transpose(1, 0, 2)

    def by_feature(s):
        return s.reshape(-1, 128).T

    wqkv = g["L1_attn_Wqkv"]
    gate_up = np.concatenate([g["L0_ffn_w_gate"], g["L0_ffn_w_up"]], axis=2)
    arrays = {
        "x": x,
        "xT": x.transpose(0, 2, 1),
        "q": g["L0_attn_Q"].transpose(1, 0, 2).reshape(rank, heads * d),
        "k": g["L0_attn_K"].transpose(1, 0, 2).reshape(rank, heads * d),
        "vo": g["L0_attn_VO"].transpose(1, 0, 2).reshape(d, heads * d),
        "rw": g["L0_ffn_router_w"].T,
        "wgu": gate_up.reshape(experts // 2, 2, d, 2 * fx).transpose(0, 2, 1, 3).reshape(experts // 2, d, 4 * fx),
        "wd": g["L0_ffn_w_down"].reshape(experts // 4, fx * 4 // 128, 128, d).transpose(0, 2, 1, 3)
        .reshape(experts // 4, 128, -1),
        "wsgu": g["L0_ffn_ws_gate_up"],
        "wsd": g["L0_ffn_ws_down"],
        "wq": wqkv[0:d].T,
        "wkv": wqkv[d:3 * d].T,
        "wout": g["L1_attn_Wout"].T,
        "bout": g["L1_attn_bout"],
        "w1": g["L1_ffn_w1_w"].T,
        "w2": g["L1_ffn_w2_w"].T,
        "h1": blocks(g["L1_ffn_h1_w"]).reshape(128, -1),
        "h2": blocks(g["L1_ffn_h2_w"]).reshape(128, -1),
        "w3": blocks(g["L1_ffn_w3_w"]).reshape(128, -1),
        "s1": by_feature(g["L1_ffn_w1_s"]),
        "s2": by_feature(g["L1_ffn_w2_s"]),
        "sh1": by_feature(g["L1_ffn_h1_s"]),
        "sh2": by_feature(g["L1_ffn_h2_s"]),
        "s3": by_feature(g["L1_ffn_w3_s"]),
    }
    nc = bacc.Bacc("TRN2", target_bir_lowering=False, num_devices=1)
    arrays = {k: np.ascontiguousarray(v) for k, v in arrays.items()}
    aps = {k: nc.dram_tensor("in_" + k, a.shape, mybir.dt.from_np(a.dtype), kind="ExternalInput").ap()
           for k, a in arrays.items()}
    aps["out"] = nc.dram_tensor("out", x.shape, F32, kind="ExternalOutput").ap()
    build(nc, aps)
    r = run_bass_kernel_spmd(nc, [{"in_" + k: a for k, a in arrays.items()}], core_ids=[0])
    return r.results[0]["out"]
```
